# Optimizing a Trainium2 kernel written in Bass

```python
import numpy as np
import jax
import jax.numpy as jnp

def _softmax(x, axis=-1):
    return jax.nn.softmax(x, axis=axis)

def _gelu(x):
    return jax.nn.gelu(x, approximate=True)

def _silu(x):
    return jax.nn.silu(x)

def _sigmoid(x):
    return jax.nn.sigmoid(x)

def _layernorm(x, axis=-1, eps=1e-05):
    m = jnp.mean(x, axis=axis, keepdims=True)
    v = jnp.var(x, axis=axis, keepdims=True)
    return (x - m) / jnp.sqrt(v + eps)

def _scatter_add(tgt, idx, src, axis=0):
    return tgt.at[idx].add(src)

def _segment_sum(src, seg, n):
    return jax.ops.segment_sum(src, seg, n)
kernel_name = 'mk_recurrent_d4_jaxref_r8_e61126'

def setup_inputs(seed: int=0):
    np.random.seed(seed)
    _w = jnp.asarray

    def _L0_attn_setup():
        import jax, jax.numpy as jnp
        import numpy as np
        D_MODEL, N_HEADS, N_KV, HEAD_DIM, D_LAT = (128, 8, 2, 128, 32)
        N_REP = N_HEADS // N_KV
        B, T = (2, 256)
        key = jax.random.key(seed)
        ks = jax.random.split(key, 8)
        s = lambda fan_in: 1.0 / np.sqrt(fan_in)
        return {'x': jax.random.normal(ks[0], (B, T, D_MODEL), jnp.float32), 'wq': jax.random.normal(ks[1], (D_MODEL, N_HEADS * HEAD_DIM), jnp.float32) * s(D_MODEL), 'wk_down': jax.random.normal(ks[2], (D_MODEL, N_KV * D_LAT), jnp.float32) * s(D_MODEL), 'wv_down': jax.random.normal(ks[3], (D_MODEL, N_KV * D_LAT), jnp.float32) * s(D_MODEL), 'wk_up': jax.random.normal(ks[4], (D_LAT, HEAD_DIM), jnp.float32) * s(D_LAT), 'wv_up': jax.random.normal(ks[5], (D_LAT, HEAD_DIM), jnp.float32) * s(D_LAT), 'wo': jax.random.normal(ks[6], (N_HEADS * HEAD_DIM, D_MODEL), jnp.float32) * s(N_HEADS * HEAD_DIM)}
    _L0_attn_in = _L0_attn_setup()

    def _L0_ffn_setup():
        import jax, jax.numpy as jnp
        import numpy as np
        B, S, D = (4, 256, 128)
        E, F = (8, 512)
        key = jax.random.key(seed)
        ks = jax.random.split(key, 5)
        x = jax.random.normal(ks[0], (B, S, D), dtype=jnp.float32)
        switch_w = jax.random.normal(ks[1], (D, E), dtype=jnp.float32) * D ** (-0.5)
        switch_b = jnp.zeros((E,), dtype=jnp.float32)
        w1 = jax.random.normal(ks[2], (E, D, F), dtype=jnp.float32) * D ** (-0.5)
        b1 = jnp.zeros((E, F), dtype=jnp.float32)
        w2 = jax.random.normal(ks[3], (E, F, D), dtype=jnp.float32) * F ** (-0.5)
        b2 = jnp.zeros((E, D), dtype=jnp.float32)
        return {'x': x, 'switch_w': switch_w, 'switch_b': switch_b, 'w1': w1, 'b1': b1, 'w2': w2, 'b2': b2}
    _L0_ffn_in = _L0_ffn_setup()

    def _L1_attn_setup():
        import jax, jax.numpy as jnp
        import numpy as np
        B, N, D, H = (4, 512, 128, 16)
        HD = D // H

        def _kernel(x):
            return jax.nn.elu(x) + 1.0
        key = jax.random.key(seed)
        k1, k2, k3, k4 = jax.random.split(key, 4)
        x = jax.random.normal(k1, (B, N, D), dtype=jnp.float32)
        w_qkv = jax.random.normal(k2, (3 * D, D), dtype=jnp.float32) * (1.0 / np.sqrt(D))
        w_out = jax.random.normal(k3, (D, D), dtype=jnp.float32) * (1.0 / np.sqrt(D))
        b_out = jax.random.normal(k4, (D,), dtype=jnp.float32) * 0.01
        return {'x': x, 'w_qkv': w_qkv, 'w_out': w_out, 'b_out': b_out}
    _L1_attn_in = _L1_attn_setup()

    def _L1_ffn_setup():
        import jax, jax.numpy as jnp
        import numpy as np
        DIM = 128
        HIDDEN = 384
        SCALE = 1.0 / 127.0

        def _dequant(w_int, dtype):
            return w_int.astype(dtype) * jnp.asarray(SCALE, dtype)
        key = jax.random.key(seed)
        k_x, k_g, k_u, k_d = jax.random.split(key, 4)
        x = jax.random.normal(k_x, (4, 256, DIM), dtype=jnp.float32)
        w_gate = jax.random.randint(k_g, (HIDDEN, DIM), -127, 128, dtype=jnp.int32)
        w_up = jax.random.randint(k_u, (HIDDEN, DIM), -127, 128, dtype=jnp.int32)
        w_down = jax.random.randint(k_d, (DIM, HIDDEN), -127, 128, dtype=jnp.int32)
        return {'x': x, 'w_gate': w_gate, 'w_up': w_up, 'w_down': w_down}
    _L1_ffn_in = _L1_ffn_setup()

    def _L2_attn_setup():
        import jax, jax.numpy as jnp
        import numpy as np
        D_MODEL = 128
        INNER = 256
        KSIZE = 3
        B, S = (8, 128)
        EPS = 1e-05

        def _layer_norm(x, gamma, beta):
            mu = jnp.mean(x, axis=-1, keepdims=True)
            var = jnp.mean(jnp.square(x - mu), axis=-1, keepdims=True)
            return (x - mu) * jax.lax.rsqrt(var + EPS) * gamma + beta

        def _causal_depthwise_conv(v, w, b):
            x = jnp.transpose(v, (0, 2, 1))
            y = jax.lax.conv_general_dilated(x, w[:, None, :], window_strides=(1,), padding=[(KSIZE - 1, 0)], feature_group_count=INNER, dimension_numbers=('NCH', 'OIH', 'NCH'))
            y = y + b[None, :, None]
            return jnp.transpose(y, (0, 2, 1))

        def _selective_scan(values, deltas):
            a = deltas
            b = (1.0 - deltas) * values

            def combine(c1, c2):
                a1, b1 = c1
                a2, b2 = c2
                return (a1 * a2, a2 * b1 + b2)
            _, out = jax.lax.associative_scan(combine, (a, b), axis=1)
            return out
        key = jax.random.key(seed)
        ks = jax.random.split(key, 12)
        sc = 0.02
        return {'x': jax.random.normal(ks[0], (B, S, D_MODEL), jnp.float32), 'ln_gamma': jnp.ones((D_MODEL,), jnp.float32), 'ln_beta': jnp.zeros((D_MODEL,), jnp.float32), 'W_in': jax.random.normal(ks[1], (D_MODEL, 2 * INNER), jnp.float32) * sc, 'b_in': jnp.zeros((2 * INNER,), jnp.float32), 'conv_w': jax.random.normal(ks[2], (INNER, KSIZE), jnp.float32) * sc, 'conv_b': jnp.zeros((INNER,), jnp.float32), 'W_delta': jax.random.normal(ks[3], (INNER, INNER), jnp.float32) * sc, 'b_delta': jnp.zeros((INNER,), jnp.float32), 'W_out': jax.random.normal(ks[4], (INNER, D_MODEL), jnp.float32) * sc, 'b_out': jnp.zeros((D_MODEL,), jnp.float32)}
    _L2_attn_in = _L2_attn_setup()

    def _L2_ffn_setup():
        import jax, jax.numpy as jnp
        import numpy as np
        NUM_GEMMS = 8
        HIDDEN = 128
        INTER = 512
        key = jax.random.key(seed)
        k_x, k_w1, k_b1, k_w2, k_b2 = jax.random.split(key, 5)
        x = jax.random.normal(k_x, (8, 256, HIDDEN), dtype=jnp.float32)
        s1 = 1.0 / np.sqrt(HIDDEN)
        s2 = 1.0 / np.sqrt(INTER)
        W1 = jax.random.uniform(k_w1, (NUM_GEMMS, INTER, HIDDEN), jnp.float32, -s1, s1)
        b1 = jax.random.uniform(k_b1, (NUM_GEMMS, INTER), jnp.float32, -s1, s1)
        W2 = jax.random.uniform(k_w2, (NUM_GEMMS, HIDDEN, INTER), jnp.float32, -s2, s2)
        b2 = jax.random.uniform(k_b2, (NUM_GEMMS, HIDDEN), jnp.float32, -s2, s2)
        return {'x': x, 'W1': W1, 'b1': b1, 'W2': W2, 'b2': b2}
    _L2_ffn_in = _L2_ffn_setup()

    def _L3_attn_setup():
        import jax, jax.numpy as jnp
        import numpy as np
        from jax import lax
        B, T, H = (4, 512, 128)
        K = 32

        def _causal_dw_conv(v, w, b):
            c = v.shape[1]
            k = w.shape[-1]
            y = lax.conv_general_dilated(v, w, window_strides=(1,), padding=[(k - 1, 0)], dimension_numbers=('NCH', 'OIH', 'NCH'), feature_group_count=c)
            return y + b[None, :, None]
        key = jax.random.key(seed)
        ks = jax.random.split(key, 9)
        s_in = 1.0 / np.sqrt(H)
        s_dw = 1.0 / np.sqrt(K)
        s_out = 1.0 / np.sqrt(2 * H)
        return {'x': jax.random.normal(ks[0], (B, T, H), jnp.float32), 'w_in': jax.random.normal(ks[1], (2 * H, H), jnp.float32) * s_in, 'b_in': jax.random.normal(ks[2], (2 * H,), jnp.float32) * s_in, 'w_a': jax.random.normal(ks[3], (H, 1, K), jnp.float32) * s_dw, 'b_a': jax.random.normal(ks[4], (H,), jnp.float32) * s_dw, 'w_b': jax.random.normal(ks[5], (H, 1, K), jnp.float32) * s_dw, 'b_b': jax.random.normal(ks[6], (H,), jnp.float32) * s_dw, 'w_out': jax.random.normal(ks[7], (H, 2 * H), jnp.float32) * s_out, 'b_out': jax.random.normal(ks[8], (H,), jnp.float32) * s_out}
    _L3_attn_in = _L3_attn_setup()

    def _L3_ffn_setup():
        import jax, jax.numpy as jnp
        import numpy as np
        DIM = 128
        DEPTH = 2
        HEADS = 8
        DIM_HEAD = 64
        WINDOW = 64
        INNER = HEADS * DIM_HEAD
        HID = int(DIM * 4 * 2 / 3)
        B, N = (2, 1024)
        QK_SCALE = 8.0

        def shift_token(t):
            t1, t2 = jnp.split(t, 2, axis=-1)
            t2 = jnp.pad(t2, ((0, 0), (1, 0), (0, 0)))[:, :-1]
            return jnp.concatenate([t1, t2], axis=-1)

        def l2norm(t):
            return t / jnp.clip(jnp.linalg.norm(t, axis=-1, keepdims=True), 1e-12)

        def rotate_half(x):
            x1, x2 = jnp.split(x, 2, axis=-1)
            return jnp.concatenate([-x2, x1], axis=-1)

        def rotary_xpos(q, k):
            n = q.shape[-2]
            half_idx = jnp.arange(0, DIM_HEAD, 2, dtype=jnp.float32)
            inv_freq = 1.0 / 10000.0 ** (half_idx / DIM_HEAD)
            t = jnp.arange(n, dtype=jnp.float32)
            freqs = t[:, None] * inv_freq[None, :]
            freqs = jnp.concatenate([freqs, freqs], axis=-1)
            base = (half_idx + 0.4 * DIM_HEAD) / (1.4 * DIM_HEAD)
            power = (t - n // 2) / float(WINDOW // 2)
            scale = base[None, :] ** power[:, None]
            scale = jnp.concatenate([scale, scale], axis=-1)
            cos, sin = (jnp.cos(freqs), jnp.sin(freqs))
            q = q * cos * scale + rotate_half(q) * sin * scale
            k = k * cos / scale + rotate_half(k) * sin / scale
            return (q, k)

        def local_attention(q, k, v):
            b, h, n, d = q.shape
            w = n // WINDOW
            bq = q.reshape(b, h, w, WINDOW, d) * QK_SCALE
            bk = k.reshape(b, h, w, WINDOW, d)
            bv = v.reshape(b, h, w, WINDOW, d)

            def look_around(t):
                p = jnp.pad(t, ((0, 0), (0, 0), (1, 0), (0, 0), (0, 0)))
                return jnp.concatenate([p[:, :, :w], p[:, :, 1:]], axis=3)
            bk, bv = (look_around(bk), look_around(bv))
            bt = jnp.arange(n).reshape(w, WINDOW)
            btp = jnp.pad(bt, ((1, 0), (0, 0)), constant_values=-1)
            btk = jnp.concatenate([btp[:w], btp[1:]], axis=1)
            sim = jnp.einsum('bhwid,bhwjd->bhwij', bq, bk)
            i = bt[:, :, None]
            j = btk[:, None, :]
            mask = (i < j) | (i > j + WINDOW) | (j == -1)
            sim = jnp.where(mask, -jnp.finfo(sim.dtype).max, sim)
            attn = jax.nn.softmax(sim, axis=-1)
            out = jnp.einsum('bhwij,bhwjd->bhwid', attn, bv)
            return out.reshape(b, h, n, d)

        def _layer(x, wqkv, qs, ksc, wo, lg, lb, w1, b1, w2, b2):
            b, n, _ = x.shape
            h = shift_token(x)
            qkv = h @ wqkv
            q, k, v = jnp.split(qkv, 3, axis=-1)
            to_heads = lambda t: t.reshape(b, n, HEADS, DIM_HEAD).transpose(0, 2, 1, 3)
            q, k, v = (to_heads(q), to_heads(k), to_heads(v))
            q = l2norm(q) * qs
            k = l2norm(k) * ksc
            q, k = rotary_xpos(q, k)
            o = local_attention(q, k, v)
            o = o.transpose(0, 2, 1, 3).reshape(b, n, INNER)
            x = x + o @ wo
            h = shift_token(x)
            mu = h.mean(-1, keepdims=True)
            var = h.var(-1, keepdims=True)
            h = (h - mu) / jnp.sqrt(var + 1e-05) * lg + lb
            h = h @ w1 + b1
            a, g = jnp.split(h, 2, axis=-1)
            h = a * jax.nn.gelu(g, approximate=False)
            x = x + h @ w2 + b2
            return x
        key = jax.random.key(seed)
        ks = jax.random.split(key, 6)
        return {'x': jax.random.normal(ks[0], (B, N, DIM), jnp.float32), 'wqkv': jax.random.normal(ks[1], (DEPTH, DIM, 3 * INNER), jnp.float32) * 0.02, 'q_scale': jnp.ones((DEPTH, DIM_HEAD), jnp.float32), 'k_scale': jnp.ones((DEPTH, DIM_HEAD), jnp.float32), 'wo': jax.random.normal(ks[2], (DEPTH, INNER, DIM), jnp.float32) * 0.02, 'ln_g': jnp.ones((DEPTH, DIM), jnp.float32), 'ln_b': jnp.zeros((DEPTH, DIM), jnp.float32), 'w1': jax.random.normal(ks[3], (DEPTH, DIM, 2 * HID), jnp.float32) * 0.02, 'b1': jnp.zeros((DEPTH, 2 * HID), jnp.float32), 'w2': jax.random.normal(ks[4], (DEPTH, HID, DIM), jnp.float32) * 0.02, 'b2': jnp.zeros((DEPTH, DIM), jnp.float32)}
    _L3_ffn_in = _L3_ffn_setup()
    _d = {'L0_attn_x': _L0_attn_in['x'], 'L0_attn_wq': _L0_attn_in['wq'], 'L0_attn_wk_down': _L0_attn_in['wk_down'], 'L0_attn_wv_down': _L0_attn_in['wv_down'], 'L0_attn_wk_up': _L0_attn_in['wk_up'], 'L0_attn_wv_up': _L0_attn_in['wv_up'], 'L0_attn_wo': _L0_attn_in['wo'], 'L0_ffn_switch_w': _L0_ffn_in['switch_w'], 'L0_ffn_switch_b': _L0_ffn_in['switch_b'], 'L0_ffn_w1': _L0_ffn_in['w1'], 'L0_ffn_b1': _L0_ffn_in['b1'], 'L0_ffn_w2': _L0_ffn_in['w2'], 'L0_ffn_b2': _L0_ffn_in['b2'], 'L1_attn_w_qkv': _L1_attn_in['w_qkv'], 'L1_attn_w_out': _L1_attn_in['w_out'], 'L1_attn_b_out': _L1_attn_in['b_out'], 'L1_ffn_w_gate': _L1_ffn_in['w_gate'], 'L1_ffn_w_up': _L1_ffn_in['w_up'], 'L1_ffn_w_down': _L1_ffn_in['w_down'], 'L2_attn_ln_gamma': _L2_attn_in['ln_gamma'], 'L2_attn_ln_beta': _L2_attn_in['ln_beta'], 'L2_attn_W_in': _L2_attn_in['W_in'], 'L2_attn_b_in': _L2_attn_in['b_in'], 'L2_attn_conv_w': _L2_attn_in['conv_w'], 'L2_attn_conv_b': _L2_attn_in['conv_b'], 'L2_attn_W_delta': _L2_attn_in['W_delta'], 'L2_attn_b_delta': _L2_attn_in['b_delta'], 'L2_attn_W_out': _L2_attn_in['W_out'], 'L2_attn_b_out': _L2_attn_in['b_out'], 'L2_ffn_W1': _L2_ffn_in['W1'], 'L2_ffn_b1': _L2_ffn_in['b1'], 'L2_ffn_W2': _L2_ffn_in['W2'], 'L2_ffn_b2': _L2_ffn_in['b2'], 'L3_attn_w_in': _L3_attn_in['w_in'], 'L3_attn_b_in': _L3_attn_in['b_in'], 'L3_attn_w_a': _L3_attn_in['w_a'], 'L3_attn_b_a': _L3_attn_in['b_a'], 'L3_attn_w_b': _L3_attn_in['w_b'], 'L3_attn_b_b': _L3_attn_in['b_b'], 'L3_attn_w_out': _L3_attn_in['w_out'], 'L3_attn_b_out': _L3_attn_in['b_out'], 'L3_ffn_wqkv': _L3_ffn_in['wqkv'], 'L3_ffn_q_scale': _L3_ffn_in['q_scale'], 'L3_ffn_k_scale': _L3_ffn_in['k_scale'], 'L3_ffn_wo': _L3_ffn_in['wo'], 'L3_ffn_ln_g': _L3_ffn_in['ln_g'], 'L3_ffn_ln_b': _L3_ffn_in['ln_b'], 'L3_ffn_w1': _L3_ffn_in['w1'], 'L3_ffn_b1': _L3_ffn_in['b1'], 'L3_ffn_w2': _L3_ffn_in['w2'], 'L3_ffn_b2': _L3_ffn_in['b2']}
    _x0 = _d['L0_attn_x']
    _d['L0_attn_x'] = jax.random.normal(jax.random.fold_in(jax.random.key(seed), 1), (32, 256, 128), dtype=_x0.dtype)
    del _x0
    return _d

def reference(L0_attn_x, L0_attn_wq, L0_attn_wk_down, L0_attn_wv_down, L0_attn_wk_up, L0_attn_wv_up, L0_attn_wo, L0_ffn_switch_w, L0_ffn_switch_b, L0_ffn_w1, L0_ffn_b1, L0_ffn_w2, L0_ffn_b2, L1_attn_w_qkv, L1_attn_w_out, L1_attn_b_out, L1_ffn_w_gate, L1_ffn_w_up, L1_ffn_w_down, L2_attn_ln_gamma, L2_attn_ln_beta, L2_attn_W_in, L2_attn_b_in, L2_attn_conv_w, L2_attn_conv_b, L2_attn_W_delta, L2_attn_b_delta, L2_attn_W_out, L2_attn_b_out, L2_ffn_W1, L2_ffn_b1, L2_ffn_W2, L2_ffn_b2, L3_attn_w_in, L3_attn_b_in, L3_attn_w_a, L3_attn_b_a, L3_attn_w_b, L3_attn_b_b, L3_attn_w_out, L3_attn_b_out, L3_ffn_wqkv, L3_ffn_q_scale, L3_ffn_k_scale, L3_ffn_wo, L3_ffn_ln_g, L3_ffn_ln_b, L3_ffn_w1, L3_ffn_b1, L3_ffn_w2, L3_ffn_b2):

    def _L0_attn_ref(x, wq, wk_down, wv_down, wk_up, wv_up, wo):
        import jax, jax.numpy as jnp
        import numpy as np
        D_MODEL, N_HEADS, N_KV, HEAD_DIM, D_LAT = (128, 8, 2, 128, 32)
        N_REP = N_HEADS // N_KV
        B, T = (2, 256)
        Bq, Tq, _ = x.shape
        scale = HEAD_DIM ** (-0.5)
        q = (x @ wq).reshape(Bq, Tq, N_KV, N_REP, HEAD_DIM)
        k_lat = (x @ wk_down).reshape(Bq, Tq, N_KV, D_LAT)
        v_lat = (x @ wv_down).reshape(Bq, Tq, N_KV, D_LAT)
        k = jnp.einsum('bkhl,ld->bkhd', k_lat, wk_up)
        v = jnp.einsum('bkhl,ld->bkhd', v_lat, wv_up)
        scores = jnp.einsum('bqhrd,bkhd->bhrqk', q, k) * scale
        causal = jnp.tril(jnp.ones((Tq, Tq), dtype=bool))
        scores = jnp.where(causal, scores, jnp.finfo(scores.dtype).min)
        probs = jax.nn.softmax(scores, axis=-1)
        y = jnp.einsum('bhrqk,bkhd->bqhrd', probs, v)
        y = y.reshape(Bq, Tq, N_HEADS * HEAD_DIM)
        return y @ wo

    def _L0_ffn_ref(x, switch_w, switch_b, w1, b1, w2, b2):
        import jax, jax.numpy as jnp
        import numpy as np
        B, S, D = (4, 256, 128)
        E, F = (8, 512)
        b, s, d = x.shape
        t = x.reshape(-1, d)
        logits = t @ switch_w + switch_b
        route_prob = jax.nn.softmax(logits, axis=-1)
        route_prob_max = jnp.max(route_prob, axis=-1)
        routes = jnp.argmax(route_prob, axis=-1)
        out = jnp.zeros_like(t)
        n_experts = w1.shape[0]
        for e in range(n_experts):
            h = jax.nn.gelu(t @ w1[e] + b1[e])
            y = h @ w2[e] + b2[e]
            mask = (routes == e)[:, None]
            out = jnp.where(mask, y, out)
        out = out * route_prob_max[:, None]
        return out.reshape(b, s, d)

    def _L1_attn_ref(x, w_qkv, w_out, b_out):
        import jax, jax.numpy as jnp
        import numpy as np
        B, N, D, H = (4, 512, 128, 16)
        HD = D // H

        def _kernel(x):
            return jax.nn.elu(x) + 1.0
        b, n, d = x.shape
        qkv = x @ w_qkv.T
        qkv = qkv.reshape(b, n, 3, H, HD)
        q, k, v = (qkv[:, :, 0], qkv[:, :, 1], qkv[:, :, 2])
        q = _kernel(q)
        k = _kernel(k)
        kv = jnp.einsum('bnhd,bnhm->bhdm', k, v)
        z = 1.0 / (jnp.einsum('bnhd,bhd->bnh', q, k.sum(axis=1)) + 1e-06)
        out = jnp.einsum('bnhd,bhdm,bnh->bnhm', q, kv, z)
        out = out.reshape(b, n, d)
        return out @ w_out.T + b_out

    def _L1_ffn_ref(x, w_gate, w_up, w_down):
        import jax, jax.numpy as jnp
        import numpy as np
        DIM = 128
        HIDDEN = 384
        SCALE = 1.0 / 127.0

        def _dequant(w_int, dtype):
            return w_int.astype(dtype) * jnp.asarray(SCALE, dtype)
        wg = _dequant(w_gate, x.dtype)
        wu = _dequant(w_up, x.dtype)
        wd = _dequant(w_down, x.dtype)
        gate = jnp.einsum('bsd,hd->bsh', x, wg)
        up = jnp.einsum('bsd,hd->bsh', x, wu)
        h = jax.nn.silu(gate) * up
        return jnp.einsum('bsh,dh->bsd', h, wd)

    def _L2_attn_ref(x, ln_gamma, ln_beta, W_in, b_in, conv_w, conv_b, W_delta, b_delta, W_out, b_out):
        import jax, jax.numpy as jnp
        import numpy as np
        D_MODEL = 128
        INNER = 256
        KSIZE = 3
        B, S = (8, 128)
        EPS = 1e-05

        def _layer_norm(x, gamma, beta):
            mu = jnp.mean(x, axis=-1, keepdims=True)
            var = jnp.mean(jnp.square(x - mu), axis=-1, keepdims=True)
            return (x - mu) * jax.lax.rsqrt(var + EPS) * gamma + beta

        def _causal_depthwise_conv(v, w, b):
            x = jnp.transpose(v, (0, 2, 1))
            y = jax.lax.conv_general_dilated(x, w[:, None, :], window_strides=(1,), padding=[(KSIZE - 1, 0)], feature_group_count=INNER, dimension_numbers=('NCH', 'OIH', 'NCH'))
            y = y + b[None, :, None]
            return jnp.transpose(y, (0, 2, 1))

        def _selective_scan(values, deltas):
            a = deltas
            b = (1.0 - deltas) * values

            def combine(c1, c2):
                a1, b1 = c1
                a2, b2 = c2
                return (a1 * a2, a2 * b1 + b2)
            _, out = jax.lax.associative_scan(combine, (a, b), axis=1)
            return out
        residual = x
        h = _layer_norm(x, ln_gamma, ln_beta)
        proj = jnp.einsum('bsd,df->bsf', h, W_in) + b_in
        values, gate = (proj[..., :INNER], proj[..., INNER:])
        values = _causal_depthwise_conv(values, conv_w, conv_b)
        values = jax.nn.silu(values)
        deltas = jax.nn.sigmoid(jnp.einsum('bsc,ce->bse', values, W_delta) + b_delta)
        fwd = _selective_scan(values, deltas)
        bwd = jnp.flip(_selective_scan(jnp.flip(values, 1), jnp.flip(deltas, 1)), 1)
        fused = (fwd + bwd) * jax.nn.sigmoid(gate)
        out = jnp.einsum('bsc,cd->bsd', fused, W_out) + b_out
        return residual + out

    def _L2_ffn_ref(x, W1, b1, W2, b2):
        import jax, jax.numpy as jnp
        import numpy as np
        NUM_GEMMS = 8
        HIDDEN = 128
        INTER = 512
        orig_shape = x.shape
        token_num = int(np.prod(orig_shape[:-1]))
        m = token_num // NUM_GEMMS
        xg = x.reshape(NUM_GEMMS, m, HIDDEN)
        h1 = jnp.einsum('gmh,goh->gmo', xg, W1) + b1[:, None, :]
        h2 = jnp.einsum('gmo,gho->gmh', h1, W2) + b2[:, None, :]
        return h2.reshape(orig_shape)

    def _L3_attn_ref(x, w_in, b_in, w_a, b_a, w_b, b_b, w_out, b_out):
        import jax, jax.numpy as jnp
        import numpy as np
        from jax import lax
        B, T, H = (4, 512, 128)
        K = 32

        def _causal_dw_conv(v, w, b):
            c = v.shape[1]
            k = w.shape[-1]
            y = lax.conv_general_dilated(v, w, window_strides=(1,), padding=[(k - 1, 0)], dimension_numbers=('NCH', 'OIH', 'NCH'), feature_group_count=c)
            return y + b[None, :, None]
        h = w_a.shape[0]
        z = jnp.einsum('bth,eh->bet', x, w_in) + b_in[None, :, None]
        za, zb = (z[:, :h, :], z[:, h:, :])
        ca = _causal_dw_conv(za, w_a, b_a)
        cb = _causal_dw_conv(zb, w_b, b_b)
        gated_a = ca * jax.nn.sigmoid(cb)
        gated_b = cb * jax.nn.sigmoid(ca)
        cat = jnp.concatenate([gated_a, gated_b], axis=1)
        return jnp.einsum('bet,he->bth', cat, w_out) + b_out[None, None, :]

    def _L3_ffn_ref(x, wqkv, q_scale, k_scale, wo, ln_g, ln_b, w1, b1, w2, b2):
        import jax, jax.numpy as jnp
        import numpy as np
        DIM = 128
        DEPTH = 2
        HEADS = 8
        DIM_HEAD = 64
        WINDOW = 64
        INNER = HEADS * DIM_HEAD
        HID = int(DIM * 4 * 2 / 3)
        B, N = (2, 1024)
        QK_SCALE = 8.0

        def shift_token(t):
            t1, t2 = jnp.split(t, 2, axis=-1)
            t2 = jnp.pad(t2, ((0, 0), (1, 0), (0, 0)))[:, :-1]
            return jnp.concatenate([t1, t2], axis=-1)

        def l2norm(t):
            return t / jnp.clip(jnp.linalg.norm(t, axis=-1, keepdims=True), 1e-12)

        def rotate_half(x):
            x1, x2 = jnp.split(x, 2, axis=-1)
            return jnp.concatenate([-x2, x1], axis=-1)

        def rotary_xpos(q, k):
            n = q.shape[-2]
            half_idx = jnp.arange(0, DIM_HEAD, 2, dtype=jnp.float32)
            inv_freq = 1.0 / 10000.0 ** (half_idx / DIM_HEAD)
            t = jnp.arange(n, dtype=jnp.float32)
            freqs = t[:, None] * inv_freq[None, :]
            freqs = jnp.concatenate([freqs, freqs], axis=-1)
            base = (half_idx + 0.4 * DIM_HEAD) / (1.4 * DIM_HEAD)
            power = (t - n // 2) / float(WINDOW // 2)
            scale = base[None, :] ** power[:, None]
            scale = jnp.concatenate([scale, scale], axis=-1)
            cos, sin = (jnp.cos(freqs), jnp.sin(freqs))
            q = q * cos * scale + rotate_half(q) * sin * scale
            k = k * cos / scale + rotate_half(k) * sin / scale
            return (q, k)

        def local_attention(q, k, v):
            b, h, n, d = q.shape
            w = n // WINDOW
            bq = q.reshape(b, h, w, WINDOW, d) * QK_SCALE
            bk = k.reshape(b, h, w, WINDOW, d)
            bv = v.reshape(b, h, w, WINDOW, d)

            def look_around(t):
                p = jnp.pad(t, ((0, 0), (0, 0), (1, 0), (0, 0), (0, 0)))
                return jnp.concatenate([p[:, :, :w], p[:, :, 1:]], axis=3)
            bk, bv = (look_around(bk), look_around(bv))
            bt = jnp.arange(n).reshape(w, WINDOW)
            btp = jnp.pad(bt, ((1, 0), (0, 0)), constant_values=-1)
            btk = jnp.concatenate([btp[:w], btp[1:]], axis=1)
            sim = jnp.einsum('bhwid,bhwjd->bhwij', bq, bk)
            i = bt[:, :, None]
            j = btk[:, None, :]
            mask = (i < j) | (i > j + WINDOW) | (j == -1)
            sim = jnp.where(mask, -jnp.finfo(sim.dtype).max, sim)
            attn = jax.nn.softmax(sim, axis=-1)
            out = jnp.einsum('bhwij,bhwjd->bhwid', attn, bv)
            return out.reshape(b, h, n, d)

        def _layer(x, wqkv, qs, ksc, wo, lg, lb, w1, b1, w2, b2):
            b, n, _ = x.shape
            h = shift_token(x)
            qkv = h @ wqkv
            q, k, v = jnp.split(qkv, 3, axis=-1)
            to_heads = lambda t: t.reshape(b, n, HEADS, DIM_HEAD).transpose(0, 2, 1, 3)
            q, k, v = (to_heads(q), to_heads(k), to_heads(v))
            q = l2norm(q) * qs
            k = l2norm(k) * ksc
            q, k = rotary_xpos(q, k)
            o = local_attention(q, k, v)
            o = o.transpose(0, 2, 1, 3).reshape(b, n, INNER)
            x = x + o @ wo
            h = shift_token(x)
            mu = h.mean(-1, keepdims=True)
            var = h.var(-1, keepdims=True)
            h = (h - mu) / jnp.sqrt(var + 1e-05) * lg + lb
            h = h @ w1 + b1
            a, g = jnp.split(h, 2, axis=-1)
            h = a * jax.nn.gelu(g, approximate=False)
            x = x + h @ w2 + b2
            return x
        for l in range(DEPTH):
            x = _layer(x, wqkv[l], q_scale[l], k_scale[l], wo[l], ln_g[l], ln_b[l], w1[l], b1[l], w2[l], b2[l])
        return x
    x = L0_attn_x
    xn = _layernorm(x, axis=-1)
    s = _L0_attn_ref(xn, L0_attn_wq, L0_attn_wk_down, L0_attn_wv_down, L0_attn_wk_up, L0_attn_wv_up, L0_attn_wo)
    g = _silu(_L0_ffn_ref(xn, L0_ffn_switch_w, L0_ffn_switch_b, L0_ffn_w1, L0_ffn_b1, L0_ffn_w2, L0_ffn_b2))
    x = x + s * g
    xn = _layernorm(x, axis=-1)
    s = _L1_attn_ref(xn, L1_attn_w_qkv, L1_attn_w_out, L1_attn_b_out)
    g = _silu(_L1_ffn_ref(xn, L1_ffn_w_gate, L1_ffn_w_up, L1_ffn_w_down))
    x = x + s * g
    xn = _layernorm(x, axis=-1)
    s = _L2_attn_ref(xn, L2_attn_ln_gamma, L2_attn_ln_beta, L2_attn_W_in, L2_attn_b_in, L2_attn_conv_w, L2_attn_conv_b, L2_attn_W_delta, L2_attn_b_delta, L2_attn_W_out, L2_attn_b_out)
    g = _silu(_L2_ffn_ref(xn, L2_ffn_W1, L2_ffn_b1, L2_ffn_W2, L2_ffn_b2))
    x = x + s * g
    xn = _layernorm(x, axis=-1)
    s = _L3_attn_ref(xn, L3_attn_w_in, L3_attn_b_in, L3_attn_w_a, L3_attn_b_a, L3_attn_w_b, L3_attn_b_b, L3_attn_w_out, L3_attn_b_out)
    g = _silu(_L3_ffn_ref(xn, L3_ffn_wqkv, L3_ffn_q_scale, L3_ffn_k_scale, L3_ffn_wo, L3_ffn_ln_g, L3_ffn_ln_b, L3_ffn_w1, L3_ffn_b1, L3_ffn_w2, L3_ffn_b2))
    x = x + s * g
    return x

_drawn_inputs = setup_inputs


def setup_inputs(seed=0):
    import zlib

    import numpy as np

    out = dict(_drawn_inputs(seed))
    spreads = {'L0_ffn_switch_b': (0.0, 0.504),
     'L0_ffn_b1': (0.0, 0.8),
     'L0_ffn_b2': (0.0, 0.644),
     'L2_attn_ln_gamma': (1.0, 0.6),
     'L2_attn_ln_beta': (0.0, 0.8),
     'L2_attn_b_in': (0.0, 0.8),
     'L2_attn_conv_b': (0.0, 0.8),
     'L2_attn_b_delta': (0.0, 0.8),
     'L2_attn_b_out': (0.0, 0.8),
     'L3_ffn_q_scale': (1.0, 0.6),
     'L3_ffn_k_scale': (1.0, 0.6),
     'L3_ffn_ln_g': (1.0, 0.6),
     'L3_ffn_ln_b': (0.0, 0.8),
     'L3_ffn_b1': (0.0, 0.8),
     'L3_ffn_b2': (0.0, 0.8)}
    factors = {'L2_attn_W_in': 8.0,
     'L2_attn_conv_w': 8.0,
     'L2_attn_W_delta': 8.0,
     'L2_attn_W_out': 8.0,
     'L2_ffn_W1': 5.65,
     'L2_ffn_b1': 8.0,
     'L2_ffn_W2': 5.603,
     'L2_ffn_b2': 8.0,
     'L3_attn_w_in': 2.943,
     'L3_attn_b_in': 8.0,
     'L3_attn_w_a': 3.853,
     'L3_attn_b_a': 8.0,
     'L3_attn_w_b': 3.74,
     'L3_attn_b_b': 8.0,
     'L3_attn_w_out': 2.924,
     'L3_attn_b_out': 8.0,
     'L3_ffn_wqkv': 8.0,
     'L3_ffn_wo': 8.0,
     'L3_ffn_w1': 8.0,
     'L3_ffn_w2': 8.0}
    for name, (base, spread) in spreads.items():
        noise = np.random.default_rng([zlib.crc32(name.encode()), seed]).standard_normal(out[name].shape)
        drawn = base * np.exp(spread * noise) if base else spread * noise
        out[name] = jnp.asarray(drawn.astype(out[name].dtype))
    for name, factor in factors.items():
        out[name] = (out[name] * factor).astype(out[name].dtype)
    return out
```

```python
from contextlib import ExitStack

import numpy as np

import concourse.bass as bass
from concourse import mybir

F32 = mybir.dt.float32
I32 = mybir.dt.int32
ALU = mybir.AluOpType
ACT = mybir.ActivationFunctionType
AX = mybir.AxisListType

P = 128
B, T = 32, 256
N = B * T
C = 512
ROUNDS = N // (2 * C)
PAIRS = B // 2
EPS = 1e-5
NEG = -3.0e38
PRIME = 64

HEADS, N_KV, LAT = 8, 2, 32
EXPERTS, FF0 = 8, 512
HD1, HID1 = 8, 384
INNER, TAPS2, GROUPS, INTER = 256, 3, 8, 512
TAPS3, DEPTH, DH, WINDOW, HID3 = 32, 2, 64, 64, 341
QKV = 3 * HEADS * DH
BLK = 32


class Step:

    def __init__(self, sem, by):
        self.sem, self.by, self.base, self.per = sem, by, by * PRIME, 0
        self.inc = (sem, by)

    def at(self, i, n=0):
        first = self.base + (n + 1) * self.by
        return (self.sem, i * (self.per * self.by) + first)


class Stage:

    def __init__(self, rounds, early=(), **per):
        self.rounds, self.early, self.per = rounds, early, per

    def __enter__(self):
        for name, per in self.per.items():
            STEPS[name].per = per
            STEPS[name].base += (name in self.early) * per * STEPS[name].by

    def __exit__(self, *_):
        for name, per in self.per.items():
            STEPS[name].base += self.rounds * per * STEPS[name].by
            STEPS[name].per = 0


STEPS = {}
NUMBER = []
COMPUTE = [
    "mean", "centered", "squared", "variance", "deviation", "logged", "scaled", "normed", "copied",
    "projected", "freed_act", "freed_dve", "scores", "masked", "rowmax", "exps", "turned", "turned_sb",
    "mixed", "rowsum", "attended", "table", "sumsq", "rnorm", "straight", "crossed", "rotated", "unit",
    "up", "act_a", "act_b", "gated", "down", "silu", "weighed", "added", "prep", "prep_sb",
    "m1", "m2", "m3", "m4", "v1", "v2", "v3", "v4", "v5", "v6", "v7", "v8", "v9", "a1", "a2", "a3",
    "a4", "g1", "g2", "g3", "g4", "g5", "t_add", "first",
]
MOVES = ["loaded", "stored", "fetched0", "fetched1"]


def cols(i, u, width, parts=2):
    return bass.ds(i * (parts * width) + u * width, width)


def build(nc, a, out):
    ctx = ExitStack()
    with ctx:
        def keep(name, shape, dt=F32):
            return ctx.enter_context(nc.sbuf_tensor(name, shape, dt))

        STEPS.clear()
        NUMBER.clear()
        for n in COMPUTE:
            STEPS[n] = Step(ctx.enter_context(nc.semaphore(n)), 1)
        for n in MOVES:
            STEPS[n] = Step(ctx.enter_context(nc.semaphore(n)), 16)
        m = {
            "x": keep("x_res", [P, N]),
            "xn": keep("xn", [P, N + T]),
            "s": keep("s_branch", [P, N]),
            "ident": keep("ident", [P, P]),
            "mean": keep("mean_matrix", [P, P]),
            "causal": keep("causal", [P, 2, T]),
            "band": keep("band", [P, 2, T]),
            "eps": keep("eps", [P, 1]),
            "half": keep("minus_half", [P, 16]),
        }
        ps = ctx.enter_context(nc.psum_tensor("banks", [P, 8, C], F32))

        start(nc, m, a)
        layer_norm(nc, ps, m, m["x"], m["xn"])
        latent_attention(nc, ps, m, a)
        experts(nc, ps, m, a)
        layer_norm(nc, ps, m, m["x"], m["xn"])
        linear_attention(nc, ps, m, a)
        integer_ffn(nc, ps, m, a)
        layer_norm(nc, ps, m, m["x"], m["xn"])
        layer_norm(nc, ps, m, m["xn"], m["s"], (a["L2_attn_ln_gamma"], a["L2_attn_ln_beta"]))
        scan_mixer(nc, ps, m, a)
        grouped_ffn(nc, ps, m, a)
        layer_norm(nc, ps, m, m["x"], m["xn"])
        conv_mixer(nc, ps, m, a)
        for layer in range(DEPTH):
            local_attention(nc, ps, m, a, layer)
            with nc.sbuf_tensor(f"h_norm{layer}", [P, N], F32) as h:
                layer_norm(nc, ps, m, m["xn"], h, (a["L3_ffn_ln_g"][layer], a["L3_ffn_ln_b"][layer]), shifted=True)
                gelu_ffn(nc, ps, m, a, layer, h)
        finish(nc, m, out)


def on_chip(nc, mem):
    NUMBER.append(len(NUMBER))
    return lambda name, *shape, dt=F32: mem.enter_context(nc.sbuf_tensor(f"{name}_{NUMBER[-1]}", list(shape), dt))


def bank(ps, n, *shape):
    size = int(np.prod(shape))
    v = ps[:, n, 0:size]
    if len(shape) == 1:
        return v
    names = "abc"[:len(shape)]
    return v.rearrange(f"p ({' '.join(names)}) -> p {' '.join(names)}", **dict(zip(names[1:], shape[1:])))


def start(nc, m, a):
    S = STEPS
    with nc.Block() as block:
        @block.sync
        def _(sp):
            for step in S.values():
                sp.sem_inc(step.sem, step.base)

        @block.gpsimd
        def _(pool):
            pool.memset(m["ident"][:], 0.0).then_inc(S["g1"].sem, 1)
            pool.memset(m["mean"][:], 1.0 / P)
            pool.memset(m["xn"][:, N:], 0.0)
            pool.memset(m["eps"][:], EPS)
            pool.memset(m["half"][:], -0.5)
            pool.memset(m["causal"][:], 0.0)
            pool.memset(m["band"][:], 0.0).then_inc(S["g1"].sem, 1)
            pool.wait_ge(S["g1"].sem, PRIME + 2)
            pool.affine_select(out=m["ident"][:], in_=m["ident"][:], compare_op=ALU.not_equal, fill=1.0,
                               base=0, pattern=[[-1, P]], channel_multiplier=1)
            for qb in range(2):
                pool.affine_select(out=m["causal"][:, qb, :], in_=m["causal"][:, qb, :], compare_op=ALU.is_ge,
                                   fill=NEG, base=qb * P, pattern=[[-1, T]], channel_multiplier=1)
                last = pool.affine_select(out=m["band"][:, qb, :], in_=m["band"][:, qb, :], compare_op=ALU.is_ge,
                                          fill=NEG, base=qb * P, pattern=[[-1, T]], channel_multiplier=1)
            last.then_inc(S["g1"].sem, 1)
            pool.wait_ge(S["g1"].sem, PRIME + 3)
            for qb in range(2):
                pool.affine_select(out=m["band"][:, qb, :], in_=m["band"][:, qb, :], compare_op=ALU.is_ge,
                                   fill=NEG, base=WINDOW - qb * P, pattern=[[1, T]], channel_multiplier=-1)
    S["g1"].base += 3
    load(nc, [(m["x"][:, k * (N // 8):(k + 1) * (N // 8)], a["x"][:, k * (N // 8):(k + 1) * (N // 8)]) for k in range(8)])


def load(nc, pairs):
    S = STEPS
    with nc.Block() as block:
        @block.sync
        def _(sp):
            for dst, src in pairs:
                sp.dma_start(dst, src).then_inc(S["loaded"].sem, 16)
            sp.wait_ge(S["loaded"].sem, S["loaded"].base + 16 * len(pairs))
    S["loaded"].base += 16 * len(pairs)


def column(vec):
    return vec.rearrange("(p o) -> p o", o=1)


def finish(nc, m, out):
    S = STEPS
    R = ROUNDS
    with ExitStack() as mem:
        gate = on_chip(nc, mem)("gate", P, 2, C)
        with Stage(R, silu=2, weighed=2, added=2), nc.Block() as block:
            @block.scalar
            def _(act):
                with act.Fori(0, R) as i:
                    for u in range(2):
                        act.wait_ge(*S["added"].at(i, u - 2))
                        act.wait_ge(S["first"].sem, PRIME)
                        act.activation(gate[:, u], m["xn"][:, cols(i, u, C)], ACT.Silu).then_inc(*S["silu"].inc)

            @block.vector
            def _(dve):
                with dve.Fori(0, R) as i:
                    for u in range(2):
                        add_gated(dve, m, gate, i, u)

            @block.sync
            def _(sp):
                with sp.Fori(0, R) as i:
                    for u in range(2):
                        sp.wait_ge(*S["added"].at(i, u))
                        sp.wait_ge(S["first"].sem, PRIME)
                        sp.dma_start(out[:, cols(i, u, C)], m["x"][:, cols(i, u, C)]).then_inc(S["stored"].sem, 16)
                sp.wait_ge(S["stored"].sem, 16 * (PRIME + 2 * R))


def add_gated(dve, m, gate, i, u):
    S = STEPS
    dve.wait_ge(*S["silu"].at(i, u))
    dve.tensor_tensor(gate[:, u], gate[:, u], m["s"][:, cols(i, u, C)], ALU.mult).then_inc(*S["weighed"].inc)
    dve.wait_ge(*S["weighed"].at(i, u))
    dve.tensor_tensor(m["x"][:, cols(i, u, C)], m["x"][:, cols(i, u, C)], gate[:, u], ALU.add)\
        .then_inc(*S["added"].inc)


def layer_norm(nc, ps, m, src, dst, affine=None, shifted=False):
    S, W = STEPS, 4
    R = N // (W * C)
    with ExitStack() as mem:
        buf = on_chip(nc, mem)

        xc, sq, sd = buf("ln_xc", P, W, C), buf("ln_sq", P, W, C), buf("ln_sd", P, W, C)
        hs = buf("ln_hs", P, W, 2, T) if shifted else None
        gb = buf("ln_gb", P, 2)
        if affine:
            load(nc, [(gb[:, 0:1], column(affine[0])), (gb[:, 1:2], column(affine[1]))])

        def source(i, u):
            if shifted:
                return hs[:, u].rearrange("p b t -> p (b t)")
            return src[:, cols(i, u, C, W)]

        with Stage(R, mean=W, centered=W, squared=W, variance=W, logged=W, deviation=W, scaled=W, normed=W,
                   copied=W), nc.Block() as block:
            @block.gpsimd
            def _(pool):
                if shifted:
                    pool.memset(hs[:], 0.0).then_inc(S["first"].sem, 1)
                    pool.wait_ge(S["first"].sem, S["first"].base + 1)
                    with pool.Fori(0, R) as i:
                        for u in range(W):
                            shift_in(pool, hs[:, u], src, i, u, C, S["centered"].at(i, u - W), W)

            @block.tensor
            def _(pe):
                with pe.Fori(0, R) as i:
                    for u in range(W):
                        if shifted:
                            pe.wait_ge(*S["copied"].at(i, u))
                        pe.wait_ge(*S["centered"].at(i, u - W))
                        pe.matmul(ps[:, u, :], m["mean"][:], source(i, u), start=True, stop=True)\
                            .then_inc(*S["mean"].inc)
                    for u in range(W):
                        pe.wait_ge(*S["squared"].at(i, u))
                        pe.wait_ge(*S["logged"].at(i, u - W))
                        pe.matmul(ps[:, W + u, :], m["mean"][:], sq[:, u], start=True, stop=True)\
                            .then_inc(*S["variance"].inc)

            @block.scalar
            def _(act):
                act.preload_act_table_set("natural_log_exp_and_others")
                with act.Fori(0, R) as i:
                    for u in range(W):
                        act.wait_ge(*S["centered"].at(i, u))
                        act.wait_ge(*S["variance"].at(i, u - W))
                        act.activation(sq[:, u], xc[:, u], ACT.Square).then_inc(*S["squared"].inc)
                    for u in range(W):
                        act.wait_ge(*S["variance"].at(i, u))
                        act.wait_ge(*S["normed"].at(i, u - W))
                        act.activation(sd[:, u], ps[:, W + u, :], ACT.Ln, bias=m["eps"][:, 0:1])\
                            .then_inc(*S["logged"].inc)
                        act.wait_ge(*S["logged"].at(i, u))
                        act.activation(sd[:, u], sd[:, u], ACT.Exp, scale=-0.5).then_inc(*S["deviation"].inc)

            @block.vector
            def _(dve):
                with dve.Fori(0, R) as i:
                    for u in range(W):
                        dve.wait_ge(*S["mean"].at(i, u))
                        dve.wait_ge(*S["normed"].at(i, u - W))
                        if shifted:
                            dve.wait_ge(*S["copied"].at(i, u))
                        dve.tensor_tensor(xc[:, u], source(i, u), ps[:, u, :], ALU.subtract)\
                            .then_inc(*S["centered"].inc)
                    for u in range(W):
                        dve.wait_ge(*S["deviation"].at(i, u))
                        if affine:
                            dve.tensor_tensor(xc[:, u], xc[:, u], sd[:, u], ALU.mult).then_inc(*S["scaled"].inc)
                            dve.wait_ge(*S["scaled"].at(i, u))
                            dve.tensor_scalar(dst[:, cols(i, u, C, W)], xc[:, u], gb[:, 0:1], gb[:, 1:2], ALU.mult,
                                              ALU.add).then_inc(*S["normed"].inc)
                        else:
                            dve.tensor_tensor(dst[:, cols(i, u, C, W)], xc[:, u], sd[:, u], ALU.mult)\
                                .then_inc(*S["normed"].inc)
        skip(affine is None, R, "scaled", W)
        skip(not shifted, R, "copied", W)
        if shifted:
            S["first"].base += 1


def skip(unused, rounds, name, per):
    if unused:
        STEPS[name].base -= rounds * per * STEPS[name].by


def shift_in(pool, dst, src, i, u, width, free, parts=2, first=None):
    S = STEPS
    seqs = width // T
    pool.wait_ge(*free)
    pool.wait_ge(S["first"].sem, PRIME)
    for b in range(seqs):
        at = (i * (parts * width) + u * width if first is None else first) + b * T
        pool.tensor_copy(dst[0:64, b, :], src[0:64, bass.ds(at, T)])
        last = pool.tensor_copy(dst[64:128, b, 1:T], src[64:128, bass.ds(at, T - 1)])
    last.then_inc(*S["copied"].inc)



UNITS = [(u, qb, par, pp) for u in range(2) for qb in range(2) for par in range(2) for pp in range(2)]
TURN, MIX = 2, 3
STEPS_T = 22


def heads_of(pp, par):
    return [(a, 2 * pp + a, 2 * (2 * pp + a) + par) for a in range(2)]


def pass_over(eng, name, n, count):
    if count:
        eng.wait_ge(*STEPS[name].at(-1, n - 1))
        eng.sem_inc(STEPS[name].sem, count)


def first_ones(eng, name, events, made, make, first=0):
    skipped = 0
    for n, x in enumerate(events):
        if made(x):
            pass_over(eng, name, first + n - skipped, skipped)
            skipped = 0
            make(x)
        else:
            skipped += 1
    pass_over(eng, name, first + len(events) - skipped, skipped)


class Core:

    def __init__(self, nc, ps, m, mem, mask, scale, dv, k_tile, v_at):
        buf = on_chip(nc, mem)
        self.ps, self.m, self.mask, self.scale, self.dv, self.k_tile, self.v_at = ps, m, mask, scale, dv, k_tile, v_at
        self.tiles = 4 if dv == DH else 2
        self.qt = buf("qt", P, 2, 4, T)
        self.kt = buf("kt", P, 2, self.tiles, T)
        self.v = buf("v_tok", P, 2, 2, HEADS * DH if dv == DH else N_KV * LAT)
        self.pr = buf("probs", P, 4, 2, T)
        self.nm = buf("minus_max", P, 4, 2)
        self.pt = buf("probs_t", P, 2, C)
        self.sums = buf("row_sums", P, 2, 2, HEADS)
        self.rs = buf("inv_sums", P, 2, 2, HEADS)
        self.o = buf("attended_tok", P, 2, HEADS * dv)

    def pe_step(self, pe, i, t, ready):
        S, ps = STEPS, self.ps
        if t < 16:
            u, qb, par, pp = UNITS[t]
            rows, nk = slice(64 * par, 64 * par + 64), P * (qb + 1)
            if t % 8 == 0:
                for what in ready(i, u):
                    pe.wait_ge(*what)
            pe.wait_ge(*S["masked"].at(i, t - 2))
            for a, tile, head in heads_of(pp, par):
                mm = pe.matmul(ps[:, t % 2, a * T:a * T + nk], self.qt[rows, u, tile, qb * P:(qb + 1) * P],
                               self.kt[rows, u, self.k_tile(tile), 0:nk], start=True, stop=True)
            mm.then_inc(*S["scores"].inc)
        n = t - TURN
        if 0 <= n < 16:
            u, qb, par, pp = UNITS[n]
            pe.wait_ge(*S["exps"].at(i, n))
            pe.wait_ge(*S["turned_sb"].at(i, n - 2))
            for a in range(2):
                for kb in range(qb + 1):
                    mm = pe.transpose(ps[:, 2 + n % 2, (2 * a + kb) * P:(2 * a + kb + 1) * P],
                                      self.pr[:, n % 4, a, kb * P:(kb + 1) * P], self.m["ident"][:])
            mm.then_inc(*S["turned"].inc)
        n = t - MIX
        if 0 <= n < 16:
            u, qb, par, pp = UNITS[n]
            pe.wait_ge(*S["turned_sb"].at(i, n))
            if n % 4 == 0:
                pe.wait_ge(*S["attended"].at(i, n // 4 - 2))
            for a, tile, head in heads_of(pp, par):
                at = self.v_at(head)
                for kb in range(qb + 1):
                    mm = pe.matmul(ps[:, 4 + qb, head * self.dv:(head + 1) * self.dv],
                                   self.pt[:, n % 2, (2 * a + kb) * P:(2 * a + kb + 1) * P],
                                   self.v[:, u, kb, at:at + self.dv], start=(kb == 0), stop=(kb == qb))
            mm.then_inc(*S["mixed"].inc)

    def act_step(self, act, i, t):
        S, ps = STEPS, self.ps
        if t < 16:
            u, qb, par, pp = UNITS[t]
            nk = P * (qb + 1)
            act.wait_ge(*S["rowmax"].at(i, t))
            if t % 4 == 0:
                act.wait_ge(*S["attended"].at(i, t // 4 - 4))
            for a, tile, head in heads_of(pp, par):
                scores = self.pr[:, t % 4, a, 0:nk]
                last = act.activation(scores, scores, ACT.Exp, bias=self.nm[:, t % 4, a:a + 1],
                                      accum_out=self.sums[:, u, qb, head:head + 1])
            last.then_inc(*S["exps"].inc)
        n = t - TURN
        if 0 <= n < 16:
            qb = UNITS[n][1]
            act.wait_ge(*S["turned"].at(i, n))
            act.wait_ge(*S["mixed"].at(i, n - 2))
            nk = P * (qb + 1)
            act.activation(self.pt[:, n % 2].rearrange("p (a k) -> p a k", a=2)[:, :, 0:nk],
                           bank(ps, 2 + n % 2, 2, T)[:, :, 0:nk], ACT.Copy).then_inc(*S["turned_sb"].inc)

    def dve_step(self, dve, i, t):
        S, ps = STEPS, self.ps
        if t < 16:
            u, qb, par, pp = UNITS[t]
            nk = P * (qb + 1)
            dve.wait_ge(*S["scores"].at(i, t))
            dve.wait_ge(*S["turned"].at(i, t - 4))
            dve.scalar_tensor_tensor(self.pr[:, t % 4, :, 0:nk], bank(ps, t % 2, 2, T)[:, :, 0:nk], self.scale,
                                     self.mask[:, qb:qb + 1, 0:nk].to_broadcast([P, 2, nk]), ALU.mult, ALU.add)\
                .then_inc(*S["masked"].inc)
            dve.wait_ge(*S["masked"].at(i, t))
            dve.tensor_reduce(self.nm[:, t % 4, :], self.pr[:, t % 4, :, 0:nk], AX.X, ALU.max, negate=True)\
                .then_inc(*S["rowmax"].inc)
        n = t - MIX - 1
        if 0 <= n < 16 and n % 4 == 3:
            u, qb = UNITS[n][0:2]
            dve.wait_ge(*S["mixed"].at(i, n))
            dve.reciprocal(self.rs[:, u, qb], self.sums[:, u, qb]).then_inc(*S["rowsum"].inc)
            dve.wait_ge(*S["rowsum"].at(i, n // 4))
            dve.wait_ge(*S["projected"].at(*self.o_read(i, n // 4)))
            dve.tensor_tensor(self.o[:, qb].rearrange("p (h d) -> p h d", h=HEADS),
                              bank(ps, 4 + qb, HEADS, self.dv),
                              self.rs[:, u, qb].unsqueeze(2).to_broadcast([P, HEADS, self.dv]), ALU.mult)\
                .then_inc(*S["attended"].inc)


CORE = dict(scores=16, masked=16, rowmax=16, exps=16, turned=16, turned_sb=16, mixed=16, rowsum=4, attended=4)


def latent_attention(nc, ps, m, a):
    S = STEPS
    with ExitStack() as mem:
        buf = on_chip(nc, mem)

        wqt, wkut, wvut, wo = buf("wqt", P, HEADS, P), buf("wkut", P, LAT), buf("wvut", P, LAT), buf("wo0", P, HEADS, P)
        wkd, wvd = buf("wkd", P, N_KV * LAT), buf("wvd", P, N_KV * LAT)
        wq, wk, wv = buf("wq_lat", P, HEADS, 64), buf("wk_lat", P, N_KV, 2, 64), buf("wo_lat", P, 2, P)
        xf, ot = buf("xf", P, 2, T), buf("ot", P, 2, 2, T)
        core = Core(nc, ps, m, mem, m["causal"], float(P) ** -0.5, LAT, lambda tile: tile // 2,
                    lambda head: head // 4 * LAT)
        load(nc, [(wqt[:], a["L0_attn_wq"]), (wkut[:], a["L0_attn_wk_up"]), (wvut[:], a["L0_attn_wv_up"]),
                  (wo[:], a["L0_attn_wo"].rearrange("(h d) o -> d h o", d=P)),
                  (wkd[:], a["L0_attn_wk_down"]), (wvd[:], a["L0_attn_wv_down"])])

        with Stage(1, prep=1, prep_sb=2), nc.Block() as block:
            @block.tensor
            def _(pe):
                for h in range(HEADS):
                    pe.matmul(ps[:, 0, h * LAT:(h + 1) * LAT], wqt[:, h], wkut[:], start=True, stop=True)
                for h in range(HEADS):
                    mm = pe.matmul(ps[32 * (h % 4):32 * (h % 4) + 32, 1, (h // 4) * P:(h // 4 + 1) * P], wvut[:],
                                   wo[:, h], start=True, stop=True)
                mm.then_inc(*S["prep"].inc)

            @block.vector
            def _(dve):
                dve.memset(wq[:], 0.0)
                dve.memset(wk[:], 0.0).then_inc(*S["prep_sb"].inc)
                dve.wait_ge(*S["prep_sb"].at(0, 0))
                dve.wait_ge(*S["prep"].at(0, 0))
                dve.tensor_copy(wq[:, :, 0:LAT], bank(ps, 0, HEADS, LAT))
                dve.tensor_copy(wv[:], bank(ps, 1, 2, P))
                for half in range(2):
                    last = dve.tensor_copy(wk[:, :, half, 0:LAT], wkd[:].rearrange("p (k l) -> p k l", k=N_KV))
                last.then_inc(*S["prep_sb"].inc)

        when = {t: [] for t in range(STEPS_T)}
        for k in range(4):
            when[2 + k].append((1, k))
            when[10 + k].append((0, k))
        for u in range(2):
            when[8 * u + 12].append((u, 4))
            when[8 * u + 13].append((u, 5))
        order = [x for t in range(STEPS_T) for x in when[t]]
        at = {x: n for n, x in enumerate(order)}
        PER = len(order)
        core.o_read = lambda i, w: (i, at[0, 4] if w >= 2 else at[1, 4] - PER)
        early = lambda x: x[0] == 0 and x[1] < 4

        def pe_part(pe, i, x):
            u, k = x
            e = at[x]
            o = ps[:, 6 + e % 2]
            pe.wait_ge(*S["freed_dve"].at(i, e - 2))
            if k < 2:
                if k == 0:
                    pe.wait_ge(*S["copied"].at(i, 1 - u))
                for tile in range(2):
                    mm = pe.matmul(o[:, tile * T:(tile + 1) * T],
                                   wq[:, 2 * (2 * k + tile):2 * (2 * k + tile) + 2].rearrange("p h l -> p (h l)"),
                                   xf[:, u], start=True, stop=True)
            elif k == 2:
                for kv in range(N_KV):
                    mm = pe.matmul(o[:, kv * T:(kv + 1) * T], wk[:, kv].rearrange("p h l -> p (h l)"),
                                   xf[:, u], start=True, stop=True)
            elif k == 3:
                for tb in range(2):
                    mm = pe.matmul(o[:, tb * 64:(tb + 1) * 64], xf[:, u, tb * P:(tb + 1) * P], wvd[:],
                                   start=True, stop=True)
            elif k == 4:
                pe.wait_ge(*S["attended"].at(i, 2 * u + 1))
                for c in range(2):
                    for qb in range(2):
                        mm = pe.transpose(o[:, (2 * c + qb) * P:(2 * c + qb + 1) * P],
                                          core.o[:, qb, c * P:(c + 1) * P], m["ident"][:])
            else:
                pe.wait_ge(*S["freed_dve"].at(i, at[u, 4]))
                for c in range(2):
                    mm = pe.matmul(o[:, 0:T], wv[:, c], ot[:, u, c], start=(c == 0), stop=(c == 1))
            mm.then_inc(*S["projected"].inc)

        def dve_part(dve, i, x):
            u, k = x
            dve.wait_ge(*S["projected"].at(i, at[x]))
            if k == 0:
                dve.wait_ge(*S["scores"].at(i, -1 if u else 7))
            if k == 3:
                dve.wait_ge(*S["mixed"].at(i, -1 if u else 7))
            src = ps[:, 6 + at[x] % 2]
            if k < 2:
                last = dve.tensor_copy(core.qt[:, u, 2 * k:2 * k + 2].rearrange("p a t -> p (a t)"), src)
            elif k == 2:
                last = dve.tensor_copy(core.kt[:, u].rearrange("p a t -> p (a t)"), src)
            elif k == 3:
                last = dve.tensor_copy(core.v[:, u].rearrange("p a t -> p (a t)"), src[:, 0:P])
            elif k == 4:
                last = dve.tensor_copy(ot[:, u].rearrange("p a t -> p (a t)"), src)
            else:
                last = dve.tensor_copy(m["s"][:, cols(i, u, T)], src[:, 0:T])
            last.then_inc(*S["freed_dve"].inc)

        with Stage(PAIRS, ["copied", "projected", "freed_dve"], copied=2, projected=PER, freed_dve=PER, **CORE), \
                nc.Block() as block:
            @block.gpsimd
            def _(pool):
                pass_over(pool, "copied", 0, 1)
                pool.tensor_copy(xf[:, 0], m["xn"][:, 0:T]).then_inc(*S["copied"].inc)
                with pool.Fori(0, PAIRS) as i:
                    for u in (1, 0):
                        pool.wait_ge(*S["projected"].at(i, at[u, 3] - PER))
                        pool.wait_ge(S["first"].sem, PRIME)
                        at_u = bass.ds(i * (2 * T) + (T if u else 2 * T), T)
                        pool.tensor_copy(xf[:, u], m["xn"][:, at_u]).then_inc(*S["copied"].inc)

            @block.tensor
            def _(pe):
                first_ones(pe, "projected", order, early, lambda x: pe_part(pe, -1, x))
                with pe.Fori(0, PAIRS) as i:
                    for t in range(STEPS_T):
                        core.pe_step(pe, i, t, lambda i, u: [S["freed_dve"].at(i, at[u, 3] - (0 if u else PER))])
                        for x in when[t]:
                            pe_part(pe, i, x)

            @block.scalar
            def _(act):
                with act.Fori(0, PAIRS) as i:
                    for t in range(STEPS_T):
                        core.act_step(act, i, t)

            @block.vector
            def _(dve):
                first_ones(dve, "freed_dve", order, early, lambda x: dve_part(dve, -1, x))
                with dve.Fori(0, PAIRS) as i:
                    for t in range(STEPS_T):
                        core.dve_step(dve, i, t)
                        for x in when[t]:
                            dve_part(dve, i, x)


def experts(nc, ps, m, a):
    S, R = STEPS, ROUNDS
    FT = FF0 // P
    with ExitStack() as mem:
        buf = on_chip(nc, mem)

        w1, w2 = buf("w1e", P, EXPERTS, FF0), buf("w2e", P, EXPERTS, FT, P)
        b1, b2 = buf("b1e", P, EXPERTS, FT), buf("b2e", EXPERTS, P)
        sw, sb = buf("switch_w", P, EXPERTS), buf("switch_b", P, EXPERTS)
        rank = buf("rank", P, EXPERTS)
        rank_i = buf("rank_i", P, EXPERTS, dt=I32)
        pick = buf("pick", EXPERTS, EXPERTS, P)
        xf, lg, ex, r1 = buf("xf", P, 2, C), buf("lg", P, 2, 4, 8), buf("ex", P, 2, 4, 8), buf("r1", P, 2, 4, 4)
        oh, gt = buf("oh", P, 2, 4, 8), buf("gt", EXPERTS, 2, C)
        hid, wt, gate = buf("hid", P, 2, C), buf("wt", P, 2, C), buf("gate", P, 2, C)
        load(nc, [(w1[:, e], a["L0_ffn_w1"][e]) for e in range(EXPERTS)]
             + [(w2[:, e], a["L0_ffn_w2"][e].rearrange("(f p) d -> p f d", p=P)) for e in range(EXPERTS)]
             + [(b1[:], a["L0_ffn_b1"]), (b2[:], a["L0_ffn_b2"]), (sw[:], a["L0_ffn_switch_w"]),
                (sb[:], a["L0_ffn_switch_b"].partition_broadcast(P))])
        HID = EXPERTS * FT
        with Stage(R, copied=2, projected=2, prep=2, prep_sb=2, v1=2, v2=2, v3=2, v4=2, v5=2, v6=2, v7=2, v8=2,
                   a1=2, m2=2 * EXPERTS, m3=2 * HID, a2=2 * HID, v9=2 * HID, silu=2, weighed=2, added=2,
                   down=2 * HID, first=2), nc.Block() as block:
            @block.gpsimd
            def _(pool):
                pool.iota(rank_i[:], pattern=[[-1, EXPERTS]], base=EXPERTS, channel_multiplier=0)
                pool.memset(pick[:], 0.0).then_inc(S["g5"].sem, 1)
                pool.wait_ge(S["g5"].sem, S["g5"].base + 1)
                pool.tensor_copy(rank[:], rank_i[:])
                pool.affine_select(out=pick[:], in_=pick[:], compare_op=ALU.not_equal, fill=1.0, base=0,
                                   pattern=[[-1, EXPERTS], [0, P]], channel_multiplier=1).then_inc(S["g5"].sem, 1)
                with pool.Fori(0, R) as i:
                    for u in range(2):
                        pool.wait_ge(*S["m3"].at(i, HID * (u + 1) - 1 - 2 * HID))
                        pool.wait_ge(S["first"].sem, PRIME)
                        pool.tensor_copy(xf[:, u], m["xn"][:, cols(i, u, C)]).then_inc(*S["copied"].inc)

            @block.tensor
            def _(pe):
                pe.wait_ge(S["g5"].sem, S["g5"].base + 2)
                with pe.Fori(0, R) as i:
                    for u in range(2):
                        pe.wait_ge(*S["copied"].at(i, u))
                        pe.wait_ge(*S["v1"].at(i, -1))
                        for k in range(4):
                            mm = pe.matmul(ps[:, 0, u * 64 + 8 * k:u * 64 + 8 * k + 8], xf[:, u, k * P:(k + 1) * P],
                                           sw[:], start=True, stop=True)
                        mm.then_inc(*S["projected"].inc)
                    for u in range(2):
                        pe.wait_ge(*S["v8"].at(i, u))
                        pe.wait_ge(*S["prep_sb"].at(i, u - 1))
                        for k in range(4):
                            mm = pe.transpose(ps[0:8, 1, k * P:(k + 1) * P], oh[:, u, k], m["ident"][:])
                        mm.then_inc(*S["prep"].inc)
                    for u in range(2):
                        pe.wait_ge(*S["prep_sb"].at(i, u))
                        pe.wait_ge(*S["silu"].at(i, u - 2))
                        pe.matmul(ps[:, 6 + u, :], b2[:], gt[:, u], start=True, stop=False)
                        for e in range(EXPERTS):
                            n = EXPERTS * u + e
                            if n >= 2:
                                pe.wait_ge(*S["v9"].at(i, FT * (n - 1) - 1))
                            else:
                                pe.wait_ge(*S["v9"].at(i, FT * (n - 1) - 1))
                            pe.matmul(ps[:, 2 + e % 2, :], pick[:, e], gt[:, u], start=True, stop=True)\
                                .then_inc(*S["m2"].inc)
                            for f in range(FT + 1):
                                h = FT * n + f
                                if f < FT:
                                    pe.wait_ge(*S["a2"].at(i, h - 2))
                                    pe.matmul(ps[:, 4 + h % 2, :], w1[:, e, f * P:(f + 1) * P], xf[:, u],
                                              start=True, stop=True).then_inc(*S["m3"].inc)
                                if f >= 1:
                                    pe.wait_ge(*S["v9"].at(i, h - 1))
                                    mm = pe.matmul(ps[:, 6 + u, :], w2[:, e, f - 1], wt[:, (h - 1) % 2],
                                                   start=False, stop=(e == EXPERTS - 1 and f == FT))
                                    mm.then_inc(*S["down"].inc)

            @block.scalar
            def _(act):
                with act.Fori(0, R) as i:
                    for u in range(2):
                        act.wait_ge(*S["v3"].at(i, u))
                        act.wait_ge(*S["v5"].at(i, u - 2))
                        act.activation(ex[:, u], lg[:, u], ACT.Exp).then_inc(*S["a1"].inc)
                    for u in range(2):
                        for h in range(HID * u, HID * (u + 1)):
                            e, f = h // FT % EXPERTS, h % FT
                            act.wait_ge(*S["m3"].at(i, h))
                            act.wait_ge(*S["v9"].at(i, h - 2))
                            act.activation(hid[:, h % 2], ps[:, 4 + h % 2, :], ACT.Gelu_apprx_tanh,
                                           bias=b1[:, e, f:f + 1]).then_inc(*S["a2"].inc)
                        act.wait_ge(*S["down"].at(i, HID * (u + 1) - 1))
                        act.wait_ge(*S["added"].at(i, u - 2))
                        act.activation(gate[:, u], ps[:, 6 + u, :], ACT.Silu).then_inc(*S["silu"].inc)

            @block.vector
            def _(dve):
                dve.wait_ge(S["g5"].sem, S["g5"].base + 2)
                with dve.Fori(0, R) as i:
                    for u in range(2):
                        dve.wait_ge(*S["projected"].at(i, 1))
                        dve.tensor_tensor(lg[:, u], ps[:, 0, u * 64:u * 64 + 32].rearrange("p (k e) -> p k e", k=4),
                                          sb[:].unsqueeze(1).to_broadcast([P, 4, 8]), ALU.add).then_inc(*S["v1"].inc)
                        dve.wait_ge(*S["v1"].at(i, u))
                        dve.tensor_reduce(r1[:, u, :, 0], lg[:, u], AX.X, ALU.max).then_inc(*S["v2"].inc)
                        dve.wait_ge(*S["v2"].at(i, u))
                        dve.tensor_tensor(lg[:, u], lg[:, u], r1[:, u, :, 0:1].to_broadcast([P, 4, 8]),
                                          ALU.subtract).then_inc(*S["v3"].inc)
                        dve.wait_ge(*S["v3"].at(i, u))
                        dve.scalar_tensor_tensor(oh[:, u], lg[:, u], 0.0,
                                                 rank[:].unsqueeze(1).to_broadcast([P, 4, 8]), ALU.is_ge, ALU.mult)\
                            .then_inc(*S["v4"].inc)
                    for u in range(2):
                        dve.wait_ge(*S["a1"].at(i, u))
                        dve.tensor_reduce(r1[:, u, :, 1], ex[:, u], AX.X, ALU.add).then_inc(*S["v5"].inc)
                        dve.wait_ge(*S["v4"].at(i, u))
                        dve.tensor_reduce(r1[:, u, :, 2], oh[:, u], AX.X, ALU.max).then_inc(*S["v6"].inc)
                        dve.wait_ge(*S["v5"].at(i, u))
                        dve.reciprocal(r1[:, u, :, 3], r1[:, u, :, 1]).then_inc(*S["v7"].inc)
                        dve.wait_ge(*S["v6"].at(i, u))
                        dve.tensor_tensor(oh[:, u], oh[:, u], r1[:, u, :, 2:3].to_broadcast([P, 4, 8]),
                                          ALU.is_equal).then_inc(*S["first"].inc)
                        dve.wait_ge(*S["v7"].at(i, u))
                        dve.wait_ge(*S["first"].at(i, u))
                        dve.tensor_tensor(oh[:, u], oh[:, u], r1[:, u, :, 3:4].to_broadcast([P, 4, 8]),
                                          ALU.mult).then_inc(*S["v8"].inc)
                    for u in range(2):
                        dve.wait_ge(*S["prep"].at(i, u))
                        dve.wait_ge(*S["m2"].at(i, EXPERTS * (u + 1) - 1 - 2 * EXPERTS))
                        dve.tensor_copy(gt[:, u], ps[0:8, 1, :]).then_inc(*S["prep_sb"].inc)
                    for u in range(2):
                        for h in range(HID * u, HID * (u + 1)):
                            e = h // FT
                            dve.wait_ge(*S["m2"].at(i, e))
                            dve.wait_ge(*S["a2"].at(i, h))
                            dve.wait_ge(*S["down"].at(i, h - 2))
                            dve.tensor_tensor(wt[:, h % 2], hid[:, h % 2], ps[:, 2 + e % 2, :], ALU.mult)\
                                .then_inc(*S["v9"].inc)
                    for u in range(2):
                        add_gated(dve, m, gate, i, u)
        S["g5"].base += 2


def linear_attention(nc, ps, m, a):
    S = STEPS
    with ExitStack() as mem:
        buf = on_chip(nc, mem)

        wq, wout, bout, blocks = buf("wqkv1", P, 3 * P), buf("wout1", P, P), buf("bout1", P, 1), buf("blocks", P, P)
        xf, ks, kx, kp = buf("xf", P, 2, T), buf("k_min", P, 2, 2, P), buf("k_exp", P, 2, 2, P), buf("k_phi", P, 2, 2, P)
        va = buf("v_one", P, 2, 2, P + 1)
        qs, qx, qp = buf("q_min", P, 2, T), buf("q_exp", P, 2, T), buf("q_phi", P, 2, T)
        kv, kd = buf("kv_heads", P, 2, P), buf("k_heads", P, 2, P)
        z, y = buf("z_inv", P, 2, T), buf("y1", P, 2, T)
        load(nc, [(wq[:], a["L1_attn_w_qkv"]), (wout[:], a["L1_attn_w_out"]), (bout[:], column(a["L1_attn_b_out"]))])
        with Stage(PAIRS, copied=2, projected=2, m1=2, m2=2, m3=2, m4=2, v1=2, v2=2, v3=2, v4=2, v5=2, v6=2, v7=2,
                   v8=2, a1=2, a2=2, a3=2, a4=2), nc.Block() as block:
            @block.gpsimd
            def _(pool):
                pool.memset(va[:], 1.0)
                pool.memset(blocks[:], 1.0).then_inc(S["g5"].sem, 1)
                pool.wait_ge(S["g5"].sem, S["g5"].base + 1)
                view = blocks[:].rearrange("p (h d) -> p h d", d=HD1)
                pool.affine_select(out=view, in_=view, compare_op=ALU.is_ge, fill=0.0, base=0,
                                   pattern=[[-HD1, P // HD1], [0, HD1]], channel_multiplier=1)\
                    .then_inc(S["g5"].sem, 1)
                pool.wait_ge(S["g5"].sem, S["g5"].base + 2)
                pool.affine_select(out=view, in_=view, compare_op=ALU.is_ge, fill=0.0, base=HD1 - 1,
                                   pattern=[[HD1, P // HD1], [0, HD1]], channel_multiplier=-1)\
                    .then_inc(S["g5"].sem, 1)
                with pool.Fori(0, PAIRS) as i:
                    for u in range(2):
                        pool.wait_ge(*S["m1"].at(i, u - 2))
                        pool.wait_ge(S["first"].sem, PRIME)
                        pool.tensor_copy(xf[:, u], m["xn"][:, cols(i, u, T)]).then_inc(*S["copied"].inc)

            @block.tensor
            def _(pe):
                with pe.Fori(0, PAIRS) as i:
                    for u in range(2):
                        pe.wait_ge(*S["copied"].at(i, u))
                        pe.wait_ge(*S["v3"].at(i, u - 2))
                        pe.wait_ge(*S["a2"].at(i, u - 2))
                        for tb in range(2):
                            mm = pe.matmul(ps[:, u, tb * 2 * P:(tb + 1) * 2 * P], xf[:, u, tb * P:(tb + 1) * P],
                                           wq[:, P:3 * P], start=True, stop=True)
                        mm.then_inc(*S["projected"].inc)
                        pe.wait_ge(*S["v6"].at(i, u - 2))
                        pe.wait_ge(*S["v8"].at(i, u - 2))
                        pe.matmul(ps[:, 2 + u, 0:T], wq[:, 0:P], xf[:, u], start=True, stop=True)\
                            .then_inc(*S["m1"].inc)
                    for u in range(2):
                        pe.wait_ge(*S["v3"].at(i, u))
                        pe.wait_ge(*S["a2"].at(i, u))
                        pe.wait_ge(*S["v5"].at(i, u - 2))
                        for tb in range(2):
                            mm = pe.matmul(ps[:, 4 + u, 0:P + 1], kp[:, u, tb], va[:, u, tb], start=(tb == 0),
                                           stop=(tb == 1))
                        mm.then_inc(*S["m2"].inc)
                    for u in range(2):
                        pe.wait_ge(*S["v6"].at(i, u))
                        pe.wait_ge(*S["v5"].at(i, u))
                        pe.wait_ge(*S["v8"].at(i, u - 2))
                        pe.wait_ge(*S["a4"].at(i, u - 2))
                        pe.matmul(ps[:, 6 + u, 0:T], kv[:, u], qp[:, u], start=True, stop=True)
                        pe.matmul(ps[:, 6 + u, T:2 * T], kd[:, u], qp[:, u], start=True, stop=True)\
                            .then_inc(*S["m3"].inc)
                    for u in range(2):
                        pe.wait_ge(*S["v8"].at(i, u))
                        pe.matmul(ps[:, 6 + u, 0:T], wout[:], y[:, u], start=True, stop=True)\
                            .then_inc(*S["m4"].inc)

            @block.scalar
            def _(act):
                with act.Fori(0, PAIRS) as i:
                    for u in range(2):
                        act.wait_ge(*S["v1"].at(i, u))
                        act.wait_ge(*S["v3"].at(i, u - 2))
                        act.activation(kx[:, u], ks[:, u], ACT.Exp).then_inc(*S["a1"].inc)
                        act.wait_ge(*S["v2"].at(i, u))
                        act.wait_ge(*S["v6"].at(i, u - 2))
                        act.activation(qx[:, u], qs[:, u], ACT.Exp).then_inc(*S["a3"].inc)
                    for u in range(2):
                        act.wait_ge(*S["m4"].at(i, u))
                        act.wait_ge(S["first"].sem, PRIME)
                        act.activation(m["s"][:, cols(i, u, T)], ps[:, 6 + u, 0:T], ACT.Identity, bias=bout[:, 0:1])\
                            .then_inc(*S["a4"].inc)

            @block.vector
            def _(dve):
                dve.wait_ge(S["g5"].sem, S["g5"].base + 3)
                with dve.Fori(0, PAIRS) as i:
                    for u in range(2):
                        k_ps = bank(ps, u, 2, 2, P)[:, :, 0]
                        dve.wait_ge(*S["projected"].at(i, u))
                        dve.tensor_scalar(ks[:, u], k_ps, 0.0, None, ALU.min).then_inc(*S["v1"].inc)
                        dve.wait_ge(*S["m2"].at(i, u - 2))
                        dve.tensor_copy(va[:, u, :, 0:P], bank(ps, u, 2, 2, P)[:, :, 1]).then_inc(*S["a2"].inc)
                        dve.wait_ge(*S["m1"].at(i, u))
                        dve.tensor_scalar(qs[:, u], ps[:, 2 + u, 0:T], 0.0, None, ALU.min).then_inc(*S["v2"].inc)
                    for u in range(2):
                        k_ps = bank(ps, u, 2, 2, P)[:, :, 0]
                        dve.wait_ge(*S["a1"].at(i, u))
                        dve.wait_ge(*S["m2"].at(i, u - 2))
                        dve.scalar_tensor_tensor(kp[:, u], k_ps, 0.0, kx[:, u], ALU.max, ALU.add)\
                            .then_inc(*S["v3"].inc)
                        dve.wait_ge(*S["a3"].at(i, u))
                        dve.wait_ge(*S["m3"].at(i, u - 2))
                        dve.scalar_tensor_tensor(qp[:, u], ps[:, 2 + u, 0:T], 0.0, qx[:, u], ALU.max, ALU.add)\
                            .then_inc(*S["v6"].inc)
                    for u in range(2):
                        dve.wait_ge(*S["m2"].at(i, u))
                        dve.tensor_tensor(kv[:, u], ps[:, 4 + u, 0:P], blocks[:], ALU.mult)
                        dve.tensor_scalar(kd[:, u], blocks[:], ps[:, 4 + u, P:P + 1], None, ALU.mult)\
                            .then_inc(*S["v5"].inc)
                    for u in range(2):
                        dve.wait_ge(*S["m3"].at(i, u))
                        dve.tensor_scalar(z[:, u], ps[:, 6 + u, T:2 * T], 1e-6, None, ALU.add).then_inc(*S["v4"].inc)
                        dve.wait_ge(*S["v4"].at(i, u))
                        dve.reciprocal(z[:, u], z[:, u]).then_inc(*S["v7"].inc)
                        dve.wait_ge(*S["v7"].at(i, u))
                        dve.wait_ge(*S["m4"].at(i, u - 2))
                        dve.tensor_tensor(y[:, u], ps[:, 6 + u, 0:T], z[:, u], ALU.mult).then_inc(*S["v8"].inc)
        S["g5"].base += 3


def integer_ffn(nc, ps, m, a):
    S, R = STEPS, ROUNDS
    FT = HID1 // P
    with ExitStack() as mem:
        buf = on_chip(nc, mem)

        raw = buf("raw", P, 3, HID1, dt=I32)
        w = buf("w_deq", P, 3, HID1)
        sg, hd, gate = buf("silu_gate", P, 2, C), buf("hid1", P, 2, C), buf("gate", P, 2, C)
        load(nc, [(raw[:, 0], a["L1_ffn_w_gate"]), (raw[:, 1], a["L1_ffn_w_up"]),
                  (raw[:, 2].rearrange("p (f d) -> p f d", f=FT),
                   a["L1_ffn_w_down"].rearrange("(f p) d -> p f d", p=P))])
        with Stage(R, up=2 * FT, act_a=2 * FT, gated=2 * FT, m1=2 * FT, silu=2, weighed=2, added=2), nc.Block() as block:
            @block.tensor
            def _(pe):
                pe.wait_ge(S["g5"].sem, S["g5"].base + 2)
                with pe.Fori(0, R) as i:
                    for u in range(2):
                        for f in range(FT + 1):
                            h = FT * u + f
                            if f < FT:
                                pe.wait_ge(*S["gated"].at(i, h - 2))
                                for g in range(2):
                                    mm = pe.matmul(ps[:, 2 * (h % 2) + g, :], w[:, g, f * P:(f + 1) * P],
                                                   m["xn"][:, cols(i, u, C)], start=True, stop=True)
                                mm.then_inc(*S["up"].inc)
                            if f >= 1:
                                pe.wait_ge(*S["gated"].at(i, h - 1))
                                if f == 1:
                                    pe.wait_ge(*S["silu"].at(i, u - 2))
                                mm = pe.matmul(ps[:, 4 + u, :], w[:, 2, (f - 1) * P:f * P], hd[:, (h - 1) % 2],
                                               start=(f == 1), stop=(f == FT))
                                mm.then_inc(*S["m1"].inc)

            @block.scalar
            def _(act):
                with act.Fori(0, R) as i:
                    for u in range(2):
                        for h in range(FT * u, FT * (u + 1)):
                            act.wait_ge(*S["up"].at(i, h))
                            act.wait_ge(*S["gated"].at(i, h - 2))
                            act.activation(sg[:, h % 2], ps[:, 2 * (h % 2), :], ACT.Silu).then_inc(*S["act_a"].inc)
                        act.wait_ge(*S["m1"].at(i, FT * (u + 1) - 1))
                        act.wait_ge(*S["added"].at(i, u - 2))
                        act.activation(gate[:, u], ps[:, 4 + u, :], ACT.Silu).then_inc(*S["silu"].inc)

            @block.vector
            def _(dve):
                dve.tensor_copy(w[:], raw[:]).then_inc(S["g5"].sem, 1)
                dve.wait_ge(S["g5"].sem, S["g5"].base + 1)
                dve.tensor_scalar(w[:], w[:], float(np.float32(1.0 / 127.0)), None, ALU.mult).then_inc(S["g5"].sem, 1)
                with dve.Fori(0, R) as i:
                    for u in range(2):
                        for h in range(FT * u, FT * (u + 1)):
                            dve.wait_ge(*S["act_a"].at(i, h))
                            dve.wait_ge(*S["m1"].at(i, h - 2))
                            dve.tensor_tensor(hd[:, h % 2], sg[:, h % 2], ps[:, 2 * (h % 2) + 1, :], ALU.mult)\
                                .then_inc(*S["gated"].inc)
                    for u in range(2):
                        add_gated(dve, m, gate, i, u)
        S["g5"].base += 2


def scan_mixer(nc, ps, m, a):
    S, R = STEPS, ROUNDS
    IT = INNER // P
    with ExitStack() as mem:
        buf = on_chip(nc, mem)

        win, wdel, wout = buf("win2", P, 2 * INNER), buf("wdel", P, IT, INNER), buf("wout2", P, IT, P)
        bin_, cw, cb = buf("bin2", P, 2 * IT), buf("cw", P, IT, TAPS2), buf("cb", P, IT)
        bdel, bout = buf("bdel", P, IT), buf("bout2", P, 1)
        vp = buf("v_pad", P, 2, 2, T + TAPS2 - 1)
        cv, sg, dl = buf("conv", P, 2, C), buf("sig", P, 2, C), buf("delta", P, IT, C)
        val, bb, sc = buf("val", P, IT, C), buf("b_scan", P, 2, C), buf("scans", P, 2, 2, C)
        gt, fu = buf("gate2", P, 2, C), buf("fused", P, IT, C)
        load(nc, [(win[:], a["L2_attn_W_in"]), (wdel[:], a["L2_attn_W_delta"].rearrange("(c p) e -> p c e", p=P)),
                  (wout[:], a["L2_attn_W_out"].rearrange("(c p) d -> p c d", p=P)),
                  (bin_[:], a["L2_attn_b_in"]), (cw[:], a["L2_attn_conv_w"].rearrange("(c p) k -> p c k", p=P)),
                  (cb[:], a["L2_attn_conv_b"]), (bdel[:], a["L2_attn_b_delta"]),
                  (bout[:], column(a["L2_attn_b_out"]))])
        with Stage(2 * R, m1=2, m2=2, m3=2, m4=1, a1=2, a2=2, a3=2, a4=2, v1=2, v2=2, v3=2, v4=2, v7=2,
                   v8=2, v9=2, g1=2, g2=2, added=1), nc.Block() as block:
            @block.tensor
            def _(pe):
                with pe.Fori(0, 2 * R) as i:
                    x = m["s"][:, bass.ds(i * C, C)]
                    for q in range(IT):
                        pe.wait_ge(*S["a1"].at(i, q - 2))
                        pe.matmul(ps[:, q, :], win[:, q * P:(q + 1) * P], x, start=True, stop=True)\
                            .then_inc(*S["m1"].inc)
                    for q in range(IT):
                        pe.wait_ge(*S["a4"].at(i, q - 2))
                        pe.matmul(ps[:, 2 + q, :], win[:, INNER + q * P:INNER + (q + 1) * P], x, start=True,
                                  stop=True).then_inc(*S["m2"].inc)
                    pe.wait_ge(*S["v4"].at(i, 1))
                    for q in range(IT):
                        pe.wait_ge(*S["a3"].at(i, q - 2))
                        for c in range(IT):
                            mm = pe.matmul(ps[:, 4 + q, :], wdel[:, c, q * P:(q + 1) * P], val[:, c],
                                           start=(c == 0), stop=(c == IT - 1))
                        mm.then_inc(*S["m3"].inc)
                    pe.wait_ge(*S["v9"].at(i, 1))
                    pe.wait_ge(*S["added"].at(i, -1))
                    for c in range(IT):
                        mm = pe.matmul(ps[:, 6, :], wout[:, c], fu[:, c], start=(c == 0), stop=(c == IT - 1))
                    mm.then_inc(*S["m4"].inc)

            @block.scalar
            def _(act):
                act.wait_ge(S["g5"].sem, S["g5"].base + 1)
                with act.Fori(0, 2 * R) as i:
                    for q in range(IT):
                        act.wait_ge(*S["m1"].at(i, q))
                        act.wait_ge(*S["v3"].at(i, q - 2))
                        act.activation(vp[:, q, :, TAPS2 - 1:], bank(ps, q, 2, T), ACT.Identity,
                                       bias=bin_[:, q:q + 1]).then_inc(*S["a1"].inc)
                    for q in range(IT):
                        act.wait_ge(*S["v3"].at(i, q))
                        act.wait_ge(*S["v4"].at(i, q - 2))
                        act.activation(sg[:, q], cv[:, q], ACT.Sigmoid).then_inc(*S["a2"].inc)
                    for q in range(IT):
                        act.wait_ge(*S["m2"].at(i, q))
                        act.wait_ge(*S["v9"].at(i, q - 2))
                        act.activation(gt[:, q], ps[:, 2 + q, :], ACT.Sigmoid, bias=bin_[:, IT + q:IT + q + 1])\
                            .then_inc(*S["a4"].inc)
                    for q in range(IT):
                        act.wait_ge(*S["m3"].at(i, q))
                        act.wait_ge(*S["v7"].at(i, q - 2))
                        act.activation(dl[:, q], ps[:, 4 + q, :], ACT.Sigmoid, bias=bdel[:, q:q + 1])\
                            .then_inc(*S["a3"].inc)

            @block.gpsimd
            def _(pool):
                with pool.Fori(0, 2 * R) as i:
                    for q in range(IT):
                        pool.wait_ge(*S["a3"].at(i, q))
                        pool.wait_ge(*S["v7"].at(i, q - 2))
                        pool.tensor_tensor(bb[:, q], dl[:, q], val[:, q], ALU.mult).then_inc(*S["g1"].inc)
                        pool.wait_ge(*S["g1"].at(i, q))
                        pool.tensor_tensor(bb[:, q], val[:, q], bb[:, q], ALU.subtract).then_inc(*S["g2"].inc)

            @block.vector
            def _(dve):
                dve.memset(vp[:], 0.0).then_inc(S["g5"].sem, 1)
                dve.wait_ge(S["g5"].sem, S["g5"].base + 1)
                with dve.Fori(0, 2 * R) as i:
                    for q in range(IT):
                        def tap(k):
                            return vp[:, q, :, k:k + T]

                        c3 = cv[:, q].rearrange("p (b t) -> p b t", b=2)
                        dve.wait_ge(*S["a1"].at(i, q))
                        dve.wait_ge(*S["a2"].at(i, q - 2))
                        dve.wait_ge(*S["v4"].at(i, q - 2))
                        dve.tensor_scalar(c3, tap(2), cw[:, q, 2:3], cb[:, q:q + 1], ALU.mult, ALU.add)\
                            .then_inc(*S["v1"].inc)
                        dve.wait_ge(*S["v1"].at(i, q))
                        dve.scalar_tensor_tensor(c3, tap(1), cw[:, q, 1:2], c3, ALU.mult, ALU.add)\
                            .then_inc(*S["v2"].inc)
                        dve.wait_ge(*S["v2"].at(i, q))
                        dve.scalar_tensor_tensor(c3, tap(0), cw[:, q, 0:1], c3, ALU.mult, ALU.add)\
                            .then_inc(*S["v3"].inc)
                    for q in range(IT):
                        dve.wait_ge(*S["a2"].at(i, q))
                        dve.wait_ge(*S["g2"].at(i, q - 2))
                        dve.wait_ge(*S["m3"].at(i, -1))
                        dve.tensor_tensor(val[:, q], cv[:, q], sg[:, q], ALU.mult).then_inc(*S["v4"].inc)
                    for q in range(IT):
                        dve.wait_ge(*S["g2"].at(i, q))
                        for b in range(2):
                            span = slice(b * T, (b + 1) * T)
                            last_at = b * T - 1 if b else None
                            back = slice((b + 1) * T - 1, last_at, -1)
                            dve.tensor_tensor_scan(sc[:, q, 0, span], dl[:, q, span], bb[:, q, span], 0.0, ALU.mult,
                                                   ALU.add)
                            last = dve.tensor_tensor_scan(sc[:, q, 1, back], dl[:, q, back], bb[:, q, back], 0.0,
                                                          ALU.mult, ALU.add)
                        last.then_inc(*S["v7"].inc)
                        dve.wait_ge(*S["v7"].at(i, q))
                        dve.tensor_tensor(sc[:, q, 0], sc[:, q, 0], sc[:, q, 1], ALU.add).then_inc(*S["v8"].inc)
                        dve.wait_ge(*S["v8"].at(i, q))
                        dve.wait_ge(*S["a4"].at(i, q))
                        dve.wait_ge(*S["m4"].at(i, -1))
                        dve.tensor_tensor(fu[:, q], sc[:, q, 0], gt[:, q], ALU.mult).then_inc(*S["v9"].inc)
                    dve.wait_ge(*S["m4"].at(i, 0))
                    dve.scalar_tensor_tensor(m["s"][:, bass.ds(i * C, C)], ps[:, 6, :], bout[:, 0:1],
                                             m["xn"][:, bass.ds(i * C, C)], ALU.add, ALU.add)\
                        .then_inc(*S["added"].inc)
        S["g5"].base += 1


def grouped_ffn(nc, ps, m, a):
    S = STEPS
    R = GROUPS // 2
    IT = INTER // P
    with ExitStack() as mem:
        buf = on_chip(nc, mem)

        w1, w2 = buf("w1g", P, 2, IT, P), buf("w2g", P, 2, IT, P)
        b1, b2 = buf("b1g", P, 2, IT), buf("b2g", P, 2)
        wc, bc = buf("wc", P, 2, P), buf("bc", P, 2)
        gate = buf("gate", P, 2, C)
        with Stage(R, fetched0=4, fetched1=4, m1=2, v1=2, m2=4, silu=4, weighed=4, added=4), nc.Block() as block:
            @block.sync
            def _(sp):
                with sp.Fori(0, R) as i:
                    for u in range(2):
                        g = i * 2 + u
                        sp.wait_ge(*S["v1"].at(i, u - 2))
                        for dst, src in ((w1[:, u], a["L2_ffn_W1"][bass.ds(g, 1)].rearrange(
                                              "g (c p) h -> p (g c) h", p=P)),
                                         (w2[:, u], a["L2_ffn_W2"][bass.ds(g, 1)].rearrange(
                                             "g (c p) h -> p (g c) h", p=P)),
                                         (b1[:, u], a["L2_ffn_b1"][:, bass.ds(g * IT, IT)]),
                                         (b2[:, u:u + 1], a["L2_ffn_b2"][bass.ds(g, 1)].rearrange("g p -> p g"))):
                            sp.wait_ge(S["first"].sem, PRIME)
                            sp.dma_start(dst, src).then_inc(*S[f"fetched{u}"].inc)

            @block.tensor
            def _(pe):
                with pe.Fori(0, R) as i:
                    for u in range(2):
                        pe.wait_ge(*S[f"fetched{u}"].at(i, 3))
                        pe.wait_ge(*S["v1"].at(i, u - 2))
                        for c in range(IT):
                            pe.matmul(ps[:, u, 0:P], w1[:, u, c], w2[:, u, c], start=(c == 0), stop=(c == IT - 1))
                        for c in range(IT):
                            mm = pe.matmul(ps[:, u, P:P + 1], w2[:, u, c], b1[:, u, c:c + 1], start=(c == 0),
                                           stop=(c == IT - 1))
                        mm.then_inc(*S["m1"].inc)
                    for u in range(2):
                        pe.wait_ge(*S["v1"].at(i, u))
                        for c in range(2):
                            k = 2 * u + c
                            pe.wait_ge(*S["silu"].at(i, k - 2))
                            pe.matmul(ps[:, 2 + k % 2, :], wc[:, u], m["xn"][:, bass.ds(i * (4 * C) + k * C, C)],
                                      start=True, stop=True).then_inc(*S["m2"].inc)

            @block.scalar
            def _(act):
                with act.Fori(0, R) as i:
                    for k in range(4):
                        act.wait_ge(*S["m2"].at(i, k))
                        act.wait_ge(*S["added"].at(i, k - 2))
                        act.activation(gate[:, k % 2], ps[:, 2 + k % 2, :], ACT.Silu, bias=bc[:, k // 2:k // 2 + 1])\
                            .then_inc(*S["silu"].inc)

            @block.vector
            def _(dve):
                with dve.Fori(0, R) as i:
                    for u in range(2):
                        dve.wait_ge(*S["m1"].at(i, u))
                        dve.wait_ge(*S["silu"].at(i, 2 * u + 1 - 4))
                        dve.tensor_tensor(bc[:, u:u + 1], ps[:, u, P:P + 1], b2[:, u:u + 1], ALU.add)
                        dve.tensor_copy(wc[:, u], ps[:, u, 0:P]).then_inc(*S["v1"].inc)
                    for k in range(4):
                        at = m["s"][:, bass.ds(i * (4 * C) + k * C, C)]
                        x = m["x"][:, bass.ds(i * (4 * C) + k * C, C)]
                        dve.wait_ge(*S["silu"].at(i, k))
                        dve.tensor_tensor(gate[:, k % 2], gate[:, k % 2], at, ALU.mult).then_inc(*S["weighed"].inc)
                        dve.wait_ge(*S["weighed"].at(i, k))
                        dve.tensor_tensor(x, x, gate[:, k % 2], ALU.add).then_inc(*S["added"].inc)


def conv_mixer(nc, ps, m, a):
    S = STEPS
    SEQS, K = 8, T // BLK
    R = B // SEQS
    SETS, CS = 4, 8
    with ExitStack() as mem:
        buf = on_chip(nc, mem)

        toep = buf("toeplitz", P, 2, BLK, 2, P)
        zt = buf("z_blocks", P, 2, BLK, SEQS, K + 1)
        zb, cc, sg = buf("z_chan", P, 2, C), buf("conv_sum", P, 2, 2, C), buf("sig3", P, 2, C)
        win, wout = buf("win3", P, 2, P), buf("wout3", P, 2, P)
        bi, bt, bo = buf("bin3", P, 2), buf("bconv3", P, 2, BLK), buf("bout3", P, 1)
        with nc.Block() as block:
            @block.vector
            def _(dve):
                dve.memset(toep[:, 0], 0.0)
                dve.memset(zt[:], 0.0).then_inc(S["g5"].sem, 1)

            @block.gpsimd
            def _(pool):
                pool.memset(toep[:, 1], 0.0).then_inc(S["g5"].sem, 1)
        S["g5"].base += 2
        pairs = [(win[:], a["L3_attn_w_in"].rearrange("p (q e) -> p q e", q=2)),
                 (wout[:], a["L3_attn_w_out"].rearrange("(q p) h -> p q h", p=P)),
                 (bi[:], a["L3_attn_b_in"]), (bo[:], column(a["L3_attn_b_out"]))]
        W = 3 * BLK
        for q, (w, b) in enumerate((("L3_attn_w_a", "L3_attn_b_a"), ("L3_attn_w_b", "L3_attn_b_b"))):
            for j in range(4):
                rows = slice(BLK * j, BLK * j + BLK)
                for before in range(2):
                    pairs.append((toep[rows, q, :, before, rows],
                                  bass.AP(a[w].tensor, BLK * j * W + 1 + BLK * before,
                                          [[1, BLK], [W, BLK], [1, BLK]])))
                pairs.append((bt[rows, q], bass.AP(a[b].tensor, BLK * j, [[0, BLK], [1, BLK]])))
        load(nc, pairs)

        with Stage(R, m1=8, a1=8, v1=8, m2=8, v2=8, a2=4, v3=4, v4=8, m3=4, a3=4), nc.Block() as block:
            @block.tensor
            def _(pe):
                with pe.Fori(0, R) as i:
                    for z in range(8):
                        pe.wait_ge(*S["a1"].at(i, z - 2))
                        pe.matmul(ps[:, z % 2, :], win[:, z % 2], m["xn"][:, bass.ds(i * (SEQS * T) + z // 2 * C, C)],
                                  start=True, stop=True).then_inc(*S["m1"].inc)
                    pe.wait_ge(*S["v1"].at(i, 7))
                    for n in range(2 * SETS):
                        q = n % 2
                        pe.wait_ge(*S["v2"].at(i, n - 4))
                        for c in range(CS):
                            ch = n // 2 * CS + c
                            o = ps[:, 2 + n % 4, c * SEQS * K:(c + 1) * SEQS * K].rearrange("p (b k) -> p b k", b=SEQS)
                            pe.matmul(o, toep[:, q, ch, 0], zt[:, q, ch, :, 1:K + 1], start=True, stop=False)
                            mm = pe.matmul(o, toep[:, q, ch, 1], zt[:, q, ch, :, 0:K], start=False, stop=True)
                        mm.then_inc(*S["m2"].inc)
                    for k in range(4):
                        pe.wait_ge(*S["v4"].at(i, 2 * k + 1))
                        pe.wait_ge(*S["a3"].at(i, k - 2))
                        for q in range(2):
                            mm = pe.matmul(ps[:, 6 + k % 2, :], wout[:, q], zb[:, q], start=(q == 0), stop=(q == 1))
                        mm.then_inc(*S["m3"].inc)

            @block.scalar
            def _(act):
                with act.Fori(0, R) as i:
                    for z in range(8):
                        act.wait_ge(*S["m1"].at(i, z))
                        act.wait_ge(*(S["v1"].at(i, z - 2) if z >= 2 else S["m3"].at(i, -1)))
                        act.activation(zb[:, z % 2], ps[:, z % 2, :], ACT.Identity, bias=bi[:, z % 2:z % 2 + 1])\
                            .then_inc(*S["a1"].inc)
                    for g in range(SETS):
                        act.wait_ge(*S["v2"].at(i, 2 * g + 1))
                        act.wait_ge(*S["v3"].at(i, g - 1))
                        act.activation(sg[:], cc[:, g % 2], ACT.Sigmoid).then_inc(*S["a2"].inc)
                    for k in range(4):
                        act.wait_ge(*S["m3"].at(i, k))
                        act.wait_ge(S["first"].sem, PRIME)
                        act.activation(m["s"][:, bass.ds(i * (SEQS * T) + k * C, C)], ps[:, 6 + k % 2, :],
                                       ACT.Identity, bias=bo[:, 0:1]).then_inc(*S["a3"].inc)

            @block.vector
            def _(dve):
                with dve.Fori(0, R) as i:
                    for z in range(8):
                        dve.wait_ge(*S["a1"].at(i, z))
                        seqs = zt[:, z % 2, :, z // 2 * 2:z // 2 * 2 + 2, 1:K + 1]
                        dve.transpose(seqs.rearrange("p c b k -> p b k c"),
                                      zb[:, z % 2].rearrange("p (b k t) -> p b k t", b=2, k=K)[:, :, :, ::-1])\
                            .then_inc(*S["v1"].inc)
                    for g in range(SETS):
                        for q in range(2):
                            n = 2 * g + q
                            dve.wait_ge(*S["m2"].at(i, n))
                            dve.wait_ge(*S["v3"].at(i, g - 2))
                            dve.tensor_tensor(cc[:, g % 2, q].rearrange("p (c n) -> p c n", c=CS),
                                              bank(ps, 2 + n % 4, CS, SEQS * K),
                                              bt[:, q, g * CS:(g + 1) * CS].unsqueeze(2)
                                              .to_broadcast([P, CS, SEQS * K]), ALU.add).then_inc(*S["v2"].inc)
                        dve.wait_ge(*S["a2"].at(i, g))
                        for q in range(2):
                            last = dve.tensor_tensor(zt[:, q, g * CS:(g + 1) * CS, :, 1:K + 1],
                                                     cc[:, g % 2, q].rearrange("p (c b k) -> p c b k", c=CS, b=SEQS),
                                                     sg[:, 1 - q].rearrange("p (c b k) -> p c b k", c=CS, b=SEQS),
                                                     ALU.mult)
                        last.then_inc(*S["v3"].inc)
                    for k in range(4):
                        dve.wait_ge(*S["v3"].at(i, SETS - 1))
                        dve.wait_ge(*S["m3"].at(i, k - 1))
                        for q in range(2):
                            seqs = zt[:, q, :, 2 * k:2 * k + 2, 1:K + 1]
                            dve.transpose(zb[:, q].rearrange("p (b k t) -> p b k t", b=2, k=K),
                                          seqs.rearrange("p c b k -> p b k c")).then_inc(*S["v4"].inc)


def local_attention(nc, ps, m, a, layer):
    S = STEPS
    QW = HEADS * DH
    with ExitStack() as mem:
        buf = on_chip(nc, mem)

        wqkv, wo = buf("wqkv3", P, QKV), buf("wo3", P, 4, P)
        rope, tab, qks = buf("rope", P, 2, 4, DH), buf("rope_scaled", P, 2, 4, DH), buf("qk_scale", P, 2, DH)
        hf, qk, sq = buf("hf", P, 2, 1, T), buf("qk_raw", P, 2, 2 * QW), buf("qk_sq", P, 2 * QW)
        st, tw, ot = buf("qk_rot", P, 2, 2 * QW), buf("qk_cross", P, 2, 2 * QW), buf("ot", P, 4, T)
        ss, rn = buf("sumsq", P, 2, 16), buf("rnorm", P, 2, 16)
        core = Core(nc, ps, m, mem, m["band"], 8.0, DH, lambda tile: tile, lambda head: head * DH)
        load(nc, [(wqkv[:], a["L3_ffn_wqkv"][layer]), (wo[:], a["L3_ffn_wo"][layer].rearrange("(c p) o -> p c o", p=P)),
                  (rope[:], a["rope"]), (qks[:, 0], a["L3_ffn_q_scale"][layer].partition_broadcast(P)),
                  (qks[:, 1], a["L3_ffn_k_scale"][layer].partition_broadcast(P))])

        when = {t: [] for t in range(STEPS_T)}
        for first, r in ((0, 2), (10, 0)):
            when[first] += [("q", r), ("k", r)]
            when[first + 1] += [("v", r), ("q", r + 1)]
            when[first + 2] += [("k", r + 1), ("v", r + 1)]
            when[first + 5] += [("qt", r), ("kt", r)]
            when[first + 7] += [("qt", r + 1), ("kt", r + 1)]
        for w in range(4):
            when[4 * w + 8].append(("ot", w))
        for u in range(2):
            when[8 * u + 13].append(("out", u))
        pos = {2: 0, 3: 1, 0: 2, 1: 3}
        NORMS = {first + 2 * (r % 2) + 1: r for first, rr in ((0, 2), (10, 0)) for r in (rr, rr + 1)}
        ROTATE = {t + 1: r for t, r in NORMS.items()}
        order = [x for t in range(STEPS_T) for x in when[t]]
        early = lambda x: x[0] in ("q", "k", "v", "qt", "kt") and x[1] < 2
        at = {x: n for n, x in enumerate(order)}
        by_act = [x for x in order if x[0] in ("q", "k", "v")]
        by_dve = [x for x in order if x not in by_act]

        def freed(i, n):
            x = order[n]
            name, mine = ("freed_act", by_act) if x in by_act else ("freed_dve", by_dve)
            return S[name].at(i, mine.index(x) - (len(mine) if n < 0 else 0))

        core.o_read = lambda i, w: (i, at["ot", w - 2] if w >= 2 else at["ot", w + 2] - len(order))

        def pe_event(pe, i, x):
            kind, r = x
            e = at[x]
            o = ps[:, 6 + e % 2]
            pe.wait_ge(*freed(i, e - 2))
            if isinstance(i, int):
                for n in [n for n in range(e % 2, e, 2) if early(order[n])][-1:]:
                    pe.wait_ge(*freed(i, n))
            if kind in ("q", "k", "v"):
                if kind == "q" and r % 2 == 0:
                    pe.wait_ge(*S["copied"].at(i, 1 - r // 2))
                w = "qkv".index(kind) * QW
                mm = pe.matmul(o, hf[:, r // 2, 0, r % 2 * P:(r % 2 + 1) * P], wqkv[:, w:w + QW], start=True, stop=True)
            elif kind in ("qt", "kt"):
                if kind == "qt":
                    pe.wait_ge(*S["unit"].at(i, pos[r]))
                for c in range(4):
                    first = (kind == "kt") * QW + c * P
                    mm = pe.transpose(o[:, c * P:(c + 1) * P], st[:, r % 2, first:first + P], m["ident"][:])
            elif kind == "ot":
                pe.wait_ge(*S["attended"].at(i, r))
                for c in range(4):
                    mm = pe.transpose(o[:, c * P:(c + 1) * P], core.o[:, r % 2, c * P:(c + 1) * P], m["ident"][:])
            else:
                pe.wait_ge(*freed(i, at["ot", 2 * r + 1]))
                for c in range(4):
                    mm = pe.matmul(o[:, 0:T], wo[:, c], ot[:, c], start=(c == 0), stop=(c == 3))
            mm.then_inc(*S["projected"].inc)

        def dve_event(dve, i, x):
            kind, r = x
            src = ps[:, 6 + at[x] % 2]
            dve.wait_ge(*S["projected"].at(i, at[x]))
            if kind in ("qt", "kt"):
                if kind == "qt" and r % 2 == 0:
                    dve.wait_ge(*S["scores"].at(i, -1 if r else 7))
                dst = core.qt if kind == "qt" else core.kt
                last = dve.tensor_copy(dst[:, r // 2, :, r % 2 * P:(r % 2 + 1) * P], bank(ps, 6 + at[x] % 2, 4, P))
            elif kind == "ot":
                last = dve.tensor_copy(ot[:, :, r % 2 * P:(r % 2 + 1) * P], bank(ps, 6 + at[x] % 2, 4, P))
            else:
                xn = m["xn"][:, cols(i, r, T)]
                last = dve.tensor_tensor(xn, xn, src[:, 0:T], ALU.add)
            last.then_inc(*S["freed_dve"].inc)

        made = ["copied", "projected", "freed_act", "freed_dve", "squared", "sumsq", "rnorm", "v1", "straight",
                "crossed", "rotated", "unit"]
        with Stage(PAIRS, made, copied=2, projected=len(order), freed_act=len(by_act), freed_dve=len(by_dve), squared=4,
                   sumsq=4, rnorm=4, v1=4, straight=4, crossed=4, rotated=4, unit=4, **CORE), nc.Block() as block:
            @block.gpsimd
            def _(pool):
                pool.memset(hf[:], 0.0).then_inc(S["g5"].sem, 1)
                for tb in range(2):
                    for w in range(2):
                        pool.tensor_tensor(tab[:, tb, 2 * w], rope[:, tb, 2 * w], qks[:, w], ALU.mult)
                        last = pool.tensor_tensor(
                            tab[:, tb, 2 * w + 1].rearrange("p (a d) -> p a d", a=2),
                            rope[:, tb, 2 * w + 1].rearrange("p (a d) -> p a d", a=2),
                            qks[:, w].rearrange("p (a d) -> p a d", a=2)[:, ::-1], ALU.mult)
                last.then_inc(S["g5"].sem, 1)
                pool.wait_ge(S["g5"].sem, S["g5"].base + 2)

                def shift(i, u, first):
                    pool.wait_ge(*S["unit"].at(i, 2 * (1 - u) - 1))
                    shift_in(pool, hf[:, u], m["xn"], i, u, T, S["projected"].at(i, at["v", 2 * u + 1] - len(order)),
                             first=first)
                    pool.wait_ge(*S["copied"].at(i, 1 - u))

                def tile(i, r):
                    p = pos[r]
                    pool.wait_ge(*S["freed_act"].at(i, by_act.index(("k", r))))
                    pool.wait_ge(*S["rotated"].at(i, p - 2))
                    for w in range(2):
                        raw = qk[:, r % 2, w * QW:(w + 1) * QW].rearrange("p (h a d) -> p h a d", a=2, d=DH // 2)
                        last = pool.tensor_tensor(
                            tw[:, r % 2, w * QW:(w + 1) * QW].rearrange("p (h a d) -> p h a d", a=2, d=DH // 2),
                            raw[:, :, ::-1, :],
                            tab[:, r % 2, 2 * w + 1].rearrange("p (a d) -> p a d", a=2).unsqueeze(1)
                            .to_broadcast([P, HEADS, 2, DH // 2]), ALU.mult)
                    last.then_inc(*S["crossed"].inc)
                    pool.wait_ge(*S["v1"].at(i, p))
                    pool.tensor_tensor(rn[:, r % 2], rn[:, r % 2], m["half"][:], ALU.pow).then_inc(*S["rnorm"].inc)
                    pool.wait_ge(*S["rnorm"].at(i, p))
                    pool.wait_ge(*S["rotated"].at(i, p))
                    heads = st[:, r % 2].rearrange("p (h d) -> p h d", d=DH)
                    pool.tensor_tensor(heads, heads, rn[:, r % 2].unsqueeze(2).to_broadcast([P, 16, DH]),
                                       ALU.mult).then_inc(*S["unit"].inc)

                for name in ("crossed", "rnorm", "unit"):
                    pass_over(pool, name, 0, 2)
                pass_over(pool, "copied", 0, 1)
                shift(-1, 0, 0)
                tile(-1, 0)
                tile(-1, 1)
                with pool.Fori(0, PAIRS) as i:
                    shift(i, 1, i * (2 * T) + T)
                    tile(i, 2)
                    tile(i, 3)
                    shift(i, 0, i * (2 * T) + 2 * T)
                    tile(i, 0)
                    tile(i, 1)

            @block.tensor
            def _(pe):
                first_ones(pe, "projected", order, early, lambda x: pe_event(pe, -1, x))
                with pe.Fori(0, PAIRS) as i:
                    for t in range(STEPS_T):
                        core.pe_step(pe, i, t, lambda i, u: [freed(i, at[x, 2 * u + 1] - (0 if u else len(order)))
                                                             for x in ("kt", "v")])
                        for x in when[t]:
                            pe_event(pe, i, x)

            def act_event(act, i, x):
                kind, r = x
                p = pos[r]
                act.wait_ge(*S["projected"].at(i, at[x]))
                if kind == "q":
                    act.wait_ge(*S["straight"].at(i, p - 2))
                    act.wait_ge(*S["crossed"].at(i, p - 2))
                    act.wait_ge(*S["squared"].at(i, p - 2))
                if kind == "v":
                    act.wait_ge(*S["mixed"].at(i, -1 if r > 1 else 7))
                    dst = core.v[:, r // 2, r % 2]
                else:
                    w = "qk".index(kind)
                    dst = qk[:, r % 2, w * QW:(w + 1) * QW]
                act.activation(dst, ps[:, 6 + at[x] % 2], ACT.Copy).then_inc(*S["freed_act"].inc)
                if kind == "k":
                    act.wait_ge(*S["sumsq"].at(i, p - 1))
                    act.wait_ge(*S["freed_act"].at(i, by_act.index(x)))
                    act.activation(sq[:], qk[:, r % 2], ACT.Square).then_inc(*S["squared"].inc)

            @block.scalar
            def _(act):
                pass_over(act, "squared", 0, 2)
                first_ones(act, "freed_act", by_act, early, lambda x: act_event(act, -1, x))
                with act.Fori(0, PAIRS) as i:
                    for t in range(STEPS_T):
                        core.act_step(act, i, t)
                        for x in when[t]:
                            if x in by_act:
                                act_event(act, i, x)

            def dve_norms(dve, i, r):
                p = pos[r]
                dve.wait_ge(*S["squared"].at(i, p))
                dve.wait_ge(*S["unit"].at(i, p - 2))
                dve.tensor_reduce(ss[:, r % 2], sq[:].rearrange("p (h d) -> p h d", d=DH), AX.X, ALU.add)\
                    .then_inc(*S["sumsq"].inc)
                dve.wait_ge(*S["sumsq"].at(i, p))
                dve.tensor_scalar(rn[:, r % 2], ss[:, r % 2], 1e-24, None, ALU.max).then_inc(*S["v1"].inc)
                dve.wait_ge(*S["projected"].at(i, at["kt", (r + 2) % 4] - (len(order) if r > 1 else 0)))
                for w in range(2):
                    last = dve.tensor_tensor(st[:, r % 2, w * QW:(w + 1) * QW].rearrange("p (h d) -> p h d", d=DH),
                                             qk[:, r % 2, w * QW:(w + 1) * QW].rearrange("p (h d) -> p h d", d=DH),
                                             tab[:, r % 2, 2 * w:2 * w + 1].to_broadcast([P, HEADS, DH]), ALU.mult)
                last.then_inc(*S["straight"].inc)

            def dve_rotate(dve, i, r):
                dve.wait_ge(*S["straight"].at(i, pos[r]))
                dve.wait_ge(*S["crossed"].at(i, pos[r]))
                dve.tensor_tensor(st[:, r % 2], st[:, r % 2], tw[:, r % 2], ALU.add).then_inc(*S["rotated"].inc)

            @block.vector
            def _(dve):
                dve.wait_ge(S["g5"].sem, S["g5"].base + 2)
                for name in ("sumsq", "v1", "straight", "rotated"):
                    pass_over(dve, name, 0, 2)
                for t in range(STEPS_T):
                    if NORMS.get(t, 2) < 2:
                        dve_norms(dve, -1, NORMS[t])
                    if ROTATE.get(t, 2) < 2:
                        dve_rotate(dve, -1, ROTATE[t])
                    mine = [x for x in when[t] if x in by_dve]
                    first_ones(dve, "freed_dve", mine, early, lambda x: dve_event(dve, -1, x),
                               by_dve.index(mine[0]) if mine else 0)
                with dve.Fori(0, PAIRS) as i:
                    for t in range(STEPS_T):
                        core.dve_step(dve, i, t)
                        if t in NORMS:
                            dve_norms(dve, i, NORMS[t])
                        if t in ROTATE:
                            dve_rotate(dve, i, ROTATE[t])
                        for x in when[t]:
                            if x in by_dve:
                                dve_event(dve, i, x)
        S["g5"].base += 2


def gelu_ffn(nc, ps, m, a, layer, h_in):
    S, R = STEPS, ROUNDS
    FT = 3
    with ExitStack() as mem:
        buf = on_chip(nc, mem)

        w1, w2, b1, b2 = buf("w1t", P, 2, FT, P), buf("w2t", P, FT, P), buf("b1t", P, 2, FT), buf("b2t", P, 1)
        gg, hd = buf("gelu_g", P, 2, C), buf("hid3", P, 2, C)
        load(nc, [(w1[:], a["L3_ffn_w1"][layer]), (w2[:], a["L3_ffn_w2"][layer].rearrange("(f p) d -> p f d", p=P)),
                  (b1[:], a["L3_ffn_b1"][layer]), (b2[:], column(a["L3_ffn_b2"][layer]))])
        with Stage(R, up=2 * FT, act_a=2 * FT, gated=2 * FT, m1=2 * FT, added=2), nc.Block() as block:
            @block.tensor
            def _(pe):
                with pe.Fori(0, R) as i:
                    for u in range(2):
                        for f in range(FT + 1):
                            h = FT * u + f
                            if f < FT:
                                pe.wait_ge(*S["gated"].at(i, h - 2))
                                for g in range(2):
                                    mm = pe.matmul(ps[:, 2 * (h % 2) + g, :], w1[:, g, f], h_in[:, cols(i, u, C)],
                                                   start=True, stop=True)
                                mm.then_inc(*S["up"].inc)
                            if f >= 1:
                                pe.wait_ge(*S["gated"].at(i, h - 1))
                                if f == 1:
                                    pe.wait_ge(*S["added"].at(i, u - 2))
                                mm = pe.matmul(ps[:, 4 + u, :], w2[:, f - 1], hd[:, (h - 1) % 2],
                                               start=(f == 1), stop=(f == FT))
                                mm.then_inc(*S["m1"].inc)

            @block.scalar
            def _(act):
                with act.Fori(0, R) as i:
                    for h in range(2 * FT):
                        act.wait_ge(*S["up"].at(i, h))
                        act.wait_ge(*S["gated"].at(i, h - 2))
                        act.activation(gg[:, h % 2], ps[:, 2 * (h % 2) + 1, :], ACT.Gelu,
                                       bias=b1[:, 1, h % FT:h % FT + 1]).then_inc(*S["act_a"].inc)

            @block.vector
            def _(dve):
                with dve.Fori(0, R) as i:
                    for u in range(2):
                        for h in range(FT * u, FT * (u + 1)):
                            dve.wait_ge(*S["act_a"].at(i, h))
                            dve.wait_ge(*S["m1"].at(i, h - 2))
                            dve.scalar_tensor_tensor(hd[:, h % 2], ps[:, 2 * (h % 2), :], b1[:, 0, h % FT:h % FT + 1],
                                                     gg[:, h % 2], ALU.add, ALU.mult).then_inc(*S["gated"].inc)
                        xn = m["xn"][:, cols(i, u, C)]
                        dve.wait_ge(*S["m1"].at(i, FT * (u + 1) - 1))
                        dve.scalar_tensor_tensor(xn, ps[:, 4 + u, :], b2[:, 0:1], xn, ALU.add, ALU.add)\
                            .then_inc(*S["added"].inc)


def rope_tables():
    half = np.arange(0, DH, 2, dtype=np.float32)
    t = np.arange(T, dtype=np.float32)
    freqs = t[:, None] * (1.0 / 10000.0 ** (half / DH))[None, :].astype(np.float32)
    base = (half + 0.4 * DH) / (1.4 * DH)
    scale = base[None, :] ** ((t - T // 2) / float(WINDOW // 2))[:, None]
    freqs, scale = np.concatenate([freqs, freqs], -1), np.concatenate([scale, scale], -1)
    sign = np.where(np.arange(DH) < DH // 2, -1.0, 1.0)[None, :]
    cos, sin = np.cos(freqs), np.sin(freqs) * sign
    tables = np.stack([cos * scale, sin * scale, cos / scale, sin / scale], 1).astype(np.float32)
    return tables.reshape(2, P, 4, DH).transpose(1, 0, 2, 3)


def lay_out(x):
    x = {k: np.asarray(v) for k, v in x.items()}
    d = dict(x)
    d["x"] = d.pop("L0_attn_x").reshape(N, P).T
    d["L0_attn_wq"] = x["L0_attn_wq"].reshape(P, HEADS, P).transpose(2, 1, 0)
    for n in ("L0_attn_wk_up", "L0_attn_wv_up", "L1_attn_w_qkv", "L1_attn_w_out", "L1_ffn_w_gate", "L1_ffn_w_up",
              "L1_ffn_w_down", "L3_attn_w_in", "L3_attn_w_out"):
        d[n] = x[n].T
    d["L0_ffn_b1"] = x["L0_ffn_b1"].reshape(EXPERTS, FF0 // P, P).transpose(2, 0, 1)
    for n, w in (("L2_attn_b_in", 4), ("L2_attn_conv_b", 2), ("L2_attn_b_delta", 2), ("L3_attn_b_in", 2)):
        d[n] = x[n].reshape(w, P).T
    d["L2_ffn_W2"] = x["L2_ffn_W2"].transpose(0, 2, 1)
    d["L2_ffn_b1"] = x["L2_ffn_b1"].reshape(GROUPS * INTER // P, P).T
    for n in ("L3_attn_w_a", "L3_attn_w_b"):
        d[n] = np.pad(x[n].reshape(P, TAPS3)[:, ::-1], ((0, 0), (BLK, BLK)))
    pad = 3 * P - HID3
    w1 = np.pad(x["L3_ffn_w1"].reshape(DEPTH, P, 2, HID3), ((0, 0), (0, 0), (0, 0), (0, pad)))
    d["L3_ffn_w1"] = w1.reshape(DEPTH, P, 2, 3, P)
    b1 = np.pad(x["L3_ffn_b1"].reshape(DEPTH, 2, HID3), ((0, 0), (0, 0), (0, pad)))
    d["L3_ffn_b1"] = b1.reshape(DEPTH, 2, 3, P).transpose(0, 3, 1, 2)
    d["L3_ffn_w2"] = np.pad(x["L3_ffn_w2"], ((0, 0), (0, pad), (0, 0)))
    d["rope"] = rope_tables()
    return {k: np.ascontiguousarray(v) for k, v in d.items()}


def kernel(**inputs):
    import concourse.bacc as bacc
    from concourse.bass_utils import run_bass_kernel_spmd

    nc = bacc.Bacc("TRN2", target_bir_lowering=False, num_devices=1)
    arrays = lay_out(inputs)
    a = {k: nc.dram_tensor(f"in_{k}", v.shape, mybir.dt.from_np(v.dtype), kind="ExternalInput").ap()
         for k, v in arrays.items()}
    out = nc.dram_tensor("out_x", (P, N), F32, kind="ExternalOutput").ap()
    build(nc, a, out)
    r = run_bass_kernel_spmd(nc, [{f"in_{k}": v for k, v in arrays.items()}], core_ids=[0])
    return np.ascontiguousarray(np.asarray(r.results[0]["out_x"]).T).reshape(B, T, P)
```

```python
from contextlib import ExitStack

import numpy as np

import concourse.bass as bass
from concourse import mybir

F32 = mybir.dt.float32
I32 = mybir.dt.int32
U32 = mybir.dt.uint32
ALU = mybir.AluOpType
ACT = mybir.ActivationFunctionType
AX = mybir.AxisListType

P = 128
B, T = 32, 256
N = B * T
C = 512
ROUNDS = N // (2 * C)
PAIRS = B // 2
EPS = 1e-5
NEG = -3.0e38
PRIME = 64

HEADS, N_KV, LAT = 8, 2, 32
EXPERTS, FF0 = 8, 512
FT0 = FF0 // P
TOK = N // P
TILES = -(-(TOK + EXPERTS - 1) // 8) * 8
HD1, HID1 = 8, 384
INNER, TAPS2, GROUPS, INTER = 256, 3, 8, 512
TAPS3, DEPTH, DH, WINDOW, HID3 = 32, 2, 64, 64, 341
QKV = 3 * HEADS * DH
BLK = 32


class Step:

    def __init__(self, sem, by):
        self.sem, self.by, self.base, self.per = sem, by, by * PRIME, 0
        self.inc = (sem, by)

    def at(self, i, n=0):
        first = self.base + (n + 1) * self.by
        return (self.sem, i * (self.per * self.by) + first)


class Stage:

    def __init__(self, rounds, early=(), **per):
        self.rounds, self.early, self.per = rounds, early, per

    def __enter__(self):
        for name, per in self.per.items():
            STEPS[name].per = per
            STEPS[name].base += (name in self.early) * per * STEPS[name].by

    def __exit__(self, *_):
        for name, per in self.per.items():
            STEPS[name].base += self.rounds * per * STEPS[name].by
            STEPS[name].per = 0


STEPS = {}
NUMBER = []
COMPUTE = [
    "mean", "centered", "squared", "variance", "deviation", "logged", "scaled", "normed", "copied",
    "projected", "freed_act", "freed_dve", "scores", "masked", "rowmax", "exps", "turned", "turned_sb",
    "mixed", "rowsum", "attended", "table", "sumsq", "rnorm", "straight", "crossed", "rotated", "unit",
    "up", "act_a", "act_b", "gated", "down", "silu", "weighed", "added", "prep", "prep_sb",
    "m1", "m2", "m3", "m4", "v1", "v2", "v3", "v4", "v5", "v6", "v7", "v8", "v9", "a1", "a2", "a3",
    "a4", "g1", "g2", "g3", "g4", "g5", "t_add", "first",
]
MOVES = ["loaded", "stored", "fetched0", "fetched1", "stored0", "stored1"]
POOL_MOVES = ["moved0", "moved1"]


def cols(i, u, width, parts=2):
    return bass.ds(i * (parts * width) + u * width, width)


def build(nc, a, out):
    ctx = ExitStack()
    with ctx:
        def keep(name, shape, dt=F32):
            return ctx.enter_context(nc.sbuf_tensor(name, shape, dt))

        STEPS.clear()
        NUMBER.clear()
        for n in COMPUTE:
            STEPS[n] = Step(ctx.enter_context(nc.semaphore(n)), 1)
        for n in MOVES:
            STEPS[n] = Step(ctx.enter_context(nc.semaphore(n)), 16)
        for n in POOL_MOVES:
            STEPS[n] = Step(ctx.enter_context(nc.semaphore(n)), 16)
            STEPS[n].base = 0
        m = {
            "x": keep("x_res", [P, N]),
            "xn": keep("xn", [P, N + T]),
            "s": keep("s_branch", [P, N]),
            "ident": keep("ident", [P, P]),
            "mean": keep("mean_matrix", [P, P]),
            "causal": keep("causal", [P, 2, T]),
            "band": keep("band", [P, 2, T]),
            "eps": keep("eps", [P, 1]),
            "half": keep("minus_half", [P, 16]),
        }
        ps = ctx.enter_context(nc.psum_tensor("banks", [P, 8, C], F32))

        start(nc, m, a)
        layer_norm(nc, ps, m, m["x"], m["xn"])
        latent_attention(nc, ps, m, a)
        experts(nc, ps, m, a)
        layer_norm(nc, ps, m, m["x"], m["xn"])
        linear_attention(nc, ps, m, a)
        integer_ffn(nc, ps, m, a)
        layer_norm(nc, ps, m, m["x"], m["xn"])
        layer_norm(nc, ps, m, m["xn"], m["s"], (a["L2_attn_ln_gamma"], a["L2_attn_ln_beta"]))
        scan_mixer(nc, ps, m, a)
        grouped_ffn(nc, ps, m, a)
        layer_norm(nc, ps, m, m["x"], m["xn"])
        conv_mixer(nc, ps, m, a)
        for layer in range(DEPTH):
            local_attention(nc, ps, m, a, layer)
            with nc.sbuf_tensor(f"h_norm{layer}", [P, N], F32) as h:
                layer_norm(nc, ps, m, m["xn"], h, (a["L3_ffn_ln_g"][layer], a["L3_ffn_ln_b"][layer]), shifted=True)
                gelu_ffn(nc, ps, m, a, layer, h)
        finish(nc, m, out)


def on_chip(nc, mem):
    NUMBER.append(len(NUMBER))
    return lambda name, *shape, dt=F32: mem.enter_context(nc.sbuf_tensor(f"{name}_{NUMBER[-1]}", list(shape), dt))


def bank(ps, n, *shape):
    size = int(np.prod(shape))
    v = ps[:, n, 0:size]
    if len(shape) == 1:
        return v
    names = "abc"[:len(shape)]
    return v.rearrange(f"p ({' '.join(names)}) -> p {' '.join(names)}", **dict(zip(names[1:], shape[1:])))


def start(nc, m, a):
    S = STEPS
    with nc.Block() as block:
        @block.sync
        def _(sp):
            for step in [step for step in S.values() if step.base]:
                sp.sem_inc(step.sem, step.base)

        @block.gpsimd
        def _(pool):
            pool.memset(m["ident"][:], 0.0).then_inc(S["g1"].sem, 1)
            pool.memset(m["mean"][:], 1.0 / P)
            pool.memset(m["xn"][:, N:], 0.0)
            pool.memset(m["eps"][:], EPS)
            pool.memset(m["half"][:], -0.5)
            pool.memset(m["causal"][:], 0.0)
            pool.memset(m["band"][:], 0.0).then_inc(S["g1"].sem, 1)
            pool.wait_ge(S["g1"].sem, PRIME + 2)
            pool.affine_select(out=m["ident"][:], in_=m["ident"][:], compare_op=ALU.not_equal, fill=1.0,
                               base=0, pattern=[[-1, P]], channel_multiplier=1)
            for qb in range(2):
                pool.affine_select(out=m["causal"][:, qb, :], in_=m["causal"][:, qb, :], compare_op=ALU.is_ge,
                                   fill=NEG, base=qb * P, pattern=[[-1, T]], channel_multiplier=1)
                last = pool.affine_select(out=m["band"][:, qb, :], in_=m["band"][:, qb, :], compare_op=ALU.is_ge,
                                          fill=NEG, base=qb * P, pattern=[[-1, T]], channel_multiplier=1)
            last.then_inc(S["g1"].sem, 1)
            pool.wait_ge(S["g1"].sem, PRIME + 3)
            for qb in range(2):
                pool.affine_select(out=m["band"][:, qb, :], in_=m["band"][:, qb, :], compare_op=ALU.is_ge,
                                   fill=NEG, base=WINDOW - qb * P, pattern=[[1, T]], channel_multiplier=-1)
    S["g1"].base += 3
    load(nc, [(m["x"][:, k * (N // 8):(k + 1) * (N // 8)], a["x"][:, k * (N // 8):(k + 1) * (N // 8)]) for k in range(8)])


def load(nc, pairs):
    S = STEPS
    with nc.Block() as block:
        @block.sync
        def _(sp):
            for dst, src in pairs:
                sp.dma_start(dst, src).then_inc(S["loaded"].sem, 16)
            sp.wait_ge(S["loaded"].sem, S["loaded"].base + 16 * len(pairs))
    S["loaded"].base += 16 * len(pairs)


def column(vec):
    return vec.rearrange("(p o) -> p o", o=1)


def finish(nc, m, out):
    S = STEPS
    R = ROUNDS
    with ExitStack() as mem:
        gate = on_chip(nc, mem)("gate", P, 2, C)
        with Stage(R, silu=2, weighed=2, added=2), nc.Block() as block:
            @block.scalar
            def _(act):
                act.preload_act_table_set("silu_and_others")
                with act.Fori(0, R) as i:
                    for u in range(2):
                        act.wait_ge(*S["added"].at(i, u - 2))
                        act.wait_ge(S["first"].sem, PRIME)
                        act.activation(gate[:, u], m["xn"][:, cols(i, u, C)], ACT.Silu).then_inc(*S["silu"].inc)

            @block.vector
            def _(dve):
                with dve.Fori(0, R) as i:
                    for u in range(2):
                        add_gated(dve, m, gate, i, u)

            @block.sync
            def _(sp):
                with sp.Fori(0, R) as i:
                    for u in range(2):
                        sp.wait_ge(*S["added"].at(i, u))
                        sp.wait_ge(S["first"].sem, PRIME)
                        sp.dma_start(out[:, cols(i, u, C)], m["x"][:, cols(i, u, C)]).then_inc(S["stored"].sem, 16)
                sp.wait_ge(S["stored"].sem, 16 * (PRIME + 2 * R))


def add_gated(dve, m, gate, i, u):
    S = STEPS
    dve.wait_ge(*S["silu"].at(i, u))
    dve.tensor_tensor(gate[:, u], gate[:, u], m["s"][:, cols(i, u, C)], ALU.mult).then_inc(*S["weighed"].inc)
    dve.wait_ge(*S["weighed"].at(i, u))
    dve.tensor_tensor(m["x"][:, cols(i, u, C)], m["x"][:, cols(i, u, C)], gate[:, u], ALU.add)\
        .then_inc(*S["added"].inc)


def layer_norm(nc, ps, m, src, dst, affine=None, shifted=False):
    S, W = STEPS, 4
    R = N // (W * C)
    with ExitStack() as mem:
        buf = on_chip(nc, mem)

        xc, sq, sd = buf("ln_xc", P, W, C), buf("ln_sq", P, W, C), buf("ln_sd", P, W, C)
        hs = buf("ln_hs", P, W, 2, T) if shifted else None
        gb = buf("ln_gb", P, 2)
        if affine:
            load(nc, [(gb[:, 0:1], column(affine[0])), (gb[:, 1:2], column(affine[1]))])

        def source(i, u):
            if shifted:
                return hs[:, u].rearrange("p b t -> p (b t)")
            return src[:, cols(i, u, C, W)]

        with Stage(R, mean=W, centered=W, squared=W, variance=W, logged=W, deviation=W, scaled=W, normed=W,
                   copied=W), nc.Block() as block:
            @block.gpsimd
            def _(pool):
                if shifted:
                    pool.memset(hs[:], 0.0).then_inc(S["first"].sem, 1)
                    pool.wait_ge(S["first"].sem, S["first"].base + 1)
                    with pool.Fori(0, R) as i:
                        for u in range(W):
                            shift_in(pool, hs[:, u], src, i, u, C, S["centered"].at(i, u - W), W)

            @block.tensor
            def _(pe):
                with pe.Fori(0, R) as i:
                    for u in range(W):
                        if shifted:
                            pe.wait_ge(*S["copied"].at(i, u))
                        pe.wait_ge(*S["centered"].at(i, u - W))
                        pe.matmul(ps[:, u, :], m["mean"][:], source(i, u), start=True, stop=True)\
                            .then_inc(*S["mean"].inc)
                    for u in range(W):
                        pe.wait_ge(*S["squared"].at(i, u))
                        pe.wait_ge(*S["logged"].at(i, u - W))
                        pe.matmul(ps[:, W + u, :], m["mean"][:], sq[:, u], start=True, stop=True)\
                            .then_inc(*S["variance"].inc)

            @block.scalar
            def _(act):
                act.preload_act_table_set("natural_log_exp_and_others")
                with act.Fori(0, R) as i:
                    for u in range(W):
                        act.wait_ge(*S["centered"].at(i, u))
                        act.wait_ge(*S["variance"].at(i, u - W))
                        act.activation(sq[:, u], xc[:, u], ACT.Square).then_inc(*S["squared"].inc)
                    for u in range(W):
                        act.wait_ge(*S["variance"].at(i, u))
                        act.wait_ge(*S["normed"].at(i, u - W))
                        act.activation(sd[:, u], ps[:, W + u, :], ACT.Ln, bias=m["eps"][:, 0:1])\
                            .then_inc(*S["logged"].inc)
                        act.wait_ge(*S["logged"].at(i, u))
                        act.activation(sd[:, u], sd[:, u], ACT.Exp, scale=-0.5).then_inc(*S["deviation"].inc)

            @block.vector
            def _(dve):
                with dve.Fori(0, R) as i:
                    for u in range(W):
                        dve.wait_ge(*S["mean"].at(i, u))
                        dve.wait_ge(*S["normed"].at(i, u - W))
                        if shifted:
                            dve.wait_ge(*S["copied"].at(i, u))
                        dve.tensor_tensor(xc[:, u], source(i, u), ps[:, u, :], ALU.subtract)\
                            .then_inc(*S["centered"].inc)
                    for u in range(W):
                        dve.wait_ge(*S["deviation"].at(i, u))
                        if affine:
                            dve.tensor_tensor(xc[:, u], xc[:, u], sd[:, u], ALU.mult).then_inc(*S["scaled"].inc)
                            dve.wait_ge(*S["scaled"].at(i, u))
                            dve.tensor_scalar(dst[:, cols(i, u, C, W)], xc[:, u], gb[:, 0:1], gb[:, 1:2], ALU.mult,
                                              ALU.add).then_inc(*S["normed"].inc)
                        else:
                            dve.tensor_tensor(dst[:, cols(i, u, C, W)], xc[:, u], sd[:, u], ALU.mult)\
                                .then_inc(*S["normed"].inc)
        skip(affine is None, R, "scaled", W)
        skip(not shifted, R, "copied", W)
        if shifted:
            S["first"].base += 1


def skip(unused, rounds, name, per):
    if unused:
        STEPS[name].base -= rounds * per * STEPS[name].by


def shift_in(pool, dst, src, i, u, width, free, parts=2, first=None):
    S = STEPS
    seqs = width // T
    pool.wait_ge(*free)
    pool.wait_ge(S["first"].sem, PRIME)
    for b in range(seqs):
        at = (i * (parts * width) + u * width if first is None else first) + b * T
        pool.tensor_copy(dst[0:64, b, :], src[0:64, bass.ds(at, T)])
        last = pool.tensor_copy(dst[64:128, b, 1:T], src[64:128, bass.ds(at, T - 1)])
    last.then_inc(*S["copied"].inc)



UNITS = [(u, qb, par, pp) for u in range(2) for qb in range(2) for par in range(2) for pp in range(2)]
TURN, MIX = 2, 4
STEPS_T = MIX + 19


def heads_of(pp, par):
    return [(a, 2 * pp + a, 2 * (2 * pp + a) + par) for a in range(2)]


def pass_over(eng, name, n, count):
    if count:
        eng.wait_ge(*STEPS[name].at(-1, n - 1))
        eng.sem_inc(STEPS[name].sem, count)


def first_ones(eng, name, events, made, make, first=0):
    skipped = 0
    for n, x in enumerate(events):
        if made(x):
            pass_over(eng, name, first + n - skipped, skipped)
            skipped = 0
            make(x)
        else:
            skipped += 1
    pass_over(eng, name, first + len(events) - skipped, skipped)


class Core:

    def __init__(self, nc, ps, m, mem, mask, scale, dv, k_tile, v_at):
        buf = on_chip(nc, mem)
        self.ps, self.m, self.mask, self.scale, self.dv, self.k_tile, self.v_at = ps, m, mask, scale, dv, k_tile, v_at
        self.tiles = 4 if dv == DH else 2
        self.qt = buf("qt", P, 2, 4, T)
        self.kt = buf("kt", P, 2, self.tiles, T)
        self.v = buf("v_tok", P, 2, 2, HEADS * DH if dv == DH else N_KV * LAT)
        self.pr = buf("probs", P, 4, 2, T)
        self.nm = buf("minus_max", P, 4, 2)
        self.pt = buf("probs_t", P, 2, C)
        self.sums = buf("row_sums", P, 2, 2, HEADS)
        self.rs = buf("inv_sums", P, 2, 2, HEADS)
        self.o = buf("attended_tok", P, 2, HEADS * dv)

    def pe_step(self, pe, i, t, ready):
        S, ps = STEPS, self.ps
        if t < 16:
            u, qb, par, pp = UNITS[t]
            rows, nk = slice(64 * par, 64 * par + 64), P * (qb + 1)
            if t % 8 == 0:
                for what in ready(i, u):
                    pe.wait_ge(*what)
            pe.wait_ge(*S["masked"].at(i, t - 2))
            for a, tile, head in heads_of(pp, par):
                mm = pe.matmul(ps[:, t % 2, a * T:a * T + nk], self.qt[rows, u, tile, qb * P:(qb + 1) * P],
                               self.kt[rows, u, self.k_tile(tile), 0:nk], start=True, stop=True)
            mm.then_inc(*S["scores"].inc)
        n = t - TURN
        if 0 <= n < 16:
            u, qb, par, pp = UNITS[n]
            pe.wait_ge(*S["exps"].at(i, n))
            pe.wait_ge(*S["turned_sb"].at(i, n - 2))
            for a in range(2):
                for kb in range(qb + 1):
                    mm = pe.transpose(ps[:, 2 + n % 2, (2 * a + kb) * P:(2 * a + kb + 1) * P],
                                      self.pr[:, n % 4, a, kb * P:(kb + 1) * P], self.m["ident"][:])
            mm.then_inc(*S["turned"].inc)
        n = t - MIX
        if 0 <= n < 16:
            u, qb, par, pp = UNITS[n]
            pe.wait_ge(*S["turned_sb"].at(i, n))
            if n % 4 == 0:
                pe.wait_ge(*S["attended"].at(i, n // 4 - 2))
            for a, tile, head in heads_of(pp, par):
                at = self.v_at(head)
                for kb in range(qb + 1):
                    mm = pe.matmul(ps[:, 4 + qb, head * self.dv:(head + 1) * self.dv],
                                   self.pt[:, n % 2, (2 * a + kb) * P:(2 * a + kb + 1) * P],
                                   self.v[:, u, kb, at:at + self.dv], start=(kb == 0), stop=(kb == qb))
            mm.then_inc(*S["mixed"].inc)

    def act_step(self, act, i, t):
        S, ps = STEPS, self.ps
        if t < 16:
            u, qb, par, pp = UNITS[t]
            nk = P * (qb + 1)
            act.wait_ge(*S["rowmax"].at(i, t))
            if t % 4 == 0:
                act.wait_ge(*S["attended"].at(i, t // 4 - 4))
            for a, tile, head in heads_of(pp, par):
                scores = self.pr[:, t % 4, a, 0:nk]
                last = act.activation(scores, scores, ACT.Exp, bias=self.nm[:, t % 4, a:a + 1],
                                      accum_out=self.sums[:, u, qb, head:head + 1])
            last.then_inc(*S["exps"].inc)
        n = t - TURN
        if 0 <= n < 16:
            qb = UNITS[n][1]
            act.wait_ge(*S["turned"].at(i, n))
            act.wait_ge(*S["mixed"].at(i, n - 2))
            nk = P * (qb + 1)
            act.activation(self.pt[:, n % 2].rearrange("p (a k) -> p a k", a=2)[:, :, 0:nk],
                           bank(ps, 2 + n % 2, 2, T)[:, :, 0:nk], ACT.Copy).then_inc(*S["turned_sb"].inc)

    def dve_step(self, dve, i, t):
        S, ps = STEPS, self.ps
        if t < 16:
            u, qb, par, pp = UNITS[t]
            nk = P * (qb + 1)
            dve.wait_ge(*S["scores"].at(i, t))
            dve.wait_ge(*S["turned"].at(i, t - 4))
            dve.scalar_tensor_tensor(self.pr[:, t % 4, :, 0:nk], bank(ps, t % 2, 2, T)[:, :, 0:nk], self.scale,
                                     self.mask[:, qb:qb + 1, 0:nk].to_broadcast([P, 2, nk]), ALU.mult, ALU.add)\
                .then_inc(*S["masked"].inc)
            dve.wait_ge(*S["masked"].at(i, t))
            dve.tensor_reduce(self.nm[:, t % 4, :], self.pr[:, t % 4, :, 0:nk], AX.X, ALU.max, negate=True)\
                .then_inc(*S["rowmax"].inc)
        n = t - MIX - 1
        if 0 <= n < 16 and n % 4 == 3:
            u, qb = UNITS[n][0:2]
            dve.wait_ge(*S["mixed"].at(i, n))
            dve.reciprocal(self.rs[:, u, qb], self.sums[:, u, qb]).then_inc(*S["rowsum"].inc)
            dve.wait_ge(*S["rowsum"].at(i, n // 4))
            dve.wait_ge(*S["projected"].at(*self.o_read(i, n // 4)))
            dve.tensor_tensor(self.o[:, qb].rearrange("p (h d) -> p h d", h=HEADS),
                              bank(ps, 4 + qb, HEADS, self.dv),
                              self.rs[:, u, qb].unsqueeze(2).to_broadcast([P, HEADS, self.dv]), ALU.mult)\
                .then_inc(*S["attended"].inc)


CORE = dict(scores=16, masked=16, rowmax=16, exps=16, turned=16, turned_sb=16, mixed=16, rowsum=4, attended=4)


def latent_attention(nc, ps, m, a):
    S = STEPS
    with ExitStack() as mem:
        buf = on_chip(nc, mem)

        wqt, wkut, wvut, wo = buf("wqt", P, HEADS, P), buf("wkut", P, LAT), buf("wvut", P, LAT), buf("wo0", P, HEADS, P)
        wkd, wvd = buf("wkd", P, N_KV * LAT), buf("wvd", P, N_KV * LAT)
        wq, wk, wv = buf("wq_lat", P, HEADS, 64), buf("wk_lat", P, N_KV, 2, 64), buf("wo_lat", P, 2, P)
        xf, ot = buf("xf", P, 2, T), buf("ot", P, 2, 2, T)
        core = Core(nc, ps, m, mem, m["causal"], float(P) ** -0.5, LAT, lambda tile: tile // 2,
                    lambda head: head // 4 * LAT)
        load(nc, [(wqt[:], a["L0_attn_wq"]), (wkut[:], a["L0_attn_wk_up"]), (wvut[:], a["L0_attn_wv_up"]),
                  (wo[:], a["L0_attn_wo"].rearrange("(h d) o -> d h o", d=P)),
                  (wkd[:], a["L0_attn_wk_down"]), (wvd[:], a["L0_attn_wv_down"])])

        with Stage(1, prep=1, prep_sb=2), nc.Block() as block:
            @block.tensor
            def _(pe):
                for h in range(HEADS):
                    pe.matmul(ps[:, 0, h * LAT:(h + 1) * LAT], wqt[:, h], wkut[:], start=True, stop=True)
                for h in range(HEADS):
                    mm = pe.matmul(ps[32 * (h % 4):32 * (h % 4) + 32, 1, (h // 4) * P:(h // 4 + 1) * P], wvut[:],
                                   wo[:, h], start=True, stop=True)
                mm.then_inc(*S["prep"].inc)

            @block.vector
            def _(dve):
                dve.memset(wq[:], 0.0)
                dve.memset(wk[:], 0.0).then_inc(*S["prep_sb"].inc)
                dve.wait_ge(*S["prep_sb"].at(0, 0))
                dve.wait_ge(*S["prep"].at(0, 0))
                dve.tensor_copy(wq[:, :, 0:LAT], bank(ps, 0, HEADS, LAT))
                dve.tensor_copy(wv[:], bank(ps, 1, 2, P))
                for half in range(2):
                    last = dve.tensor_copy(wk[:, :, half, 0:LAT], wkd[:].rearrange("p (k l) -> p k l", k=N_KV))
                last.then_inc(*S["prep_sb"].inc)

        when = {t: [] for t in range(STEPS_T)}
        for k in range(4):
            when[2 + k].append((1, k))
            when[10 + k].append((0, k))
        for u in range(2):
            when[8 * u + 12].append((u, 4))
            when[8 * u + MIX + 10].append((u, 5))
        order = [x for t in range(STEPS_T) for x in when[t]]
        at = {x: n for n, x in enumerate(order)}
        PER = len(order)
        core.o_read = lambda i, w: (i, at[0, 4] if w >= 2 else at[1, 4] - PER)
        early = lambda x: x[0] == 0 and x[1] < 4

        def pe_part(pe, i, x):
            u, k = x
            e = at[x]
            o = ps[:, 6 + e % 2]
            pe.wait_ge(*S["freed_dve"].at(i, e - 2))
            if k < 2:
                if k == 0:
                    pe.wait_ge(*S["copied"].at(i, 1 - u))
                for tile in range(2):
                    mm = pe.matmul(o[:, tile * T:(tile + 1) * T],
                                   wq[:, 2 * (2 * k + tile):2 * (2 * k + tile) + 2].rearrange("p h l -> p (h l)"),
                                   xf[:, u], start=True, stop=True)
            elif k == 2:
                for kv in range(N_KV):
                    mm = pe.matmul(o[:, kv * T:(kv + 1) * T], wk[:, kv].rearrange("p h l -> p (h l)"),
                                   xf[:, u], start=True, stop=True)
            elif k == 3:
                for tb in range(2):
                    mm = pe.matmul(o[:, tb * 64:(tb + 1) * 64], xf[:, u, tb * P:(tb + 1) * P], wvd[:],
                                   start=True, stop=True)
            elif k == 4:
                pe.wait_ge(*S["attended"].at(i, 2 * u + 1))
                for c in range(2):
                    for qb in range(2):
                        mm = pe.transpose(o[:, (2 * c + qb) * P:(2 * c + qb + 1) * P],
                                          core.o[:, qb, c * P:(c + 1) * P], m["ident"][:])
            else:
                pe.wait_ge(*S["freed_dve"].at(i, at[u, 4]))
                for c in range(2):
                    mm = pe.matmul(o[:, 0:T], wv[:, c], ot[:, u, c], start=(c == 0), stop=(c == 1))
            mm.then_inc(*S["projected"].inc)

        def dve_part(dve, i, x):
            u, k = x
            dve.wait_ge(*S["projected"].at(i, at[x]))
            if k == 0:
                dve.wait_ge(*S["scores"].at(i, -1 if u else 7))
            if k == 3:
                dve.wait_ge(*S["mixed"].at(i, -1 if u else 7))
            src = ps[:, 6 + at[x] % 2]
            if k < 2:
                last = dve.tensor_copy(core.qt[:, u, 2 * k:2 * k + 2].rearrange("p a t -> p (a t)"), src)
            elif k == 2:
                last = dve.tensor_copy(core.kt[:, u].rearrange("p a t -> p (a t)"), src)
            elif k == 3:
                last = dve.tensor_copy(core.v[:, u].rearrange("p a t -> p (a t)"), src[:, 0:P])
            elif k == 4:
                last = dve.tensor_copy(ot[:, u].rearrange("p a t -> p (a t)"), src)
            else:
                last = dve.tensor_copy(m["s"][:, cols(i, u, T)], src[:, 0:T])
            last.then_inc(*S["freed_dve"].inc)

        with Stage(PAIRS, ["copied", "projected", "freed_dve"], copied=2, projected=PER, freed_dve=PER, **CORE), \
                nc.Block() as block:
            @block.gpsimd
            def _(pool):
                pass_over(pool, "copied", 0, 1)
                pool.tensor_copy(xf[:, 0], m["xn"][:, 0:T]).then_inc(*S["copied"].inc)
                with pool.Fori(0, PAIRS) as i:
                    for u in (1, 0):
                        pool.wait_ge(*S["projected"].at(i, at[u, 3] - PER))
                        pool.wait_ge(S["first"].sem, PRIME)
                        at_u = bass.ds(i * (2 * T) + (T if u else 2 * T), T)
                        pool.tensor_copy(xf[:, u], m["xn"][:, at_u]).then_inc(*S["copied"].inc)

            @block.tensor
            def _(pe):
                first_ones(pe, "projected", order, early, lambda x: pe_part(pe, -1, x))
                with pe.Fori(0, PAIRS) as i:
                    for t in range(STEPS_T):
                        core.pe_step(pe, i, t, lambda i, u: [S["freed_dve"].at(i, at[u, 3] - (0 if u else PER))])
                        for x in when[t]:
                            pe_part(pe, i, x)

            @block.scalar
            def _(act):
                act.preload_act_table_set("exp_and_others")
                with act.Fori(0, PAIRS) as i:
                    for t in range(STEPS_T):
                        core.act_step(act, i, t)

            @block.vector
            def _(dve):
                first_ones(dve, "freed_dve", order, early, lambda x: dve_part(dve, -1, x))
                with dve.Fori(0, PAIRS) as i:
                    for t in range(STEPS_T):
                        core.dve_step(dve, i, t)
                        for x in when[t]:
                            dve_part(dve, i, x)


def experts(nc, ps, m, a):
    with ExitStack() as mem:
        buf = on_chip(nc, mem)
        sorted_x = nc.dram_tensor("sorted_x", [(TILES + 8) * P, P], F32).ap()
        sorted_y = nc.dram_tensor("sorted_y", [TILES * P, P], F32).ap()
        up_w, down_w = buf("w1b1", P, EXPERTS, FF0 + FT0), buf("w2b2", P, EXPERTS, FF0 + P)
        sw, sb = buf("switch_w", P, EXPERTS), buf("switch_b", P, EXPERTS)
        r = {"lg": buf("logits", P, TOK, EXPERTS), "prob": buf("prob", P, TOK), "zeros": buf("zero_rows", P, 8, P),
             "pos": buf("row_of_token", P, TOK, dt=U32), "tile": buf("expert_of_tile", P, TILES + 8, dt=I32)}
        load(nc, [(up_w[:, e, 0:FF0], a["L0_ffn_w1"][e]) for e in range(EXPERTS)]
             + [(down_w[:, e, 0:FF0].rearrange("p (f d) -> p f d", d=P),
                 a["L0_ffn_w2"][e].rearrange("(f p) d -> p f d", p=P)) for e in range(EXPERTS)]
             + [(down_w[:, e, FF0:], a["L0_ffn_b2"][e].partition_broadcast(P)) for e in range(EXPERTS)]
             + [(up_w[:, :, FF0:], a["L0_ffn_b1"]), (sw[:], a["L0_ffn_switch_w"]),
                (sb[:], a["L0_ffn_switch_b"].partition_broadcast(P))])
        router_logits(nc, ps, m, r, sw, sb, sorted_x)
        route(nc, ps, r)
        scatter_tokens(nc, ps, m, r, sorted_x)
        expert_tiles(nc, ps, m, r, up_w, down_w, sorted_x, sorted_y)
        gather_tokens(nc, ps, m, r, sorted_y)


def tile_rows(dram, first, count):
    return dram[:].rearrange("(t p) d -> p t d", p=P)[:, bass.ds(first, count), :]


def router_logits(nc, ps, m, r, sw, sb, sorted_x):
    S, R = STEPS, ROUNDS
    with ExitStack() as mem:
        xf = on_chip(nc, mem)("xf", P, 2, C)
        copied = ["copied", "normed"]
        with Stage(R, copied=1, normed=1, projected=2, v1=2), nc.Block() as block:
            @block.gpsimd
            def _(pool):
                pool.memset(r["zeros"][:], 0.0).then_inc(S["g5"].sem, 1)
                pool.wait_ge(S["g5"].sem, S["g5"].base + 1)
                for k in range(TILES // 8 + 1):
                    pool.dma_start(tile_rows(sorted_x, 8 * k, 8), r["zeros"][:]).then_inc(*S[f"moved{k % 2}"].inc)
                with pool.Fori(0, R) as i:
                    pool.wait_ge(*S["projected"].at(i, -2))
                    pool.wait_ge(S["first"].sem, PRIME)
                    pool.tensor_copy(xf[:, 0], m["xn"][:, cols(i, 0, C)]).then_inc(*S["copied"].inc)

            @block.scalar
            def _(act):
                with act.Fori(0, R) as i:
                    act.wait_ge(*S["projected"].at(i, -1))
                    act.wait_ge(S["first"].sem, PRIME)
                    act.activation(xf[:, 1], m["xn"][:, cols(i, 1, C)], ACT.Copy).then_inc(*S["normed"].inc)

            @block.tensor
            def _(pe):
                with pe.Fori(0, R) as i:
                    for u in range(2):
                        pe.wait_ge(*S[copied[u]].at(i, 0))
                        pe.wait_ge(*S["v1"].at(i, u - 2))
                        for k in range(4):
                            mm = pe.matmul(ps[:, u, 8 * k:8 * k + 8], xf[:, u, k * P:(k + 1) * P], sw[:],
                                           start=True, stop=True)
                        mm.then_inc(*S["projected"].inc)

            @block.vector
            def _(dve):
                with dve.Fori(0, R) as i:
                    for u in range(2):
                        dve.wait_ge(*S["projected"].at(i, u))
                        dve.tensor_tensor(r["lg"][:, bass.ds(i * 8 + 4 * u, 4), :], bank(ps, u, 4, EXPERTS),
                                          sb[:].unsqueeze(1).to_broadcast([P, 4, EXPERTS]), ALU.add)\
                            .then_inc(*S["v1"].inc)
    S["g5"].base += 1
    for k in range(TILES // 8 + 1):
        S[f"moved{k % 2}"].base += 16


def route(nc, ps, r):
    S = STEPS
    E = EXPERTS
    with ExitStack() as mem:
        buf = on_chip(nc, mem)
        ints = buf("iotas_i", P, E + TOK + TILES + 8, dt=I32)
        nums = buf("iotas", P, E + TOK + TILES + 8)
        rank, starts, tile_no = nums[:, 0:E], nums[:, E:E + TOK], nums[:, E + TOK:]
        before, ones = buf("before", P, P), buf("ones", P, E * TOK)
        mx, oh, ex, big = buf("top", P, TOK), buf("chosen", P, TOK, E), buf("ex", P, TOK, E), buf("first_top", P, TOK)
        cnt, cum, pos = buf("count", P, E, TOK), buf("cum_count", P, E, TOK), buf("pos", P, E, TOK)
        ends, tiles, rows, adj = buf("row_ends", P, E + 1), buf("tile_ends", P, E + 1), buf("rows", P, E), buf("adj", P, E)
        over, nt, posf = buf("over", P, E, TOK), buf("n_tiles", P, E), buf("pos_f", P, TOK)
        past, ef = buf("past", P, TILES + 8, E), buf("tile_f", P, TILES + 8)
        lg = r["lg"]
        ek = [P, E, TOK]
        with Stage(1, v1=25, a1=1, m1=1), nc.Block() as block:
            @block.gpsimd
            def _(pool):
                pool.iota(ints[:, 0:E], pattern=[[-1, E]], base=E, channel_multiplier=0)
                pool.iota(ints[:, E:E + TOK], pattern=[[P, TOK]], base=0, channel_multiplier=0)
                pool.iota(ints[:, E + TOK:], pattern=[[1, TILES + 8]], base=0, channel_multiplier=0)
                pool.memset(before[:], 1.0)
                pool.memset(ends[:], 0.0)
                pool.memset(tiles[:], 0.0)
                pool.memset(ones[:], 1.0).then_inc(S["g5"].sem, 1)
                pool.wait_ge(S["g5"].sem, S["g5"].base + 1)
                pool.tensor_copy(nums[:], ints[:])
                pool.affine_select(out=before[:], in_=before[:], compare_op=ALU.is_ge, fill=0.0, base=-1,
                                   pattern=[[1, P]], channel_multiplier=-1).then_inc(S["g5"].sem, 1)

            @block.tensor
            def _(pe):
                pe.wait_ge(S["g5"].sem, S["g5"].base + 2)
                pe.wait_ge(*S["v1"].at(0, 4))
                flat = oh[:].rearrange("p k e -> p (k e)")
                pe.matmul(ps[:, 2, :], before[:], flat, start=True, stop=True)
                pe.matmul(ps[:, 3, :], ones[:, 0:P], flat, start=True, stop=True).then_inc(*S["m1"].inc)

            @block.scalar
            def _(act):
                act.wait_ge(*S["v1"].at(0, 1))
                act.activation(ex[:], lg[:], ACT.Exp).then_inc(*S["a1"].inc)

            @block.vector
            def _(dve):
                dve.wait_ge(S["g5"].sem, S["g5"].base + 2)
                done = S["v1"].inc
                dve.tensor_reduce(mx[:], lg[:], AX.X, ALU.max).then_inc(*done)
                dve.wait_ge(*S["v1"].at(0, 0))
                dve.tensor_tensor(lg[:], lg[:], mx[:].unsqueeze(2).to_broadcast([P, TOK, E]), ALU.subtract)\
                    .then_inc(*done)
                dve.wait_ge(*S["v1"].at(0, 1))
                dve.scalar_tensor_tensor(oh[:], lg[:], 0.0, rank.unsqueeze(1).to_broadcast([P, TOK, E]),
                                         ALU.is_ge, ALU.mult).then_inc(*done)
                dve.wait_ge(*S["v1"].at(0, 2))
                dve.tensor_reduce(big[:], oh[:], AX.X, ALU.max).then_inc(*done)
                dve.wait_ge(*S["v1"].at(0, 3))
                dve.tensor_tensor(oh[:], oh[:], big[:].unsqueeze(2).to_broadcast([P, TOK, E]), ALU.is_equal)\
                    .then_inc(*done)
                dve.wait_ge(*S["a1"].at(0, 0))
                dve.tensor_reduce(mx[:], ex[:], AX.X, ALU.add).then_inc(*done)
                dve.wait_ge(*S["v1"].at(0, 5))
                dve.reciprocal(r["prob"][:], mx[:]).then_inc(*done)
                dve.wait_ge(*S["m1"].at(0, 0))
                dve.tensor_copy(cnt[:], bank(ps, 3, TOK, E).rearrange("p k e -> p e k")).then_inc(*done)
                dve.wait_ge(*S["v1"].at(0, 7))
                flat = "p e k -> p (e k)"
                dve.tensor_tensor_scan(cum[:].rearrange(flat), ones[:], cnt[:].rearrange(flat), 0.0, ALU.mult,
                                       ALU.add).then_inc(*done)
                dve.wait_ge(*S["v1"].at(0, 8))
                dve.tensor_copy(ends[:, 1:], cum[:, :, TOK - 1]).then_inc(*done)
                dve.wait_ge(*S["v1"].at(0, 9))
                dve.tensor_tensor(rows[:], ends[:, 1:], ends[:, 0:E], ALU.subtract).then_inc(*done)
                dve.wait_ge(*S["v1"].at(0, 10))
                dve.tensor_tensor(over[:], rows[:].unsqueeze(2).to_broadcast(ek),
                                  starts.unsqueeze(1).to_broadcast(ek), ALU.is_gt).then_inc(*done)
                dve.wait_ge(*S["v1"].at(0, 11))
                dve.tensor_reduce(nt[:], over[:], AX.X, ALU.add).then_inc(*done)
                dve.wait_ge(*S["v1"].at(0, 12))
                dve.tensor_tensor_scan(tiles[:, 1:], ones[:, 0:E], nt[:], 0.0, ALU.mult, ALU.add).then_inc(*done)
                dve.wait_ge(*S["v1"].at(0, 13))
                dve.scalar_tensor_tensor(adj[:], tiles[:, 0:E], float(P), ends[:, 0:E], ALU.mult, ALU.subtract)\
                    .then_inc(*done)
                dve.tensor_tensor(pos[:], cum[:], cnt[:], ALU.subtract).then_inc(*done)
                dve.wait_ge(*S["v1"].at(0, 15))
                dve.tensor_tensor(pos[:], pos[:], adj[:].unsqueeze(2).to_broadcast(ek), ALU.add).then_inc(*done)
                dve.wait_ge(*S["v1"].at(0, 16))
                dve.tensor_tensor(pos[:], pos[:], bank(ps, 2, TOK, E).rearrange("p k e -> p e k"), ALU.add)\
                    .then_inc(*done)
                dve.wait_ge(*S["v1"].at(0, 17))
                dve.tensor_tensor(pos[:], pos[:], oh[:].rearrange("p k e -> p e k"), ALU.mult).then_inc(*done)
                dve.wait_ge(*S["v1"].at(0, 18))
                dve.tensor_reduce(posf[:], pos[:].rearrange("p e k -> p k e"), AX.X, ALU.add).then_inc(*done)
                dve.wait_ge(*S["v1"].at(0, 19))
                dve.tensor_copy(r["pos"][:], posf[:]).then_inc(*done)
                te = [P, TILES + 8, E]
                dve.tensor_tensor(past[:], tile_no.unsqueeze(2).to_broadcast(te),
                                  tiles[:, 1:].unsqueeze(1).to_broadcast(te), ALU.is_ge).then_inc(*done)
                dve.wait_ge(*S["v1"].at(0, 21))
                dve.tensor_reduce(ef[:], past[:], AX.X, ALU.add).then_inc(*done)
                dve.wait_ge(*S["v1"].at(0, 22))
                dve.tensor_scalar(ef[:], ef[:], float(E - 1), None, ALU.min).then_inc(*done)
                dve.wait_ge(*S["v1"].at(0, 23))
                dve.tensor_copy(r["tile"][:], ef[:]).then_inc(*done)
    S["g5"].base += 2


def scatter_tokens(nc, ps, m, r, sorted_x):
    S, R = STEPS, ROUNDS
    with ExitStack() as mem:
        buf = on_chip(nc, mem)
        xf, rows, idx = buf("xf", P, 2, C), buf("token_rows", P, 2, C), buf("row_idx", P, 2, 4, dt=U32)
        with Stage(R, copied=2, turned=2, turned_sb=2, g1=2, g2=2, moved0=4, moved1=4), nc.Block() as block:
            @block.scalar
            def _(act):
                with act.Fori(0, R) as i:
                    for u in range(2):
                        act.wait_ge(*S["turned"].at(i, u - 2))
                        act.wait_ge(S["first"].sem, PRIME)
                        act.activation(xf[:, u], m["xn"][:, cols(i, u, C)], ACT.Copy).then_inc(*S["copied"].inc)

            @block.tensor
            def _(pe):
                with pe.Fori(0, R) as i:
                    for u in range(2):
                        pe.wait_ge(*S["copied"].at(i, u))
                        pe.wait_ge(*S["turned_sb"].at(i, u - 2))
                        for k in range(4):
                            mm = pe.transpose(ps[:, u, k * P:(k + 1) * P], xf[:, u, k * P:(k + 1) * P], m["ident"][:])
                        mm.then_inc(*S["turned"].inc)

            @block.vector
            def _(dve):
                with dve.Fori(0, R) as i:
                    for u in range(2):
                        dve.wait_ge(*S["turned"].at(i, u))
                        dve.wait_ge(*S[f"moved{u}"].at(i, -1))
                        dve.tensor_copy(rows[:, u], ps[:, u]).then_inc(*S["turned_sb"].inc)

            @block.gpsimd
            def _(pool):
                for u in range(2):
                    pool.wait_ge(S[f"moved{u}"].sem, S[f"moved{u}"].base)
                with pool.Fori(0, R) as i:
                    for u in range(2):
                        pool.wait_ge(*S[f"moved{u}"].at(i, -1))
                        pool.wait_ge(S["first"].sem, PRIME)
                        pool.tensor_copy(idx[:, u], r["pos"][:, bass.ds(i * 8 + 4 * u, 4)]).then_inc(*S["g1"].inc)
                        pool.wait_ge(*S["g1"].at(i, u))
                        pool.wait_ge(*S["turned_sb"].at(i, u))
                        pool.sem_inc(S["g2"].sem, 1)
                        for k in range(4):
                            pool.indirect_dma_start(sorted_x[:], bass.IndirectOffsetOnAxis(idx[:, u, k:k + 1], 0),
                                                    rows[:, u, k * P:(k + 1) * P], None)\
                                .then_inc(*S[f"moved{u}"].inc)
                for u in range(2):
                    pool.wait_ge(*S[f"moved{u}"].at(R - 1, 3))


def expert_tiles(nc, ps, m, r, up_w, down_w, sorted_x, sorted_y):
    S = STEPS
    R, LAG = TILES // 8, 2
    with ExitStack() as mem:
        buf = on_chip(nc, mem)
        xs, xt, ys = buf("rows_in", P, 2, 4, P), buf("rows_turned", P, 2, C), buf("rows_out", P, 2, 4, P)
        w1, w2, hs = buf("w1b1_now", P, 2, FF0 + FT0), buf("w2b2_now", P, 4, FF0 + P), buf("hidden", P, 4, FT0, P)
        made = ["turned", "copied", "g1"]
        with Stage(R, made, turned=2, copied=2, up=8, gated=8, act_a=8, down=8, added=8, g1=8, g2=8, fetched0=1,
                   fetched1=1, stored0=1, stored1=1), nc.Block() as block:
            @block.sync
            def _(sp):
                sp.dma_start(xs[:, 0], tile_rows(sorted_x, 0, 4)).then_inc(*S["fetched0"].inc)
                sp.dma_start(xs[:, 1], tile_rows(sorted_x, 4, 4)).then_inc(*S["fetched1"].inc)
                with sp.Fori(0, R) as i:
                    for u in range(2):
                        sp.wait_ge(*S["added"].at(i, 4 * u + 3))
                        sp.wait_ge(S["first"].sem, PRIME)
                        sp.dma_start(tile_rows(sorted_y, i * 8 + 4 * u, 4), ys[:, u]).then_inc(*S[f"stored{u}"].inc)
                        sp.wait_ge(*S["turned"].at(i, u - 1))
                        sp.wait_ge(S["first"].sem, PRIME)
                        sp.dma_start(xs[:, u], tile_rows(sorted_x, i * 8 + 8 + 4 * u, 4))\
                            .then_inc(*S[f"fetched{u}"].inc)
                for u in range(2):
                    sp.wait_ge(*S[f"stored{u}"].at(R - 1, 0))
                    sp.wait_ge(*S[f"fetched{u}"].at(R, 0))

            def turn(pe, i, event):
                u = 1 - event
                pe.wait_ge(*S[f"fetched{u}"].at(i, event))
                pe.wait_ge(*S["copied"].at(i, event - 1))
                for k in range(4):
                    mm = pe.transpose(ps[:, 0, k * P:(k + 1) * P], xs[:, u, k], m["ident"][:])
                mm.then_inc(*S["turned"].inc)

            @block.tensor
            def _(pe):
                pass_over(pe, "turned", 0, 1)
                turn(pe, -1, 1)
                with pe.Fori(0, R) as i:
                    for n in range(8 + LAG):
                        if n < 8:
                            pe.wait_ge(*S["g1"].at(i, n - 1))
                            if n % 4 == 0:
                                pe.wait_ge(*S["copied"].at(i, n // 4 - 1))
                            pe.wait_ge(*S["gated"].at(i, n - 2))
                            for f in range(FT0):
                                mm = pe.matmul(ps[:, 2 + n % 2, f * P:(f + 1) * P], w1[:, n % 2, f * P:(f + 1) * P],
                                               xt[:, n // 4, n % 4 * P:(n % 4 + 1) * P], start=True, stop=True)
                            mm.then_inc(*S["up"].inc)
                        d = n - LAG
                        if d >= 0:
                            pe.wait_ge(*S["act_a"].at(i, d))
                            pe.wait_ge(*S["g2"].at(i, d))
                            pe.wait_ge(*S["added"].at(i, d - 2))
                            for f in range(FT0):
                                mm = pe.matmul(ps[:, 4 + d % 2, 0:P], hs[:, d % 4, f], w2[:, d % 4, f * P:(f + 1) * P],
                                               start=(f == 0), stop=(f == FT0 - 1))
                            mm.then_inc(*S["down"].inc)
                        if n in (1, 5):
                            turn(pe, i, n // 4)

            @block.gpsimd
            def _(pool):
                with pool.Fori(0, R) as i:
                    for n in range(8):
                        e = pool.value_load(r["tile"][0:1, bass.ds(i * 8 + n, 1)], min_val=0, max_val=EXPERTS - 1)
                        pool.wait_ge(*S["added"].at(i, n - 4))
                        pool.wait_ge(S["first"].sem, PRIME)
                        pool.tensor_copy(w2[:, n % 4], down_w[:, bass.ds(e, 1), :].rearrange("p a b -> p (a b)"))\
                            .then_inc(*S["g2"].inc)

            def take_w1(act, i, n):
                e = act.value_load(r["tile"][0:1, bass.ds(i * 8 + n, 1)], min_val=0, max_val=EXPERTS - 1)
                act.wait_ge(*S["up"].at(i, n - 2))
                act.wait_ge(*S["gated"].at(i, n - 2))
                act.wait_ge(S["first"].sem, PRIME)
                act.activation(w1[:, n % 2], up_w[:, bass.ds(e, 1), :].rearrange("p a b -> p (a b)"), ACT.Copy)\
                    .then_inc(*S["g1"].inc)

            @block.scalar
            def _(act):
                act.preload_act_table_set("gelu_apprx_tanh_and_others")
                pass_over(act, "g1", 0, 7)
                take_w1(act, -1, 8)
                with act.Fori(0, R) as i:
                    for n in range(8):
                        take_w1(act, i, n + 1)
                        act.wait_ge(*S["gated"].at(i, n))
                        act.activation(hs[:, n % 4], hs[:, n % 4], ACT.Gelu_apprx_tanh).then_inc(*S["act_a"].inc)

            def keep_turned(dve, i, event):
                dve.wait_ge(*S["turned"].at(i, event))
                dve.wait_ge(*S["up"].at(i, 3 if event else -1))
                dve.tensor_copy(xt[:, 1 - event], ps[:, 0]).then_inc(*S["copied"].inc)

            @block.vector
            def _(dve):
                pass_over(dve, "copied", 0, 1)
                dve.wait_ge(*S["turned"].at(-1, 1))
                dve.tensor_copy(xt[:, 0], ps[:, 0]).then_inc(*S["copied"].inc)
                with dve.Fori(0, R) as i:
                    for n in range(8 + LAG):
                        if n < 8:
                            dve.wait_ge(*S["up"].at(i, n))
                            dve.wait_ge(*S["down"].at(i, n - 4))
                            dve.tensor_tensor(hs[:, n % 4], bank(ps, 2 + n % 2, FT0, P),
                                              w1[:, n % 2, FF0:].unsqueeze(2).to_broadcast([P, FT0, P]), ALU.add)\
                                .then_inc(*S["gated"].inc)
                        d = n - LAG
                        if d >= 0:
                            dve.wait_ge(*S["down"].at(i, d))
                            if d % 4 == 0:
                                dve.wait_ge(*S[f"stored{d // 4}"].at(i, -1))
                            dve.tensor_tensor(ys[:, d // 4, d % 4], ps[:, 4 + d % 2, 0:P], w2[:, d % 4, FF0:], ALU.add)\
                                .then_inc(*S["added"].inc)
                        if n in (1, 5):
                            keep_turned(dve, i, n // 4)
        for u in range(2):
            S[f"fetched{u}"].base += 16


def gather_tokens(nc, ps, m, r, sorted_y):
    S, R = STEPS, ROUNDS
    with ExitStack() as mem:
        buf = on_chip(nc, mem)
        yg, idx, gate = buf("rows_got", P, 2, 4, P), buf("row_idx", P, 2, 4, dt=U32), buf("gate", P, 2, C)
        with Stage(R, g1=2, g2=2, moved0=4, moved1=4, v1=2, silu=2, turned=2, weighed=2, added=2), \
                nc.Block() as block:
            @block.gpsimd
            def _(pool):
                with pool.Fori(0, R) as i:
                    for u in range(2):
                        pool.wait_ge(*S[f"moved{u}"].at(i, -1))
                        pool.wait_ge(S["first"].sem, PRIME)
                        pool.tensor_copy(idx[:, u], r["pos"][:, bass.ds(i * 8 + 4 * u, 4)]).then_inc(*S["g1"].inc)
                        pool.wait_ge(*S["g1"].at(i, u))
                        pool.wait_ge(*S["turned"].at(i, u - 2))
                        pool.sem_inc(S["g2"].sem, 1)
                        for k in range(4):
                            pool.indirect_dma_start(yg[:, u, k], None, sorted_y[:],
                                                    bass.IndirectOffsetOnAxis(idx[:, u, k:k + 1], 0))\
                                .then_inc(*S[f"moved{u}"].inc)

            @block.scalar
            def _(act):
                act.preload_act_table_set("silu_and_others")
                with act.Fori(0, R) as i:
                    for u in range(2):
                        act.wait_ge(*S["v1"].at(i, u))
                        act.activation(yg[:, u], yg[:, u], ACT.Silu).then_inc(*S["silu"].inc)

            @block.tensor
            def _(pe):
                with pe.Fori(0, R) as i:
                    for u in range(2):
                        pe.wait_ge(*S["silu"].at(i, u))
                        pe.wait_ge(*S["weighed"].at(i, u - 2))
                        for k in range(4):
                            mm = pe.transpose(ps[:, u, k * P:(k + 1) * P], yg[:, u, k], m["ident"][:])
                        mm.then_inc(*S["turned"].inc)

            @block.vector
            def _(dve):
                with dve.Fori(0, R) as i:
                    for u in range(2):
                        dve.wait_ge(*S[f"moved{u}"].at(i, 3))
                        dve.tensor_tensor(yg[:, u], yg[:, u], r["prob"][:, bass.ds(i * 8 + 4 * u, 4)].unsqueeze(2)
                                          .to_broadcast([P, 4, P]), ALU.mult).then_inc(*S["v1"].inc)
                    for u in range(2):
                        dve.wait_ge(*S["turned"].at(i, u))
                        dve.wait_ge(*S["added"].at(i, u - 2))
                        dve.tensor_tensor(gate[:, u], ps[:, u], m["s"][:, cols(i, u, C)], ALU.mult)\
                            .then_inc(*S["weighed"].inc)
                        dve.wait_ge(*S["weighed"].at(i, u))
                        x = m["x"][:, cols(i, u, C)]
                        dve.tensor_tensor(x, x, gate[:, u], ALU.add).then_inc(*S["added"].inc)


def linear_attention(nc, ps, m, a):
    S = STEPS
    with ExitStack() as mem:
        buf = on_chip(nc, mem)

        wq, wout, bout, blocks = buf("wqkv1", P, 3 * P), buf("wout1", P, P), buf("bout1", P, 1), buf("blocks", P, P)
        xf, ks, kx, kp = buf("xf", P, 2, T), buf("k_min", P, 2, 2, P), buf("k_exp", P, 2, 2, P), buf("k_phi", P, 2, 2, P)
        va = buf("v_one", P, 2, 2, P + 1)
        qs, qx, qp = buf("q_min", P, 2, T), buf("q_exp", P, 2, T), buf("q_phi", P, 2, T)
        kv, kd = buf("kv_heads", P, 2, P), buf("k_heads", P, 2, P)
        z, y = buf("z_inv", P, 2, T), buf("y1", P, 2, T)
        load(nc, [(wq[:], a["L1_attn_w_qkv"]), (wout[:], a["L1_attn_w_out"]), (bout[:], column(a["L1_attn_b_out"]))])
        with Stage(PAIRS, copied=2, projected=2, m1=2, m2=2, m3=2, m4=2, v1=2, v2=2, v3=2, v4=2, v5=2, v6=2, v7=2,
                   v8=2, a1=2, a2=2, a3=2, a4=2), nc.Block() as block:
            @block.gpsimd
            def _(pool):
                pool.memset(va[:], 1.0)
                pool.memset(blocks[:], 1.0).then_inc(S["g5"].sem, 1)
                pool.wait_ge(S["g5"].sem, S["g5"].base + 1)
                view = blocks[:].rearrange("p (h d) -> p h d", d=HD1)
                pool.affine_select(out=view, in_=view, compare_op=ALU.is_ge, fill=0.0, base=0,
                                   pattern=[[-HD1, P // HD1], [0, HD1]], channel_multiplier=1)\
                    .then_inc(S["g5"].sem, 1)
                pool.wait_ge(S["g5"].sem, S["g5"].base + 2)
                pool.affine_select(out=view, in_=view, compare_op=ALU.is_ge, fill=0.0, base=HD1 - 1,
                                   pattern=[[HD1, P // HD1], [0, HD1]], channel_multiplier=-1)\
                    .then_inc(S["g5"].sem, 1)
                with pool.Fori(0, PAIRS) as i:
                    for u in range(2):
                        pool.wait_ge(*S["m1"].at(i, u - 2))
                        pool.wait_ge(S["first"].sem, PRIME)
                        pool.tensor_copy(xf[:, u], m["xn"][:, cols(i, u, T)]).then_inc(*S["copied"].inc)

            @block.tensor
            def _(pe):
                with pe.Fori(0, PAIRS) as i:
                    for u in range(2):
                        pe.wait_ge(*S["copied"].at(i, u))
                        pe.wait_ge(*S["v3"].at(i, u - 2))
                        pe.wait_ge(*S["a2"].at(i, u - 2))
                        for tb in range(2):
                            mm = pe.matmul(ps[:, u, tb * 2 * P:(tb + 1) * 2 * P], xf[:, u, tb * P:(tb + 1) * P],
                                           wq[:, P:3 * P], start=True, stop=True)
                        mm.then_inc(*S["projected"].inc)
                        pe.wait_ge(*S["v6"].at(i, u - 2))
                        pe.wait_ge(*S["v8"].at(i, u - 2))
                        pe.matmul(ps[:, 2 + u, 0:T], wq[:, 0:P], xf[:, u], start=True, stop=True)\
                            .then_inc(*S["m1"].inc)
                    for u in range(2):
                        pe.wait_ge(*S["v3"].at(i, u))
                        pe.wait_ge(*S["a2"].at(i, u))
                        pe.wait_ge(*S["v5"].at(i, u - 2))
                        for tb in range(2):
                            mm = pe.matmul(ps[:, 4 + u, 0:P + 1], kp[:, u, tb], va[:, u, tb], start=(tb == 0),
                                           stop=(tb == 1))
                        mm.then_inc(*S["m2"].inc)
                    for u in range(2):
                        pe.wait_ge(*S["v6"].at(i, u))
                        pe.wait_ge(*S["v5"].at(i, u))
                        pe.wait_ge(*S["v8"].at(i, u - 2))
                        pe.wait_ge(*S["a4"].at(i, u - 2))
                        pe.matmul(ps[:, 6 + u, 0:T], kv[:, u], qp[:, u], start=True, stop=True)
                        pe.matmul(ps[:, 6 + u, T:2 * T], kd[:, u], qp[:, u], start=True, stop=True)\
                            .then_inc(*S["m3"].inc)
                    for u in range(2):
                        pe.wait_ge(*S["v8"].at(i, u))
                        pe.matmul(ps[:, 6 + u, 0:T], wout[:], y[:, u], start=True, stop=True)\
                            .then_inc(*S["m4"].inc)

            @block.scalar
            def _(act):
                act.preload_act_table_set("exp_and_others")
                with act.Fori(0, PAIRS) as i:
                    for u in range(2):
                        act.wait_ge(*S["v1"].at(i, u))
                        act.wait_ge(*S["v3"].at(i, u - 2))
                        act.activation(kx[:, u], ks[:, u], ACT.Exp).then_inc(*S["a1"].inc)
                        act.wait_ge(*S["v2"].at(i, u))
                        act.wait_ge(*S["v6"].at(i, u - 2))
                        act.activation(qx[:, u], qs[:, u], ACT.Exp).then_inc(*S["a3"].inc)
                    for u in range(2):
                        act.wait_ge(*S["m4"].at(i, u))
                        act.wait_ge(S["first"].sem, PRIME)
                        act.activation(m["s"][:, cols(i, u, T)], ps[:, 6 + u, 0:T], ACT.Identity, bias=bout[:, 0:1])\
                            .then_inc(*S["a4"].inc)

            @block.vector
            def _(dve):
                dve.wait_ge(S["g5"].sem, S["g5"].base + 3)
                with dve.Fori(0, PAIRS) as i:
                    for u in range(2):
                        k_ps = bank(ps, u, 2, 2, P)[:, :, 0]
                        dve.wait_ge(*S["projected"].at(i, u))
                        dve.tensor_scalar(ks[:, u], k_ps, 0.0, None, ALU.min).then_inc(*S["v1"].inc)
                        dve.wait_ge(*S["m2"].at(i, u - 2))
                        dve.tensor_copy(va[:, u, :, 0:P], bank(ps, u, 2, 2, P)[:, :, 1]).then_inc(*S["a2"].inc)
                        dve.wait_ge(*S["m1"].at(i, u))
                        dve.tensor_scalar(qs[:, u], ps[:, 2 + u, 0:T], 0.0, None, ALU.min).then_inc(*S["v2"].inc)
                    for u in range(2):
                        k_ps = bank(ps, u, 2, 2, P)[:, :, 0]
                        dve.wait_ge(*S["a1"].at(i, u))
                        dve.wait_ge(*S["m2"].at(i, u - 2))
                        dve.scalar_tensor_tensor(kp[:, u], k_ps, 0.0, kx[:, u], ALU.max, ALU.add)\
                            .then_inc(*S["v3"].inc)
                        dve.wait_ge(*S["a3"].at(i, u))
                        dve.wait_ge(*S["m3"].at(i, u - 2))
                        dve.scalar_tensor_tensor(qp[:, u], ps[:, 2 + u, 0:T], 0.0, qx[:, u], ALU.max, ALU.add)\
                            .then_inc(*S["v6"].inc)
                    for u in range(2):
                        dve.wait_ge(*S["m2"].at(i, u))
                        dve.tensor_tensor(kv[:, u], ps[:, 4 + u, 0:P], blocks[:], ALU.mult)
                        dve.tensor_scalar(kd[:, u], blocks[:], ps[:, 4 + u, P:P + 1], None, ALU.mult)\
                            .then_inc(*S["v5"].inc)
                    for u in range(2):
                        dve.wait_ge(*S["m3"].at(i, u))
                        dve.tensor_scalar(z[:, u], ps[:, 6 + u, T:2 * T], 1e-6, None, ALU.add).then_inc(*S["v4"].inc)
                        dve.wait_ge(*S["v4"].at(i, u))
                        dve.reciprocal(z[:, u], z[:, u]).then_inc(*S["v7"].inc)
                        dve.wait_ge(*S["v7"].at(i, u))
                        dve.wait_ge(*S["m4"].at(i, u - 2))
                        dve.tensor_tensor(y[:, u], ps[:, 6 + u, 0:T], z[:, u], ALU.mult).then_inc(*S["v8"].inc)
        S["g5"].base += 3


def integer_ffn(nc, ps, m, a):
    S, R = STEPS, ROUNDS
    FT = HID1 // P
    with ExitStack() as mem:
        buf = on_chip(nc, mem)

        raw = buf("raw", P, 3, HID1, dt=I32)
        w = buf("w_deq", P, 3, HID1)
        sg, hd, gate = buf("silu_gate", P, 2, C), buf("hid1", P, 2, C), buf("gate", P, 2, C)
        load(nc, [(raw[:, 0], a["L1_ffn_w_gate"]), (raw[:, 1], a["L1_ffn_w_up"]),
                  (raw[:, 2].rearrange("p (f d) -> p f d", f=FT),
                   a["L1_ffn_w_down"].rearrange("(f p) d -> p f d", p=P))])
        with Stage(R, up=2 * FT, act_a=2 * FT, gated=2 * FT, m1=2 * FT, silu=2, weighed=2, added=2), nc.Block() as block:
            @block.tensor
            def _(pe):
                pe.wait_ge(S["g5"].sem, S["g5"].base + 2)
                with pe.Fori(0, R) as i:
                    for u in range(2):
                        for f in range(FT + 1):
                            h = FT * u + f
                            if f < FT:
                                pe.wait_ge(*S["gated"].at(i, h - 2))
                                for g in range(2):
                                    mm = pe.matmul(ps[:, 2 * (h % 2) + g, :], w[:, g, f * P:(f + 1) * P],
                                                   m["xn"][:, cols(i, u, C)], start=True, stop=True)
                                mm.then_inc(*S["up"].inc)
                            if f >= 1:
                                pe.wait_ge(*S["gated"].at(i, h - 1))
                                if f == 1:
                                    pe.wait_ge(*S["silu"].at(i, u - 2))
                                mm = pe.matmul(ps[:, 4 + u, :], w[:, 2, (f - 1) * P:f * P], hd[:, (h - 1) % 2],
                                               start=(f == 1), stop=(f == FT))
                                mm.then_inc(*S["m1"].inc)

            @block.scalar
            def _(act):
                act.preload_act_table_set("silu_and_others")
                with act.Fori(0, R) as i:
                    for u in range(2):
                        for h in range(FT * u, FT * (u + 1)):
                            act.wait_ge(*S["up"].at(i, h))
                            act.wait_ge(*S["gated"].at(i, h - 2))
                            act.activation(sg[:, h % 2], ps[:, 2 * (h % 2), :], ACT.Silu).then_inc(*S["act_a"].inc)
                        act.wait_ge(*S["m1"].at(i, FT * (u + 1) - 1))
                        act.wait_ge(*S["added"].at(i, u - 2))
                        act.activation(gate[:, u], ps[:, 4 + u, :], ACT.Silu).then_inc(*S["silu"].inc)

            @block.vector
            def _(dve):
                dve.tensor_copy(w[:], raw[:]).then_inc(S["g5"].sem, 1)
                dve.wait_ge(S["g5"].sem, S["g5"].base + 1)
                dve.tensor_scalar(w[:], w[:], float(np.float32(1.0 / 127.0)), None, ALU.mult).then_inc(S["g5"].sem, 1)
                with dve.Fori(0, R) as i:
                    for u in range(2):
                        for h in range(FT * u, FT * (u + 1)):
                            dve.wait_ge(*S["act_a"].at(i, h))
                            dve.wait_ge(*S["m1"].at(i, h - 2))
                            dve.tensor_tensor(hd[:, h % 2], sg[:, h % 2], ps[:, 2 * (h % 2) + 1, :], ALU.mult)\
                                .then_inc(*S["gated"].inc)
                    for u in range(2):
                        add_gated(dve, m, gate, i, u)
        S["g5"].base += 2


def scan_mixer(nc, ps, m, a):
    S, R = STEPS, ROUNDS
    IT = INNER // P
    with ExitStack() as mem:
        buf = on_chip(nc, mem)

        win, wdel, wout = buf("win2", P, 2 * INNER), buf("wdel", P, IT, INNER), buf("wout2", P, IT, P)
        bin_, cw, cb = buf("bin2", P, 2 * IT), buf("cw", P, IT, TAPS2), buf("cb", P, IT)
        bdel, bout = buf("bdel", P, IT), buf("bout2", P, 1)
        vp = buf("v_pad", P, 4, 2, T + TAPS2 - 1)
        cv, sg, dl = buf("conv", P, 4, C), buf("sig", P, 4, C), buf("delta", P, 4, C)
        val, bb, sc = buf("val", P, 4, C), buf("b_scan", P, 4, C), buf("scans", P, 4, 2, C)
        gt, fu = buf("gate2", P, 4, C), buf("fused", P, 4, C)
        load(nc, [(win[:], a["L2_attn_W_in"]), (wdel[:], a["L2_attn_W_delta"].rearrange("(c p) e -> p c e", p=P)),
                  (wout[:], a["L2_attn_W_out"].rearrange("(c p) d -> p c d", p=P)),
                  (bin_[:], a["L2_attn_b_in"]), (cw[:], a["L2_attn_conv_w"].rearrange("(c p) k -> p c k", p=P)),
                  (cb[:], a["L2_attn_conv_b"]), (bdel[:], a["L2_attn_b_delta"]),
                  (bout[:], column(a["L2_attn_b_out"]))])
        FRONT = ["m1", "m2", "m3", "a1", "a2", "a3", "a4", "v1", "v2", "v3", "v4", "g1", "g2"]

        def slot(k, q):
            return 2 * (1 - k) + q

        def front_of(u, q):
            return 2 * u + q - 2

        def last_back(k, q):
            return q - 2 if k == 0 else q

        def rounds(eng, mine, front, turn):
            for name in mine:
                pass_over(eng, name, 0, 2)
            front(-1, 1)
            with eng.Fori(0, R - 1) as i:
                for k in range(2):
                    turn(i, k, True)
            turn(R - 1, 0, True)
            turn(R - 1, 1, False)
            for name in mine:
                eng.wait_ge(*S[name].at(R - 1, 1))
                eng.sem_inc(S[name].sem, 2)

        with Stage(R, FRONT, m4=2, v7=4, v8=4, v9=4, added=2, **{n: 4 for n in FRONT}), nc.Block() as block:
            def pe_in(pe, i, k):
                x = m["s"][:, bass.ds((i * 2 + 1 + k) * C, C)]
                for q in range(IT):
                    pe.wait_ge(*S["a1"].at(i, 2 * k + q - 2))
                    pe.matmul(ps[:, q, :], win[:, q * P:(q + 1) * P], x, start=True, stop=True)\
                        .then_inc(*S["m1"].inc)
                for q in range(IT):
                    pe.wait_ge(*S["a4"].at(i, 2 * k + q - 2))
                    pe.matmul(ps[:, 2 + q, :], win[:, INNER + q * P:INNER + (q + 1) * P], x, start=True,
                              stop=True).then_inc(*S["m2"].inc)

            def pe_delta(pe, i, k):
                pe.wait_ge(*S["v4"].at(i, 2 * k + 1))
                for q in range(IT):
                    pe.wait_ge(*S["a3"].at(i, 2 * k + q - 2))
                    for c in range(IT):
                        mm = pe.matmul(ps[:, 4 + q, :], wdel[:, c, q * P:(q + 1) * P], val[:, slot(k, c)],
                                       start=(c == 0), stop=(c == IT - 1))
                    mm.then_inc(*S["m3"].inc)

            @block.tensor
            def _(pe):
                def front(i, k):
                    pe_in(pe, i, k)
                    pe_delta(pe, i, k)

                def turn(i, k, ahead):
                    if ahead:
                        front(i, k)
                    pe.wait_ge(*S["v9"].at(i, 2 * k + 1))
                    pe.wait_ge(*S["added"].at(i, k - 2))
                    for c in range(IT):
                        mm = pe.matmul(ps[:, 6 + k, :], wout[:, c], fu[:, 2 * k + c], start=(c == 0),
                                       stop=(c == IT - 1))
                    mm.then_inc(*S["m4"].inc)

                rounds(pe, ["m1", "m2", "m3"], front, turn)

            @block.scalar
            def _(act):
                act.preload_act_table_set("sigmoid_and_others")
                act.wait_ge(S["g5"].sem, S["g5"].base + 1)

                def front(i, k):
                    for q in range(IT):
                        e = 2 * k + q
                        act.wait_ge(*S["m1"].at(i, e))
                        act.wait_ge(*S["v3"].at(i, e - 4))
                        act.activation(vp[:, slot(k, q), :, TAPS2 - 1:], bank(ps, q, 2, T), ACT.Identity,
                                       bias=bin_[:, q:q + 1]).then_inc(*S["a1"].inc)
                    for q in range(IT):
                        e = 2 * k + q
                        act.wait_ge(*S["m2"].at(i, e))
                        act.wait_ge(*S["v9"].at(i, last_back(k, q)))
                        act.activation(gt[:, slot(k, q)], ps[:, 2 + q, :], ACT.Sigmoid,
                                       bias=bin_[:, IT + q:IT + q + 1]).then_inc(*S["a4"].inc)
                    for q in range(IT):
                        e = 2 * k + q
                        act.wait_ge(*S["v3"].at(i, e))
                        act.wait_ge(*S["v4"].at(i, e - 4))
                        act.activation(sg[:, slot(k, q)], cv[:, slot(k, q)], ACT.Sigmoid).then_inc(*S["a2"].inc)
                    for q in range(IT):
                        e = 2 * k + q
                        act.wait_ge(*S["m3"].at(i, e))
                        act.wait_ge(*S["v7"].at(i, last_back(k, q)))
                        act.activation(dl[:, slot(k, q)], ps[:, 4 + q, :], ACT.Sigmoid, bias=bdel[:, q:q + 1])\
                            .then_inc(*S["a3"].inc)

                rounds(act, ["a1", "a2", "a3", "a4"], front, lambda i, k, ahead: ahead and front(i, k))

            @block.gpsimd
            def _(pool):
                def front(i, k):
                    for q in range(IT):
                        e, h = 2 * k + q, slot(k, q)
                        pool.wait_ge(*S["a3"].at(i, e))
                        pool.wait_ge(*S["v7"].at(i, last_back(k, q)))
                        pool.tensor_tensor(bb[:, h], dl[:, h], val[:, h], ALU.mult).then_inc(*S["g1"].inc)
                        pool.wait_ge(*S["g1"].at(i, e))
                        pool.tensor_tensor(bb[:, h], val[:, h], bb[:, h], ALU.subtract).then_inc(*S["g2"].inc)

                rounds(pool, ["g1", "g2"], front, lambda i, k, ahead: ahead and front(i, k))

            def dve_conv(dve, i, k, q):
                def tap(t):
                    return vp[:, slot(k, q), :, t:t + T]

                e = 2 * k + q
                c3 = cv[:, slot(k, q)].rearrange("p (b t) -> p b t", b=2)
                dve.wait_ge(*S["a1"].at(i, e))
                dve.wait_ge(*S["a2"].at(i, e - 4))
                dve.wait_ge(*S["v4"].at(i, e - 4))
                dve.tensor_scalar(c3, tap(2), cw[:, q, 2:3], cb[:, q:q + 1], ALU.mult, ALU.add)\
                    .then_inc(*S["v1"].inc)
                dve.wait_ge(*S["v1"].at(i, e))
                dve.scalar_tensor_tensor(c3, tap(1), cw[:, q, 1:2], c3, ALU.mult, ALU.add)\
                    .then_inc(*S["v2"].inc)
                dve.wait_ge(*S["v2"].at(i, e))
                dve.scalar_tensor_tensor(c3, tap(0), cw[:, q, 0:1], c3, ALU.mult, ALU.add)\
                    .then_inc(*S["v3"].inc)

            def dve_value(dve, i, k, q):
                e, h = 2 * k + q, slot(k, q)
                dve.wait_ge(*S["a2"].at(i, e))
                dve.wait_ge(*S["g2"].at(i, e - 4))
                dve.wait_ge(*S["m3"].at(i, 2 * k + 1 - 4))
                dve.tensor_tensor(val[:, h], cv[:, h], sg[:, h], ALU.mult).then_inc(*S["v4"].inc)

            def dve_scan(dve, i, u, q):
                h = 2 * u + q
                dve.wait_ge(*S["g2"].at(i, front_of(u, q)))
                dve.wait_ge(*S["v9"].at(i, h - 4))
                for b in range(2):
                    span = slice(b * T, (b + 1) * T)
                    last_at = b * T - 1 if b else None
                    back = slice((b + 1) * T - 1, last_at, -1)
                    dve.tensor_tensor_scan(sc[:, h, 0, span], dl[:, h, span], bb[:, h, span], 0.0, ALU.mult, ALU.add)
                    last = dve.tensor_tensor_scan(sc[:, h, 1, back], dl[:, h, back], bb[:, h, back], 0.0,
                                                  ALU.mult, ALU.add)
                last.then_inc(*S["v7"].inc)
                dve.wait_ge(*S["v7"].at(i, h))
                dve.tensor_tensor(sc[:, h, 0], sc[:, h, 0], sc[:, h, 1], ALU.add).then_inc(*S["v8"].inc)
                dve.wait_ge(*S["v8"].at(i, h))
                dve.wait_ge(*S["a4"].at(i, front_of(u, q)))
                dve.wait_ge(*S["m4"].at(i, u - 2))
                dve.tensor_tensor(fu[:, h], sc[:, h, 0], gt[:, h], ALU.mult).then_inc(*S["v9"].inc)

            @block.vector
            def _(dve):
                dve.memset(vp[:], 0.0).then_inc(S["g5"].sem, 1)
                dve.wait_ge(S["g5"].sem, S["g5"].base + 1)

                def front(i, k):
                    for q in range(IT):
                        dve_conv(dve, i, k, q)
                    for q in range(IT):
                        dve_value(dve, i, k, q)

                def turn(i, k, ahead):
                    if ahead:
                        front(i, k)
                    for q in range(IT):
                        dve_scan(dve, i, k, q)
                    dve.wait_ge(*S["m4"].at(i, k))
                    chunk = bass.ds((i * 2 + k) * C, C)
                    dve.scalar_tensor_tensor(m["s"][:, chunk], ps[:, 6 + k, :], bout[:, 0:1], m["xn"][:, chunk],
                                             ALU.add, ALU.add).then_inc(*S["added"].inc)

                rounds(dve, ["v1", "v2", "v3", "v4"], front, turn)
        S["g5"].base += 1


def grouped_ffn(nc, ps, m, a):
    S = STEPS
    R = GROUPS // 2
    IT = INTER // P
    with ExitStack() as mem:
        buf = on_chip(nc, mem)

        w1, w2 = buf("w1g", P, 2, IT, P), buf("w2g", P, 2, IT, P)
        b1, b2 = buf("b1g", P, 2, IT), buf("b2g", P, 2)
        wc, bc = buf("wc", P, 2, P), buf("bc", P, 2)
        gate = buf("gate", P, 2, C)
        with Stage(R, fetched0=4, fetched1=4, m1=2, v1=2, m2=4, silu=4, weighed=4, added=4), nc.Block() as block:
            @block.sync
            def _(sp):
                with sp.Fori(0, R) as i:
                    for u in range(2):
                        g = i * 2 + u
                        sp.wait_ge(*S["v1"].at(i, u - 2))
                        for dst, src in ((w1[:, u], a["L2_ffn_W1"][bass.ds(g, 1)].rearrange(
                                              "g (c p) h -> p (g c) h", p=P)),
                                         (w2[:, u], a["L2_ffn_W2"][bass.ds(g, 1)].rearrange(
                                             "g (c p) h -> p (g c) h", p=P)),
                                         (b1[:, u], a["L2_ffn_b1"][:, bass.ds(g * IT, IT)]),
                                         (b2[:, u:u + 1], a["L2_ffn_b2"][bass.ds(g, 1)].rearrange("g p -> p g"))):
                            sp.wait_ge(S["first"].sem, PRIME)
                            sp.dma_start(dst, src).then_inc(*S[f"fetched{u}"].inc)

            @block.tensor
            def _(pe):
                with pe.Fori(0, R) as i:
                    for u in range(2):
                        pe.wait_ge(*S[f"fetched{u}"].at(i, 3))
                        pe.wait_ge(*S["v1"].at(i, u - 2))
                        for c in range(IT):
                            pe.matmul(ps[:, u, 0:P], w1[:, u, c], w2[:, u, c], start=(c == 0), stop=(c == IT - 1))
                        for c in range(IT):
                            mm = pe.matmul(ps[:, u, P:P + 1], w2[:, u, c], b1[:, u, c:c + 1], start=(c == 0),
                                           stop=(c == IT - 1))
                        mm.then_inc(*S["m1"].inc)
                    for u in range(2):
                        pe.wait_ge(*S["v1"].at(i, u))
                        for c in range(2):
                            k = 2 * u + c
                            pe.wait_ge(*S["silu"].at(i, k - 2))
                            pe.matmul(ps[:, 2 + k % 2, :], wc[:, u], m["xn"][:, bass.ds(i * (4 * C) + k * C, C)],
                                      start=True, stop=True).then_inc(*S["m2"].inc)

            @block.scalar
            def _(act):
                act.preload_act_table_set("silu_and_others")
                with act.Fori(0, R) as i:
                    for k in range(4):
                        act.wait_ge(*S["m2"].at(i, k))
                        act.wait_ge(*S["added"].at(i, k - 2))
                        act.activation(gate[:, k % 2], ps[:, 2 + k % 2, :], ACT.Silu, bias=bc[:, k // 2:k // 2 + 1])\
                            .then_inc(*S["silu"].inc)

            @block.vector
            def _(dve):
                with dve.Fori(0, R) as i:
                    for u in range(2):
                        dve.wait_ge(*S["m1"].at(i, u))
                        dve.wait_ge(*S["silu"].at(i, 2 * u + 1 - 4))
                        dve.tensor_tensor(bc[:, u:u + 1], ps[:, u, P:P + 1], b2[:, u:u + 1], ALU.add)
                        dve.tensor_copy(wc[:, u], ps[:, u, 0:P]).then_inc(*S["v1"].inc)
                    for k in range(4):
                        at = m["s"][:, bass.ds(i * (4 * C) + k * C, C)]
                        x = m["x"][:, bass.ds(i * (4 * C) + k * C, C)]
                        dve.wait_ge(*S["silu"].at(i, k))
                        dve.tensor_tensor(gate[:, k % 2], gate[:, k % 2], at, ALU.mult).then_inc(*S["weighed"].inc)
                        dve.wait_ge(*S["weighed"].at(i, k))
                        dve.tensor_tensor(x, x, gate[:, k % 2], ALU.add).then_inc(*S["added"].inc)


def conv_mixer(nc, ps, m, a):
    S = STEPS
    SEQS, K = 8, T // BLK
    R = B // SEQS
    SETS, CS = 4, 8
    with ExitStack() as mem:
        buf = on_chip(nc, mem)

        toep = buf("toeplitz", P, 2, BLK, 2, P)
        zt = buf("z_blocks", P, 2, BLK, SEQS, K + 1)
        zb, cc, sg = buf("z_chan", P, 2, C), buf("conv_sum", P, 2, 2, C), buf("sig3", P, 2, C)
        win, wout = buf("win3", P, 2, P), buf("wout3", P, 2, P)
        bi, bt, bo = buf("bin3", P, 2), buf("bconv3", P, 2, BLK), buf("bout3", P, 1)
        with nc.Block() as block:
            @block.vector
            def _(dve):
                dve.memset(toep[:, 0], 0.0)
                dve.memset(zt[:], 0.0).then_inc(S["g5"].sem, 1)

            @block.gpsimd
            def _(pool):
                pool.memset(toep[:, 1], 0.0).then_inc(S["g5"].sem, 1)
        S["g5"].base += 2
        pairs = [(win[:], a["L3_attn_w_in"].rearrange("p (q e) -> p q e", q=2)),
                 (wout[:], a["L3_attn_w_out"].rearrange("(q p) h -> p q h", p=P)),
                 (bi[:], a["L3_attn_b_in"]), (bo[:], column(a["L3_attn_b_out"]))]
        W = 3 * BLK
        for q, (w, b) in enumerate((("L3_attn_w_a", "L3_attn_b_a"), ("L3_attn_w_b", "L3_attn_b_b"))):
            for j in range(4):
                rows = slice(BLK * j, BLK * j + BLK)
                for before in range(2):
                    pairs.append((toep[rows, q, :, before, rows],
                                  bass.AP(a[w].tensor, BLK * j * W + 1 + BLK * before,
                                          [[1, BLK], [W, BLK], [1, BLK]])))
                pairs.append((bt[rows, q], bass.AP(a[b].tensor, BLK * j, [[0, BLK], [1, BLK]])))
        load(nc, pairs)

        with Stage(R, m1=8, a1=8, v1=8, m2=8, v2=8, a2=4, v3=4, v4=8, m3=4, a3=4), nc.Block() as block:
            @block.tensor
            def _(pe):
                with pe.Fori(0, R) as i:
                    for z in range(8):
                        pe.wait_ge(*S["a1"].at(i, z - 2))
                        pe.matmul(ps[:, z % 2, :], win[:, z % 2], m["xn"][:, bass.ds(i * (SEQS * T) + z // 2 * C, C)],
                                  start=True, stop=True).then_inc(*S["m1"].inc)
                    pe.wait_ge(*S["v1"].at(i, 7))
                    for n in range(2 * SETS):
                        q = n % 2
                        pe.wait_ge(*S["v2"].at(i, n - 4))
                        for c in range(CS):
                            ch = n // 2 * CS + c
                            o = ps[:, 2 + n % 4, c * SEQS * K:(c + 1) * SEQS * K].rearrange("p (b k) -> p b k", b=SEQS)
                            pe.matmul(o, toep[:, q, ch, 0], zt[:, q, ch, :, 1:K + 1], start=True, stop=False)
                            mm = pe.matmul(o, toep[:, q, ch, 1], zt[:, q, ch, :, 0:K], start=False, stop=True)
                        mm.then_inc(*S["m2"].inc)
                    for k in range(4):
                        pe.wait_ge(*S["v4"].at(i, 2 * k + 1))
                        pe.wait_ge(*S["a3"].at(i, k - 2))
                        for q in range(2):
                            mm = pe.matmul(ps[:, 6 + k % 2, :], wout[:, q], zb[:, q], start=(q == 0), stop=(q == 1))
                        mm.then_inc(*S["m3"].inc)

            @block.scalar
            def _(act):
                act.preload_act_table_set("sigmoid_and_others")
                with act.Fori(0, R) as i:
                    for z in range(8):
                        act.wait_ge(*S["m1"].at(i, z))
                        act.wait_ge(*(S["v1"].at(i, z - 2) if z >= 2 else S["m3"].at(i, -1)))
                        act.activation(zb[:, z % 2], ps[:, z % 2, :], ACT.Identity, bias=bi[:, z % 2:z % 2 + 1])\
                            .then_inc(*S["a1"].inc)
                    for g in range(SETS):
                        act.wait_ge(*S["v2"].at(i, 2 * g + 1))
                        act.wait_ge(*S["v3"].at(i, g - 1))
                        act.activation(sg[:], cc[:, g % 2], ACT.Sigmoid).then_inc(*S["a2"].inc)
                    for k in range(4):
                        act.wait_ge(*S["m3"].at(i, k))
                        act.wait_ge(S["first"].sem, PRIME)
                        act.activation(m["s"][:, bass.ds(i * (SEQS * T) + k * C, C)], ps[:, 6 + k % 2, :],
                                       ACT.Identity, bias=bo[:, 0:1]).then_inc(*S["a3"].inc)

            @block.vector
            def _(dve):
                with dve.Fori(0, R) as i:
                    for z in range(8):
                        dve.wait_ge(*S["a1"].at(i, z))
                        seqs = zt[:, z % 2, :, z // 2 * 2:z // 2 * 2 + 2, 1:K + 1]
                        dve.transpose(seqs.rearrange("p c b k -> p b k c"),
                                      zb[:, z % 2].rearrange("p (b k t) -> p b k t", b=2, k=K)[:, :, :, ::-1])\
                            .then_inc(*S["v1"].inc)
                    for g in range(SETS):
                        for q in range(2):
                            n = 2 * g + q
                            dve.wait_ge(*S["m2"].at(i, n))
                            dve.wait_ge(*S["v3"].at(i, g - 2))
                            dve.tensor_tensor(cc[:, g % 2, q].rearrange("p (c n) -> p c n", c=CS),
                                              bank(ps, 2 + n % 4, CS, SEQS * K),
                                              bt[:, q, g * CS:(g + 1) * CS].unsqueeze(2)
                                              .to_broadcast([P, CS, SEQS * K]), ALU.add).then_inc(*S["v2"].inc)
                        dve.wait_ge(*S["a2"].at(i, g))
                        for q in range(2):
                            last = dve.tensor_tensor(zt[:, q, g * CS:(g + 1) * CS, :, 1:K + 1],
                                                     cc[:, g % 2, q].rearrange("p (c b k) -> p c b k", c=CS, b=SEQS),
                                                     sg[:, 1 - q].rearrange("p (c b k) -> p c b k", c=CS, b=SEQS),
                                                     ALU.mult)
                        last.then_inc(*S["v3"].inc)
                    for k in range(4):
                        dve.wait_ge(*S["v3"].at(i, SETS - 1))
                        dve.wait_ge(*S["m3"].at(i, k - 1))
                        for q in range(2):
                            seqs = zt[:, q, :, 2 * k:2 * k + 2, 1:K + 1]
                            dve.transpose(zb[:, q].rearrange("p (b k t) -> p b k t", b=2, k=K),
                                          seqs.rearrange("p c b k -> p b k c")).then_inc(*S["v4"].inc)


def local_attention(nc, ps, m, a, layer):
    S = STEPS
    QW = HEADS * DH
    with ExitStack() as mem:
        buf = on_chip(nc, mem)

        wqkv, wo = buf("wqkv3", P, QKV), buf("wo3", P, 4, P)
        rope, tab, qks = buf("rope", P, 2, 4, DH), buf("rope_scaled", P, 2, 4, DH), buf("qk_scale", P, 2, DH)
        hf, qk, sq = buf("hf", P, 2, 1, T), buf("qk_raw", P, 2, 2 * QW), buf("qk_sq", P, 2 * QW)
        st, tw, ot = buf("qk_rot", P, 2, 2 * QW), buf("qk_cross", P, 2, 2 * QW), buf("ot", P, 4, T)
        ss, rn = buf("sumsq", P, 2, 16), buf("rnorm", P, 2, 16)
        core = Core(nc, ps, m, mem, m["band"], 8.0, DH, lambda tile: tile, lambda head: head * DH)
        load(nc, [(wqkv[:], a["L3_ffn_wqkv"][layer]), (wo[:], a["L3_ffn_wo"][layer].rearrange("(c p) o -> p c o", p=P)),
                  (rope[:], a["rope"]), (qks[:, 0], a["L3_ffn_q_scale"][layer].partition_broadcast(P)),
                  (qks[:, 1], a["L3_ffn_k_scale"][layer].partition_broadcast(P))])

        when = {t: [] for t in range(STEPS_T)}
        for first, r in ((0, 2), (10, 0)):
            when[first] += [("q", r), ("k", r)]
            when[first + 1] += [("v", r)]
            when[first + 2] += [("q", r + 1), ("k", r + 1)]
            when[first + 3] += [("v", r + 1)]
            when[first + 5] += [("qt", r), ("kt", r)]
            when[first + 7] += [("qt", r + 1), ("kt", r + 1)]
        for w in range(4):
            when[4 * w + MIX + 5].append(("ot", w))
        for u in range(2):
            when[8 * u + MIX + 10].append(("out", u))
        pos = {2: 0, 3: 1, 0: 2, 1: 3}
        NORMS = {first + 2 * (r % 2) + 1: r for first, rr in ((0, 2), (10, 0)) for r in (rr, rr + 1)}
        ROTATE = {t + 1: r for t, r in NORMS.items()}
        order = [x for t in range(STEPS_T) for x in when[t]]
        early = lambda x: x[0] in ("q", "k", "v", "qt", "kt") and x[1] < 2
        at = {x: n for n, x in enumerate(order)}
        by_act = [x for x in order if x[0] in ("q", "k", "v")]
        by_dve = [x for x in order if x not in by_act]

        def freed(i, n):
            x = order[n]
            name, mine = ("freed_act", by_act) if x in by_act else ("freed_dve", by_dve)
            return S[name].at(i, mine.index(x) - (len(mine) if n < 0 else 0))

        core.o_read = lambda i, w: (i, at["ot", w - 2] if w >= 2 else at["ot", w + 2] - len(order))

        def pe_event(pe, i, x):
            kind, r = x
            e = at[x]
            o = ps[:, 6 + e % 2]
            pe.wait_ge(*freed(i, e - 2))
            if isinstance(i, int):
                for n in [n for n in range(e % 2, e, 2) if early(order[n])][-1:]:
                    pe.wait_ge(*freed(i, n))
            if kind in ("q", "k", "v"):
                if kind == "q" and r % 2 == 0:
                    pe.wait_ge(*S["copied"].at(i, 1 - r // 2))
                w = "qkv".index(kind) * QW
                mm = pe.matmul(o, hf[:, r // 2, 0, r % 2 * P:(r % 2 + 1) * P], wqkv[:, w:w + QW], start=True, stop=True)
            elif kind in ("qt", "kt"):
                if kind == "qt":
                    pe.wait_ge(*S["unit"].at(i, pos[r]))
                for c in range(4):
                    first = (kind == "kt") * QW + c * P
                    mm = pe.transpose(o[:, c * P:(c + 1) * P], st[:, r % 2, first:first + P], m["ident"][:])
            elif kind == "ot":
                pe.wait_ge(*S["attended"].at(i, r))
                for c in range(4):
                    mm = pe.transpose(o[:, c * P:(c + 1) * P], core.o[:, r % 2, c * P:(c + 1) * P], m["ident"][:])
            else:
                pe.wait_ge(*freed(i, at["ot", 2 * r + 1]))
                for c in range(4):
                    mm = pe.matmul(o[:, 0:T], wo[:, c], ot[:, c], start=(c == 0), stop=(c == 3))
            mm.then_inc(*S["projected"].inc)

        def dve_event(dve, i, x):
            kind, r = x
            src = ps[:, 6 + at[x] % 2]
            dve.wait_ge(*S["projected"].at(i, at[x]))
            if kind in ("qt", "kt"):
                if kind == "qt" and r % 2 == 0:
                    dve.wait_ge(*S["scores"].at(i, -1 if r else 7))
                dst = core.qt if kind == "qt" else core.kt
                last = dve.tensor_copy(dst[:, r // 2, :, r % 2 * P:(r % 2 + 1) * P], bank(ps, 6 + at[x] % 2, 4, P))
            elif kind == "ot":
                last = dve.tensor_copy(ot[:, :, r % 2 * P:(r % 2 + 1) * P], bank(ps, 6 + at[x] % 2, 4, P))
            else:
                xn = m["xn"][:, cols(i, r, T)]
                last = dve.tensor_tensor(xn, xn, src[:, 0:T], ALU.add)
            last.then_inc(*S["freed_dve"].inc)

        made = ["copied", "projected", "freed_act", "freed_dve", "squared", "sumsq", "rnorm", "v1", "straight",
                "crossed", "rotated", "unit"]
        with Stage(PAIRS, made, copied=2, projected=len(order), freed_act=len(by_act), freed_dve=len(by_dve), squared=4,
                   sumsq=4, rnorm=4, v1=4, straight=4, crossed=4, rotated=4, unit=4, **CORE), nc.Block() as block:
            @block.gpsimd
            def _(pool):
                pool.memset(hf[:], 0.0).then_inc(S["g5"].sem, 1)
                for tb in range(2):
                    for w in range(2):
                        pool.tensor_tensor(tab[:, tb, 2 * w], rope[:, tb, 2 * w], qks[:, w], ALU.mult)
                        last = pool.tensor_tensor(
                            tab[:, tb, 2 * w + 1].rearrange("p (a d) -> p a d", a=2),
                            rope[:, tb, 2 * w + 1].rearrange("p (a d) -> p a d", a=2),
                            qks[:, w].rearrange("p (a d) -> p a d", a=2)[:, ::-1], ALU.mult)
                last.then_inc(S["g5"].sem, 1)
                pool.wait_ge(S["g5"].sem, S["g5"].base + 2)

                def shift(i, u, first):
                    pool.wait_ge(*S["unit"].at(i, 2 * (1 - u) - 1))
                    shift_in(pool, hf[:, u], m["xn"], i, u, T, S["projected"].at(i, at["v", 2 * u + 1] - len(order)),
                             first=first)
                    pool.wait_ge(*S["copied"].at(i, 1 - u))

                def tile(i, r):
                    p = pos[r]
                    pool.wait_ge(*S["freed_act"].at(i, by_act.index(("k", r))))
                    pool.wait_ge(*S["rotated"].at(i, p - 2))
                    for w in range(2):
                        raw = qk[:, r % 2, w * QW:(w + 1) * QW].rearrange("p (h a d) -> p h a d", a=2, d=DH // 2)
                        last = pool.tensor_tensor(
                            tw[:, r % 2, w * QW:(w + 1) * QW].rearrange("p (h a d) -> p h a d", a=2, d=DH // 2),
                            raw[:, :, ::-1, :],
                            tab[:, r % 2, 2 * w + 1].rearrange("p (a d) -> p a d", a=2).unsqueeze(1)
                            .to_broadcast([P, HEADS, 2, DH // 2]), ALU.mult)
                    last.then_inc(*S["crossed"].inc)
                    pool.wait_ge(*S["v1"].at(i, p))
                    pool.tensor_tensor(rn[:, r % 2], rn[:, r % 2], m["half"][:], ALU.pow).then_inc(*S["rnorm"].inc)
                    pool.wait_ge(*S["rnorm"].at(i, p))
                    pool.wait_ge(*S["rotated"].at(i, p))
                    heads = st[:, r % 2].rearrange("p (h d) -> p h d", d=DH)
                    pool.tensor_tensor(heads, heads, rn[:, r % 2].unsqueeze(2).to_broadcast([P, 16, DH]),
                                       ALU.mult).then_inc(*S["unit"].inc)

                for name in ("crossed", "rnorm", "unit"):
                    pass_over(pool, name, 0, 2)
                pass_over(pool, "copied", 0, 1)
                shift(-1, 0, 0)
                tile(-1, 0)
                tile(-1, 1)
                with pool.Fori(0, PAIRS) as i:
                    shift(i, 1, i * (2 * T) + T)
                    tile(i, 2)
                    tile(i, 3)
                    shift(i, 0, i * (2 * T) + 2 * T)
                    tile(i, 0)
                    tile(i, 1)

            @block.tensor
            def _(pe):
                first_ones(pe, "projected", order, early, lambda x: pe_event(pe, -1, x))
                with pe.Fori(0, PAIRS) as i:
                    for t in range(STEPS_T):
                        core.pe_step(pe, i, t, lambda i, u: [freed(i, at[x, 2 * u + 1] - (0 if u else len(order)))
                                                             for x in ("kt", "v")])
                        for x in when[t]:
                            pe_event(pe, i, x)

            def act_event(act, i, x):
                kind, r = x
                p = pos[r]
                act.wait_ge(*S["projected"].at(i, at[x]))
                if kind == "q":
                    act.wait_ge(*S["straight"].at(i, p - 2))
                    act.wait_ge(*S["crossed"].at(i, p - 2))
                    act.wait_ge(*S["squared"].at(i, p - 2))
                if kind == "v":
                    act.wait_ge(*S["mixed"].at(i, -1 if r > 1 else 7))
                    dst = core.v[:, r // 2, r % 2]
                else:
                    w = "qk".index(kind)
                    dst = qk[:, r % 2, w * QW:(w + 1) * QW]
                act.activation(dst, ps[:, 6 + at[x] % 2], ACT.Copy).then_inc(*S["freed_act"].inc)
                if kind == "k":
                    act.wait_ge(*S["sumsq"].at(i, p - 1))
                    act.wait_ge(*S["freed_act"].at(i, by_act.index(x)))
                    act.activation(sq[:], qk[:, r % 2], ACT.Square).then_inc(*S["squared"].inc)

            @block.scalar
            def _(act):
                act.preload_act_table_set("exp_and_others")
                pass_over(act, "squared", 0, 2)
                first_ones(act, "freed_act", by_act, early, lambda x: act_event(act, -1, x))
                with act.Fori(0, PAIRS) as i:
                    for t in range(STEPS_T):
                        core.act_step(act, i, t)
                        for x in when[t]:
                            if x in by_act:
                                act_event(act, i, x)

            def dve_norms(dve, i, r):
                p = pos[r]
                dve.wait_ge(*S["squared"].at(i, p))
                dve.wait_ge(*S["unit"].at(i, p - 2))
                dve.tensor_reduce(ss[:, r % 2], sq[:].rearrange("p (h d) -> p h d", d=DH), AX.X, ALU.add)\
                    .then_inc(*S["sumsq"].inc)
                dve.wait_ge(*S["sumsq"].at(i, p))
                dve.tensor_scalar(rn[:, r % 2], ss[:, r % 2], 1e-24, None, ALU.max).then_inc(*S["v1"].inc)
                dve.wait_ge(*S["projected"].at(i, at["kt", (r + 2) % 4] - (len(order) if r > 1 else 0)))
                for w in range(2):
                    last = dve.tensor_tensor(st[:, r % 2, w * QW:(w + 1) * QW].rearrange("p (h d) -> p h d", d=DH),
                                             qk[:, r % 2, w * QW:(w + 1) * QW].rearrange("p (h d) -> p h d", d=DH),
                                             tab[:, r % 2, 2 * w:2 * w + 1].to_broadcast([P, HEADS, DH]), ALU.mult)
                last.then_inc(*S["straight"].inc)

            def dve_rotate(dve, i, r):
                dve.wait_ge(*S["straight"].at(i, pos[r]))
                dve.wait_ge(*S["crossed"].at(i, pos[r]))
                dve.tensor_tensor(st[:, r % 2], st[:, r % 2], tw[:, r % 2], ALU.add).then_inc(*S["rotated"].inc)

            @block.vector
            def _(dve):
                dve.wait_ge(S["g5"].sem, S["g5"].base + 2)
                for name in ("sumsq", "v1", "straight", "rotated"):
                    pass_over(dve, name, 0, 2)
                for t in range(STEPS_T):
                    if NORMS.get(t, 2) < 2:
                        dve_norms(dve, -1, NORMS[t])
                    if ROTATE.get(t, 2) < 2:
                        dve_rotate(dve, -1, ROTATE[t])
                    mine = [x for x in when[t] if x in by_dve]
                    first_ones(dve, "freed_dve", mine, early, lambda x: dve_event(dve, -1, x),
                               by_dve.index(mine[0]) if mine else 0)
                with dve.Fori(0, PAIRS) as i:
                    for t in range(STEPS_T):
                        core.dve_step(dve, i, t)
                        if t in NORMS:
                            dve_norms(dve, i, NORMS[t])
                        if t in ROTATE:
                            dve_rotate(dve, i, ROTATE[t])
                        for x in when[t]:
                            if x in by_dve:
                                dve_event(dve, i, x)
        S["g5"].base += 2


def gelu_ffn(nc, ps, m, a, layer, h_in):
    S, R = STEPS, ROUNDS
    FT = 3
    with ExitStack() as mem:
        buf = on_chip(nc, mem)

        w1, w2, b1, b2 = buf("w1t", P, 2, FT, P), buf("w2t", P, FT, P), buf("b1t", P, 2, FT), buf("b2t", P, 1)
        gg, hd = buf("gelu_g", P, 2, C), buf("hid3", P, 2, C)
        load(nc, [(w1[:], a["L3_ffn_w1"][layer]), (w2[:], a["L3_ffn_w2"][layer].rearrange("(f p) d -> p f d", p=P)),
                  (b1[:], a["L3_ffn_b1"][layer]), (b2[:], column(a["L3_ffn_b2"][layer]))])
        with Stage(R, up=2 * FT, act_a=2 * FT, gated=2 * FT, m1=2 * FT, added=2), nc.Block() as block:
            @block.tensor
            def _(pe):
                with pe.Fori(0, R) as i:
                    for u in range(2):
                        for f in range(FT + 1):
                            h = FT * u + f
                            if f < FT:
                                pe.wait_ge(*S["gated"].at(i, h - 2))
                                for g in range(2):
                                    mm = pe.matmul(ps[:, 2 * (h % 2) + g, :], w1[:, g, f], h_in[:, cols(i, u, C)],
                                                   start=True, stop=True)
                                mm.then_inc(*S["up"].inc)
                            if f >= 1:
                                pe.wait_ge(*S["gated"].at(i, h - 1))
                                if f == 1:
                                    pe.wait_ge(*S["added"].at(i, u - 2))
                                mm = pe.matmul(ps[:, 4 + u, :], w2[:, f - 1], hd[:, (h - 1) % 2],
                                               start=(f == 1), stop=(f == FT))
                                mm.then_inc(*S["m1"].inc)

            @block.scalar
            def _(act):
                act.preload_act_table_set("gelu_and_others")
                with act.Fori(0, R) as i:
                    for h in range(2 * FT):
                        act.wait_ge(*S["up"].at(i, h))
                        act.wait_ge(*S["gated"].at(i, h - 2))
                        act.activation(gg[:, h % 2], ps[:, 2 * (h % 2) + 1, :], ACT.Gelu,
                                       bias=b1[:, 1, h % FT:h % FT + 1]).then_inc(*S["act_a"].inc)

            @block.vector
            def _(dve):
                with dve.Fori(0, R) as i:
                    for u in range(2):
                        for h in range(FT * u, FT * (u + 1)):
                            dve.wait_ge(*S["act_a"].at(i, h))
                            dve.wait_ge(*S["m1"].at(i, h - 2))
                            dve.scalar_tensor_tensor(hd[:, h % 2], ps[:, 2 * (h % 2), :], b1[:, 0, h % FT:h % FT + 1],
                                                     gg[:, h % 2], ALU.add, ALU.mult).then_inc(*S["gated"].inc)
                        xn = m["xn"][:, cols(i, u, C)]
                        dve.wait_ge(*S["m1"].at(i, FT * (u + 1) - 1))
                        dve.scalar_tensor_tensor(xn, ps[:, 4 + u, :], b2[:, 0:1], xn, ALU.add, ALU.add)\
                            .then_inc(*S["added"].inc)


def rope_tables():
    half = np.arange(0, DH, 2, dtype=np.float32)
    t = np.arange(T, dtype=np.float32)
    freqs = t[:, None] * (1.0 / 10000.0 ** (half / DH))[None, :].astype(np.float32)
    base = (half + 0.4 * DH) / (1.4 * DH)
    scale = base[None, :] ** ((t - T // 2) / float(WINDOW // 2))[:, None]
    freqs, scale = np.concatenate([freqs, freqs], -1), np.concatenate([scale, scale], -1)
    sign = np.where(np.arange(DH) < DH // 2, -1.0, 1.0)[None, :]
    cos, sin = np.cos(freqs), np.sin(freqs) * sign
    tables = np.stack([cos * scale, sin * scale, cos / scale, sin / scale], 1).astype(np.float32)
    return tables.reshape(2, P, 4, DH).transpose(1, 0, 2, 3)


def lay_out(x):
    x = {k: np.asarray(v) for k, v in x.items()}
    d = dict(x)
    d["x"] = d.pop("L0_attn_x").reshape(N, P).T
    d["L0_attn_wq"] = x["L0_attn_wq"].reshape(P, HEADS, P).transpose(2, 1, 0)
    for n in ("L0_attn_wk_up", "L0_attn_wv_up", "L1_attn_w_qkv", "L1_attn_w_out", "L1_ffn_w_gate", "L1_ffn_w_up",
              "L1_ffn_w_down", "L3_attn_w_in", "L3_attn_w_out"):
        d[n] = x[n].T
    d["L0_ffn_b1"] = x["L0_ffn_b1"].reshape(EXPERTS, FF0 // P, P).transpose(2, 0, 1)
    for n, w in (("L2_attn_b_in", 4), ("L2_attn_conv_b", 2), ("L2_attn_b_delta", 2), ("L3_attn_b_in", 2)):
        d[n] = x[n].reshape(w, P).T
    d["L2_ffn_W2"] = x["L2_ffn_W2"].transpose(0, 2, 1)
    d["L2_ffn_b1"] = x["L2_ffn_b1"].reshape(GROUPS * INTER // P, P).T
    for n in ("L3_attn_w_a", "L3_attn_w_b"):
        d[n] = np.pad(x[n].reshape(P, TAPS3)[:, ::-1], ((0, 0), (BLK, BLK)))
    pad = 3 * P - HID3
    w1 = np.pad(x["L3_ffn_w1"].reshape(DEPTH, P, 2, HID3), ((0, 0), (0, 0), (0, 0), (0, pad)))
    d["L3_ffn_w1"] = w1.reshape(DEPTH, P, 2, 3, P)
    b1 = np.pad(x["L3_ffn_b1"].reshape(DEPTH, 2, HID3), ((0, 0), (0, 0), (0, pad)))
    d["L3_ffn_b1"] = b1.reshape(DEPTH, 2, 3, P).transpose(0, 3, 1, 2)
    d["L3_ffn_w2"] = np.pad(x["L3_ffn_w2"], ((0, 0), (0, pad), (0, 0)))
    d["rope"] = rope_tables()
    return {k: np.ascontiguousarray(v) for k, v in d.items()}


def kernel(**inputs):
    import concourse.bacc as bacc
    from concourse.bass_utils import run_bass_kernel_spmd

    nc = bacc.Bacc("TRN2", target_bir_lowering=False, num_devices=1)
    arrays = lay_out(inputs)
    a = {k: nc.dram_tensor(f"in_{k}", v.shape, mybir.dt.from_np(v.dtype), kind="ExternalInput").ap()
         for k, v in arrays.items()}
    out = nc.dram_tensor("out_x", (P, N), F32, kind="ExternalOutput").ap()
    build(nc, a, out)
    r = run_bass_kernel_spmd(nc, [{f"in_{k}": v for k, v in arrays.items()}], core_ids=[0])
    return np.ascontiguousarray(np.asarray(r.results[0]["out_x"]).T).reshape(B, T, P)
```
